# Optimizing a Trainium2 kernel written in Bass

```python
import numpy as np
import jax
import jax.numpy as jnp

def _softmax(x, axis=-1):
    return jax.nn.softmax(x, axis=axis)

def _gelu(x):
    return jax.nn.gelu(x, approximate=True)

def _silu(x):
    return jax.nn.silu(x)

def _sigmoid(x):
    return jax.nn.sigmoid(x)

def _layernorm(x, axis=-1, eps=1e-05):
    m = jnp.mean(x, axis=axis, keepdims=True)
    v = jnp.var(x, axis=axis, keepdims=True)
    return (x - m) / jnp.sqrt(v + eps)

def _scatter_add(tgt, idx, src, axis=0):
    return tgt.at[idx].add(src)

def _segment_sum(src, seg, n):
    return jax.ops.segment_sum(src, seg, n)
kernel_name = 'mk_gnn_ffn_d1_gnn_r32_9c66ad'

def setup_inputs(seed: int=0):
    np.random.seed(seed)
    _w = jnp.asarray

    def _rec_inputs():
        import jax
        import jax.numpy as jnp
        _gk = jax.random.key(seed)
        x = -0.0002117 + 1 * jax.random.normal(jax.random.fold_in(_gk, 1), (3125, 256), jnp.float32)
        _s = jax.random.randint(jax.random.fold_in(_gk, 2), (25000,), 0, 3125, jnp.int32)
        _d = jax.random.randint(jax.random.fold_in(_gk, 3), (25000,), 0, 3125, jnp.int32)
        _loop = jnp.arange(3125, dtype=jnp.int32)
        src = jnp.concatenate([_s, _d, _loop])
        dst = jnp.concatenate([_d, _s, _loop])
        _o = jnp.argsort(dst, stable=True)
        src = src[_o]
        dst = dst[_o]
        return (x, src, dst)
    x, src, dst = _rec_inputs()

    def _L0_gnn_setup():
        import jax, jax.numpy as jnp
        import numpy as np
        N_NODES = 3125
        N_EDGES = 50000
        D_IN = 256
        D_HID = 256
        BN_EPS = 1e-05
        key = jax.random.key(seed)
        ks = jax.random.split(key, 10)
        s_in = 1.0 / np.sqrt(D_IN)
        s_hid = 1.0 / np.sqrt(D_HID)
        return {'x': jax.random.normal(ks[0], (N_NODES, D_IN), dtype=jnp.float32), 'edge_index': jax.random.randint(ks[1], (2, N_EDGES), 0, N_NODES, dtype=jnp.int64), 'gcn_W': jax.random.normal(ks[2], (D_IN, D_HID), dtype=jnp.float32) * s_in, 'gcn_b': jnp.zeros((D_HID,), dtype=jnp.float32), 'lin_W': jax.random.normal(ks[3], (D_IN, D_HID), dtype=jnp.float32) * s_in, 'lin_b': jnp.zeros((D_HID,), dtype=jnp.float32), 'gate_W': jax.random.normal(ks[4], (D_HID, D_HID), dtype=jnp.float32) * s_hid, 'gate_b': jnp.zeros((D_HID,), dtype=jnp.float32), 'bn_gamma': jnp.ones((D_HID,), dtype=jnp.float32), 'bn_beta': jnp.zeros((D_HID,), dtype=jnp.float32)}
    _L0_gnn_all = _L0_gnn_setup()
    _L0_gnn_in = {k: v for k, v in _L0_gnn_all.items() if k in ('gcn_W', 'gcn_b', 'lin_W', 'lin_b', 'gate_W', 'gate_b', 'bn_gamma', 'bn_beta')}
    del _L0_gnn_all

    def _L0_ffn_setup():
        import jax, jax.numpy as jnp
        import numpy as np
        TOP_K = 2
        LN_EPS = 1e-05
        key = jax.random.key(seed)
        ks = jax.random.split(key, 8)
        B, S, D, E, H = (16, 1024, 256, 8, 1024)
        x = jax.random.normal(ks[0], (B, S, D), dtype=jnp.float32)
        Wr = jax.random.normal(ks[1], (D, E), dtype=jnp.float32) * 0.1
        br = jnp.zeros((E,), dtype=jnp.float32)
        ln_g = jnp.ones((E, D), dtype=jnp.float32)
        ln_b = jnp.zeros((E, D), dtype=jnp.float32)
        W1 = jax.random.normal(ks[2], (E, D, H), dtype=jnp.float32) * (1.0 / np.sqrt(D))
        b1 = jnp.zeros((E, H), dtype=jnp.float32)
        W2 = jax.random.normal(ks[3], (E, H, D), dtype=jnp.float32) * (1.0 / np.sqrt(H))
        b2 = jnp.zeros((E, D), dtype=jnp.float32)
        return {'x': x, 'Wr': Wr, 'br': br, 'ln_g': ln_g, 'ln_b': ln_b, 'W1': W1, 'b1': b1, 'W2': W2, 'b2': b2}
    _L0_ffn_all = _L0_ffn_setup()
    _L0_ffn_in = {k: v for k, v in _L0_ffn_all.items() if k in ('Wr', 'br', 'ln_g', 'ln_b', 'W1', 'b1', 'W2', 'b2')}
    del _L0_ffn_all
    return {'x': x, 'src': src, 'dst': dst, 'L0_gnn_gcn_W': _L0_gnn_in['gcn_W'], 'L0_gnn_gcn_b': _L0_gnn_in['gcn_b'], 'L0_gnn_lin_W': _L0_gnn_in['lin_W'], 'L0_gnn_lin_b': _L0_gnn_in['lin_b'], 'L0_gnn_gate_W': _L0_gnn_in['gate_W'], 'L0_gnn_gate_b': _L0_gnn_in['gate_b'], 'L0_gnn_bn_gamma': _L0_gnn_in['bn_gamma'], 'L0_gnn_bn_beta': _L0_gnn_in['bn_beta'], 'L0_ffn_Wr': _L0_ffn_in['Wr'], 'L0_ffn_br': _L0_ffn_in['br'], 'L0_ffn_ln_g': _L0_ffn_in['ln_g'], 'L0_ffn_ln_b': _L0_ffn_in['ln_b'], 'L0_ffn_W1': _L0_ffn_in['W1'], 'L0_ffn_b1': _L0_ffn_in['b1'], 'L0_ffn_W2': _L0_ffn_in['W2'], 'L0_ffn_b2': _L0_ffn_in['b2']}

def reference(x, src, dst, L0_gnn_gcn_W, L0_gnn_gcn_b, L0_gnn_lin_W, L0_gnn_lin_b, L0_gnn_gate_W, L0_gnn_gate_b, L0_gnn_bn_gamma, L0_gnn_bn_beta, L0_ffn_Wr, L0_ffn_br, L0_ffn_ln_g, L0_ffn_ln_b, L0_ffn_W1, L0_ffn_b1, L0_ffn_W2, L0_ffn_b2):
    import jax
    import jax.numpy as jnp

    def _L0_gnn_ref(x, edge_index, gcn_W, gcn_b, lin_W, lin_b, gate_W, gate_b, bn_gamma, bn_beta):
        import jax, jax.numpy as jnp
        import numpy as np
        N_NODES = 3125
        N_EDGES = 50000
        D_IN = 256
        D_HID = 256
        BN_EPS = 1e-05
        N = x.shape[0]
        loops = jnp.arange(N, dtype=edge_index.dtype)
        row = jnp.concatenate([edge_index[0], loops])
        col = jnp.concatenate([edge_index[1], loops])
        ones = jnp.ones(row.shape[0], dtype=x.dtype)
        deg = jax.ops.segment_sum(ones, col, num_segments=N)
        dinv = jnp.where(deg > 0, jax.lax.rsqrt(deg), 0.0)
        norm = dinv[row] * dinv[col]
        xw = x @ gcn_W
        msgs = xw[row] * norm[:, None]
        z = jax.ops.segment_sum(msgs, col, num_segments=N) + gcn_b
        z = jnp.tanh(z)
        g = jax.nn.sigmoid(z @ gate_W + gate_b)
        xl = x @ lin_W + lin_b
        h = jax.nn.relu((1.0 - g) * xl + g * z)
        mean = h.mean(axis=0)
        var = h.var(axis=0)
        h = (h - mean) * jax.lax.rsqrt(var + BN_EPS) * bn_gamma + bn_beta
        return h

    def _L0_ffn_ref(x, Wr, br, ln_g, ln_b, W1, b1, W2, b2):
        import jax, jax.numpy as jnp
        import numpy as np
        TOP_K = 2
        LN_EPS = 1e-05
        B, S, D = x.shape
        N = B * S
        xt = x.reshape(N, D)
        logits = xt @ Wr + br
        probs = jax.nn.softmax(logits, axis=-1)
        top_p, top_idx = jax.lax.top_k(probs, TOP_K)
        weights = top_p / top_p.sum(axis=-1, keepdims=True)
        mu = xt.mean(axis=-1, keepdims=True)
        var = ((xt - mu) ** 2).mean(axis=-1, keepdims=True)
        xn = (xt - mu) * jax.lax.rsqrt(var + LN_EPS)
        xe = xn[None, :, :] * ln_g[:, None, :] + ln_b[:, None, :]
        h = jax.nn.gelu(jnp.einsum('end,edh->enh', xe, W1) + b1[:, None, :], approximate=False)
        y = jnp.einsum('enh,ehd->end', h, W2) + b2[:, None, :]
        y_tok = jnp.transpose(y, (1, 0, 2))
        sel = jnp.take_along_axis(y_tok, top_idx[:, :, None], axis=1)
        out = (weights[:, :, None] * sel).sum(axis=1)
        return out.reshape(B, S, D)
    edge_index = jnp.stack([src, dst])
    x = x + _L0_gnn_ref(_layernorm(x, axis=-1), edge_index, L0_gnn_gcn_W, L0_gnn_gcn_b, L0_gnn_lin_W, L0_gnn_lin_b, L0_gnn_gate_W, L0_gnn_gate_b, L0_gnn_bn_gamma, L0_gnn_bn_beta)
    x = x + _L0_ffn_ref(_layernorm(x, axis=-1)[None], L0_ffn_Wr, L0_ffn_br, L0_ffn_ln_g, L0_ffn_ln_b, L0_ffn_W1, L0_ffn_b1, L0_ffn_W2, L0_ffn_b2)[0]
    return x

_drawn_inputs = setup_inputs


def setup_inputs(seed=0):
    import zlib

    import numpy as np

    out = dict(_drawn_inputs(seed))
    spreads = {'L0_gnn_gcn_b': (0.0, 0.1),
     'L0_gnn_lin_b': (0.0, 0.1),
     'L0_gnn_gate_b': (0.0, 0.1),
     'L0_gnn_bn_gamma': (1.0, 0.2),
     'L0_gnn_bn_beta': (0.0, 0.1),
     'L0_ffn_br': (0.0, 0.1),
     'L0_ffn_ln_g': (1.0, 0.2),
     'L0_ffn_ln_b': (0.0, 0.1),
     'L0_ffn_b1': (0.0, 0.1),
     'L0_ffn_b2': (0.0, 0.1)}
    factors = {}
    for name, (base, spread) in spreads.items():
        noise = np.random.default_rng([zlib.crc32(name.encode()), seed]).standard_normal(out[name].shape)
        drawn = base * np.exp(spread * noise) if base else spread * noise
        out[name] = jnp.asarray(drawn.astype(out[name].dtype))
    for name, factor in factors.items():
        out[name] = (out[name] * factor).astype(out[name].dtype)
    return out
```

```python
from contextlib import ExitStack

import concourse.bass as bass
from concourse import mybir

P = 128
F32, F16, I32 = mybir.dt.float32, mybir.dt.float16, mybir.dt.int32
ALU = mybir.AluOpType
ACT = mybir.ActivationFunctionType
AX = mybir.AxisListType.X

EPS = 1e-5
WINDOW = 64
SLOTS = 13
U = 4
XN_SCALE = 1024.0
EXPONENT = 0x7F800000


def build_gnn_moe(nc, x, src, dst, gcn_W, gcn_b, lin_W, lin_b, gate_W, gate_b, bn_gamma, bn_beta,
                  Wr, br, ln_g, ln_b, W1, b1, W2, b2, out):
    N, D = x.shape
    E, _, H = W1.shape
    EDGES = src.shape[0]
    NT = -(-N // P)
    NPAD = NT * P
    KD, KH = D // P, H // P
    LAST = N - (NT - 1) * P
    BODY = 2 * SLOTS
    ET = BODY * 2 * E
    ROWS = ET // 4
    FULL = EDGES // (4 * P)
    TAIL = EDGES - FULL * 4 * P
    XG = (NT - 1) // 4
    CH = 400
    NCH = NPAD // CH
    ST = (2 * N + E * (P - 1)) // P
    NB = ST // U
    DUMP = 2 * NPAD
    EW = E * KD * H
    assert KD == 2 and ET * P >= EDGES and FULL == ROWS - 1 and 0 < TAIL <= 4 * P and ROWS <= P
    assert ST % U == 0 and NPAD % CH == 0 and (P + NT) * ET <= 4 * EW - 2 * KD * D and NPAD < 2 ** 15
    CB1, CG = 0, E * KH
    CB = CG + E * KD
    CV = CB + E * KD
    PROWS = CV + 5 * KD

    t_dram = nc.dram_tensor("message_table", (NPAD, D), F32, kind="Internal").ap()
    xnT_dram = nc.dram_tensor("xnT_table", (P, KD, NPAD), F32, kind="Internal").ap()
    dinv_dram = nc.dram_tensor("dinv_row", (NT, P), F32, kind="Internal").ap()
    xn_dram = nc.dram_tensor("token_table", (NPAD, 2 * D), F16, kind="Internal").ap()
    y_dram = nc.dram_tensor("expert_rows", (DUMP + ST * P, D), F32, kind="Internal").ap()

    with ExitStack() as ctx:
        def sb(name, shape, dt):
            return ctx.enter_context(nc.sbuf_tensor(name, shape, dt))

        def sem(name):
            return ctx.enter_context(nc.semaphore(name))

        WALL = sb("WALL", [P, 4 * EW], F16)
        W1hi = WALL[:, 0:EW].rearrange("p (e k h) -> p e k h", e=E, k=KD)
        W1lo = WALL[:, EW:2 * EW].rearrange("p (e k h) -> p e k h", e=E, k=KD)
        W2hi = WALL[:, 2 * EW:3 * EW].rearrange("p (e c d) -> p e c d", e=E, c=KH)
        W2lo = WALL[:, 3 * EW:4 * EW].rearrange("p (e c d) -> p e c d", e=E, c=KH)
        mask_lo = WALL[:, 0:P * ET].rearrange("p (k t) -> p k t", t=ET)
        mask_hi = WALL[:, P * ET:(P + NT) * ET].rearrange("p (k t) -> p k t", t=ET)

        A = sb("A", [P, KD * NPAD], F32)
        B = sb("B", [P, KD * NPAD], F32)
        R = sb("R", [P, SLOTS * D], F32)
        S = sb("S", [P, KD * H], F32)

        AT = A[:].rearrange("p (k n) -> p k n", k=KD)
        BT = B[:].rearrange("p (k n) -> p k n", k=KD)
        BR = B[:].rearrange("p (t d) -> p t d", d=D)
        RS = R[:].rearrange("p (s d) -> p s d", d=D)

        edge_d = A[:, 0:4 * P].bitcast(I32)
        edge_s = A[:, 4 * P:8 * P].bitcast(I32)
        edge_df = A[:, 8 * P:12 * P]
        edge_sf = A[:, 12 * P:16 * P]
        tmin_w = A[:, 16 * P:20 * P]
        prow = A[:, 20 * P:21 * P]
        tmin = A[:, 21 * P:21 * P + 4]
        tmax = A[:, 21 * P + 4:21 * P + 8]
        tdif = A[:, 21 * P + 8:21 * P + 12]
        tspan = A[:, 21 * P + 12:21 * P + 13]
        dst_f = R[:, 0:ET]
        dst_i = R[:, ET:2 * ET].bitcast(I32)
        lohi_i = R[:, 2 * ET:3 * ET].bitcast(I32)
        lo16 = R[:, 3 * ET:3 * ET + ET // 2].bitcast(F16)
        hi16 = R[:, 3 * ET + ET // 2:4 * ET].bitcast(F16)
        XN = [RS[:, 7, :], RS[:, 8, :]]
        XS = [RS[:, 9, :], RS[:, 10, :]]
        TS = [RS[:, 11, :], RS[:, 12, :]]
        gcnW = S[:, 0:KD * D].rearrange("p (k n) -> p k n", k=KD)
        linWv = WALL[:, 4 * EW - 2 * KD * D:4 * EW].bitcast(F32).rearrange("p (k n) -> p k n", k=KD)
        gateW = gcnW
        DX = S[:, KD * D:KD * D + KD * CH].rearrange("p (k n) -> p k n", k=KD)
        SW1 = S[:].rearrange("p (k h) -> p k h", k=KD)
        b2bc = S[:].rearrange("p (e d) -> p e d", e=E)

        ident = sb("ident", [P, P], F32)
        ones = sb("ones", [P, P], F32)
        iota = sb("iota", [P, P], F32)
        iota_w = sb("iota_w", [P, WINDOW], F32)
        src_i = sb("src_i", [P, ET], I32)
        dst_rel = sb("dst_rel", [P, ET], F32)
        route = sb("route", [P, ET], F32)
        base_i = route[0:1, :].bitcast(I32)
        params = sb("params", [P, PROWS], F32)
        oh = sb("oh", [P, 2, WINDOW], F32)
        idx_ring = sb("idx_ring", [P, BODY], I32)
        dinv = sb("dinv", [P, NT], F32)
        small = sb("small", [P, 64], F32)
        npass_f, npass_i = small[0:1, 0:1], small[0:1, 1:4].bitcast(I32)
        wam, wmax = small[:, 4:5], small[:, 5:6]
        wp2 = small[:, 6:7]
        wsc = small[:, 7:8]
        epst = small[:, 8:9]
        bmv = small[:, 12:16].rearrange("p (k v) -> p k v", k=KD)
        bsq, brs, bsc, bbi = small[:, 16:18], small[:, 18:20], small[:, 20:22], small[:, 22:24]
        iota_p = small[:, 24:25]
        wam2 = small[:, 25:26]
        wamr = small[:, 26:27]
        sc1, shs, sc2 = small[:, 32:32 + E], small[:, 40:40 + E], small[:, 48:48 + E]
        svx = A[:, 22 * P:22 * P + 6 * NT].rearrange("p (t v) -> p t v", v=6)
        bsv = R[:, NPAD:NPAD + KD * NCH * 6].rearrange("p (k c v) -> p k c v", k=KD, v=6)
        svh = RS[:, 10, 0:6 * NT].rearrange("p (t v) -> p t v", v=6)
        nst = sb("nst", [P, 8, NT], F32)

        HN = [RS[:, 0, :], RS[:, 1, :]]
        V = [RS[:, 2, :], RS[:, 3, :]]
        VT = [RS[:, 4, :], RS[:, 5, :]]
        XH = [RS[:, 6, :].bitcast(F16), RS[:, 7, :].bitcast(F16)]
        WrS = RS[:, 8, 0:KD * E].rearrange("p (k e) -> p k e", k=KD)
        brS = RS[:, 8, 16:16 + E]
        NE = NT * E

        def rt(i):
            return A[:, i * 256:i * 256 + NE].rearrange("p (t e) -> p t e", e=E)
        tri = A[:, 20 * 256:20 * 256 + P]
        valid = A[:, 21 * 256:21 * 256 + NT]
        far = A[:, 21 * 256 + 32:21 * 256 + 32 + NT]
        LO = [A[:, 22 * 256 + 64 * i:22 * 256 + 64 * i + 64].bitcast(F16) for i in range(2)]
        V2 = [A[:, 22 * 256 + 128 + 56 * i:22 * 256 + 128 + 56 * i + ST].bitcast(F16)
              .rearrange("p (v t) -> p v t", v=2) for i in range(2)]
        wts = route[:, 0:2 * NT].rearrange("p (k t) -> p k t", k=2)
        gidx = route[:, 2 * NT:2 * NT + ST].bitcast(I32)
        sidx = route[:, 2 * NT + ST:2 * NT + 2 * ST].bitcast(I32)
        exp_i = route[:, 2 * NT + 2 * ST:2 * NT + 3 * ST].bitcast(I32)
        gi = route[:, 2 * NT + 3 * ST:2 * NT + 3 * ST + U].bitcast(I32)
        si = route[:, 2 * NT + 3 * ST + U:2 * NT + 3 * ST + 2 * U].bitcast(I32)
        XGr = [A[:, 256 * i:256 * i + 256].bitcast(F16) for i in range(U)]
        XT16 = [A[:, 256 * (4 + i):256 * (5 + i)].bitcast(F16).rearrange("p (v k t) -> p v k t", v=2, k=KD)
                for i in range(2)]
        HF = [A[:, 256 * (6 + 4 * i):256 * (10 + 4 * i)] for i in range(2)]
        HHI = [A[:, 256 * (14 + 2 * i):256 * (16 + 2 * i)].bitcast(F16) for i in range(2)]
        HLO = [A[:, 256 * (18 + 2 * i):256 * (20 + 2 * i)].bitcast(F16) for i in range(2)]
        Y = [RS[:, i, :] for i in range(U)]
        FIN = [R[:, 256 * (4 + 2 * i):256 * (6 + 2 * i)].rearrange("p (k d) -> p k d", k=2) for i in range(4)]
        ident16 = oh[:, 0, :].bitcast(F16)

        def ps(name, shape, dt=F32):
            return ctx.enter_context(nc.psum_tensor(name, shape, dt))
        PH = [ps("ph0", [P, 1024]), ps("ph1", [P, 1024])]
        PA = [ps("pa0", [P, 512]), ps("pa1", [P, 512])]
        PB = ps("pb", [P, 512])
        P16 = ps("p16", [P, 1024], F16)
        Q = [PH[0][:, 0:512], PH[0][:, 512:1024], PH[1][:, 0:512], PH[1][:, 512:1024]]

        s_const0, s_const, s_pads = sem("const0"), sem("const"), sem("pads")
        s_edges, s_xlast, s_par, s_gcnw, s_linw = (sem(n) for n in ("edges", "xlast", "par", "gcnw", "linw"))
        s_x = [sem(f"xin{i}") for i in range(4)]
        s_edge_f, s_tmin, s_edge_T, s_tmin_bc, s_span_T = (
            sem(n) for n in ("edge_f", "tmin", "edge_T", "tmin_bc", "span_T"))
        s_dve = sem("dve_chain")
        s_edges_done, s_masks, s_hist, s_degsq, s_dinv = (
            sem(n) for n in ("edges_done", "masks", "hist", "degsq", "dinv"))
        s_par_T, s_params, s_mean, s_sq = (sem(n) for n in ("par_T", "params", "mean", "sq"))
        s_xn, s_xT, s_xTc, s_xw, s_ts, s_tT, s_z0 = (sem(n) for n in ("xn", "xT", "xTc", "xw", "ts", "tT", "z0"))
        s_t_st = [sem(f"t_st{i}") for i in range(2)]
        s_xs_st = [sem(f"xs_st{i}") for i in range(2)]
        s_dinv_T, s_dinv_Tc, s_dinv_st = (sem(n) for n in ("dinv_T", "dinv_Tc", "dinv_st"))
        s_slot = [sem(f"slot{i}") for i in range(SLOTS)]
        s_idx, s_hold, s_oh, s_msg, s_zadd, s_passb, s_passgo = (
            sem(n) for n in ("idx", "hold", "oh", "msg", "zadd", "passb", "passgo"))
        s_xnT_ld, s_xl, s_xlc = (sem(n) for n in ("xnT_ld", "xl", "xlc"))
        s_w_ld, s_w_bias, s_w_fold, s_w_am, s_w_amT, s_w_amr, s_w_bc, s_w_sc, s_w_hi, s_w_lo, s_w_sc0, s_w_am0 = (
            sem(n) for n in ("w_ld", "w_bias", "w_fold", "w_am", "w_amT", "w_amr", "w_bc", "w_sc", "w_hi", "w_lo",
                             "w_sc0", "w_am0"))
        s_gathered, s_gate_ld = sem("gathered"), sem("gate_ld")
        s_dbc = [sem(f"dbc{i}") for i in range(NCH)]
        s_zs, s_tanh, s_gate, s_sig, s_dx, s_dxg, s_mix, s_h = (
            sem(n) for n in ("zs", "tanh", "gate", "sig", "dx", "dxg", "mix", "h"))
        s_bnsq, s_bn = sem("bnsq"), sem("bn")
        s_hn, s_hT, s_x2 = (sem(n) for n in ("hn", "hT", "x2"))
        s_xr = [sem(f"xr{i}") for i in range(5)]
        s_xpad2, s_wr = sem("xpad2"), sem("wr")
        s_var, s_sq1, s_v2, s_sq2 = (sem(n) for n in ("var", "sq1", "v2", "sq2"))
        s_v, s_vT, s_vTc, s_log, s_xhi, s_xlo = (sem(n) for n in ("v", "vT", "vTc", "log", "xhi", "xlo"))
        s_xh_st = [sem(f"xh_st{i}") for i in range(2)]
        s_tri, s_sh, s_exp, s_msum, s_cnt, s_onehots, s_perm, s_routed = (
            sem(n) for n in ("tri", "sh", "exp", "msum", "cnt", "onehots", "perm", "routed"))
        s_b2 = sem("b2")
        s_xg = [sem(f"xg{i}") for i in range(U)]
        s_sc = [sem(f"sc{i}") for i in range(U)]
        s_gcopy, s_xgT, s_xt, s_h1, s_gelu, s_hs, s_y, s_yr = (
            sem(n) for n in ("gcopy", "xgT", "xt", "h1", "gelu", "hs", "y", "yr"))
        s_yload = [sem(f"yload{i}") for i in range(4)]
        s_fin0, s_fin, s_out = sem("fin0"), sem("fin"), sem("out")

        block = ctx.enter_context(nc.Block())
        ds = bass.ds

        def ranges(n, unroll, first=True, last=True):
            return range(0), n

        def col(v, n):
            return v[:, ds(n, 1)]

        @block.sync
        def _(sp):
            for i in range(4):
                sp.dma_start(BR[:, i * XG:(i + 1) * XG, :],
                             x[i * XG * P:(i + 1) * XG * P, :].rearrange("(t p) d -> p t d", p=P)).then_inc(s_x[i], 16)
            sp.wait_ge(s_pads, 3)
            for rows, v in ((edge_d, dst), (edge_s, src)):
                sp.dma_start(rows[0:FULL, :], v[0:FULL * 4 * P].rearrange("(r c) -> r c", c=4 * P)).then_inc(s_edges, 16)
                sp.dma_start(rows[FULL:FULL + 1, 0:TAIL],
                             v[FULL * 4 * P:EDGES].rearrange("(r c) -> r c", r=1)).then_inc(s_edges, 16)
            sp.dma_start(BR[0:LAST, NT - 1, :], x[(NT - 1) * P:N, :]).then_inc(s_xlast, 16)
            sp.dma_start(gcnW, gcn_W.rearrange("(k p) n -> p k n", p=P)).then_inc(s_gcnw, 16)
            sp.dma_start(linWv, lin_W.rearrange("(k p) n -> p k n", p=P)).then_inc(s_linw, 16)

            def store_tile(t, i):
                sp.wait_ge(s_xTc, t + 1)
                sp.dma_start(xnT_dram[:, :, ds(t * P, P)], XS[i].rearrange("p (k n) -> p k n", k=KD)).then_inc(s_xs_st[i], 16)
                sp.wait_ge(s_ts, t + 1)
                sp.dma_start(t_dram[ds(t * P, P), :], TS[i]).then_inc(s_t_st[i], 16)
            with sp.Fori(0, NT // 2) as g:
                for i in range(2):
                    store_tile(g * 2 + i, i)
            store_tile(NT - 1, 0)
            sp.wait_ge(s_dinv_Tc, 1)
            sp.dma_start(dinv_dram[:, :], XN[1][0:NT, 0:P]).then_inc(s_dinv_st, 16)
            sp.wait_ge(s_xs_st[0], 16 * (NT - NT // 2))
            sp.wait_ge(s_xs_st[1], 16 * (NT // 2))
            sp.wait_ge(s_xn, NT)
            sp.dma_start(BT, xnT_dram[:, :, :]).then_inc(s_xnT_ld, 16)

            sp.wait_ge(s_xw, NT)
            with sp.Fori(0, E) as e:
                sp.wait_ge(s_w_lo, e + 1)
                sp.dma_start(SW1, W1[ds(e, 1), :, :].rearrange("a (k p) h -> p (a k) h", p=P)).then_inc(s_w_ld, 16)
            with sp.Fori(0, E) as e:
                sp.wait_ge(s_w_lo, e + (E + 1))
                sp.dma_start(S[:].rearrange("p (c d) -> p c d", c=KH),
                             W2[ds(e, 1), :, :].rearrange("a (c p) d -> p (a c) d", p=P)).then_inc(s_w_ld, 16)
            sp.wait_ge(s_w_lo, 2 * E + 1)
            sp.dma_start(gateW, gate_W.rearrange("(k p) n -> p k n", p=P)).then_inc(s_gate_ld, 16)
            sp.wait_ge(s_gathered, 1)
            sp.wait_ge(s_dinv_st, 16)
            for c in range(NCH):
                sp.dma_start(R[:, c * CH:(c + 1) * CH],
                             dinv_dram.rearrange("t p -> (t p)")[c * CH:(c + 1) * CH].rearrange("(a n) -> a n", a=1)
                             .to_broadcast([P, CH])).then_inc(s_dbc[c], 16)
            sp.wait_ge(s_h, NCH)
            sp.wait_ge(s_xpad2, 1)
            for i in range(4):
                sp.dma_start(BR[:, i * XG:(i + 1) * XG, :],
                             x[i * XG * P:(i + 1) * XG * P, :].rearrange("(t p) d -> p t d", p=P)).then_inc(s_xr[i], 16)
            sp.dma_start(BR[0:LAST, NT - 1, :], x[(NT - 1) * P:N, :]).then_inc(s_xr[4], 16)
            sp.dma_start(WrS, Wr.rearrange("(k p) e -> p k e", p=P)).then_inc(s_wr, 16)
            sp.dma_start(brS, br.rearrange("(a e) -> a e", a=1).to_broadcast([P, E])).then_inc(s_wr, 16)
            sp.dma_start(S[:], b2.rearrange("(a e) d -> a (e d)", a=1).to_broadcast([P, E * D])).then_inc(s_b2, 16)

            def store_token(t, i):
                sp.wait_ge(s_xlo, t + 1)
                sp.dma_start(xn_dram[ds(t * P, P), :], XH[i]).then_inc(s_xh_st[i], 16)
            with sp.Fori(0, NT // 2) as g:
                for i in range(2):
                    store_token(g * 2 + i, i)
            store_token(NT - 1, 0)

            for i in range(U):
                sp.wait_ge(s_sc[i], 16 * NB)

            def load_y(t, i, rows):
                sp.dma_start(FIN[i][0:rows], y_dram[ds(t * 2 * P, 2 * rows), :].rearrange("(p k) d -> p k d", k=2)
                             ).then_inc(s_yload[i], 16)

            def store_out(t, rows):
                sp.wait_ge(s_fin, t + 1)
                sp.dma_start(out[ds(t * P, rows), :], BR[0:rows, ds(t, 1), :].rearrange("p a d -> p (a d)")
                             ).then_inc(s_out, 16)
            for i in range(4):
                load_y(i, i, P)
            with sp.Fori(0, (NT - 1) // 4 - 1) as g:
                for i in range(4):
                    store_out(g * 4 + i, P)
                    load_y(g * 4 + i + 4, i, P)
            store_out(NT - 5, P)
            load_y(NT - 1, 0, LAST)
            for t in range(NT - 4, NT - 1):
                store_out(t, P)
            store_out(NT - 1, LAST)
            sp.wait_ge(s_out, 16 * NT)
            for i in range(2):
                sp.wait_ge(s_t_st[i], 16)

        @block.gpsimd
        def _(pool):
            pool.memset(edge_d, N).then_inc(s_pads, 1)
            pool.memset(edge_s, N).then_inc(s_pads, 1)
            pool.memset(BR[:, NT - 1, :], 0.0).then_inc(s_pads, 1)
            pool.memset(ident[:], 0.0).then_inc(s_const0, 1)
            pool.memset(ones[:], 1.0).then_inc(s_const, 1)
            pool.memset(epst, EPS).then_inc(s_const, 1)
            pool.iota(iota[:], pattern=[[1, P]], base=0, channel_multiplier=0,
                      allow_small_or_imprecise_dtypes=True).then_inc(s_const, 1)
            pool.iota(iota_w[:], pattern=[[1, WINDOW]], base=0, channel_multiplier=0,
                      allow_small_or_imprecise_dtypes=True).then_inc(s_const, 1)
            pool.iota(iota_p, pattern=[[1, 1]], base=0, channel_multiplier=1,
                      allow_small_or_imprecise_dtypes=True).then_inc(s_const, 1)
            pool.wait_ge(s_const0, 1)
            pool.affine_select(out=ident[:], in_=ident[:], compare_op=ALU.not_equal, fill=1.0, base=0,
                               pattern=[[-1, P]], channel_multiplier=1).then_inc(s_const, 1)

            pool.wait_ge(s_t_st[0], 16 * (NT - NT // 2))
            pool.wait_ge(s_t_st[1], 16 * (NT // 2))
            pool.wait_ge(s_edges_done, 1)
            pool.wait_ge(s_tT, NT)
            pool.wait_ge(s_dinv_st, 16)
            pool.wait_ge(s_xs_st[0], 16 * (NT - NT // 2))
            pool.wait_ge(s_xs_st[1], 16 * (NT // 2))

            def gather_body(n0, c0, round0):
                for r in range(2):
                    pool.tensor_copy(idx_ring[:, r * SLOTS:(r + 1) * SLOTS],
                                     src_i[:, ds(c0 + r * SLOTS, SLOTS)]).then_inc(s_idx, 1)
                    pool.wait_ge(s_idx, round0 + (r + 1))
                    for j in range(SLOTS):
                        pool.wait_ge(s_msg, n0 + (r * SLOTS + j + 1))
                        pool.sem_inc(s_hold, 1)
                        pool.indirect_dma_start(
                            out=RS[:, j, :], out_offset=None, in_=t_dram[:, :],
                            in_offset=bass.IndirectOffsetOnAxis(ap=idx_ring[:, r * SLOTS + j:r * SLOTS + j + 1], axis=0),
                        ).then_inc(s_slot[j], 16)

            with pool.Fori(0, 2 * E) as b:
                gather_body(b * BODY, b * BODY, b * 2)
            pool.wait_ge(s_edges_done, 1)
            npass = pool.value_load(npass_i[:, 2:3], min_val=1, max_val=NPAD // WINDOW)
            with pool.If(npass > 1):
                with pool.Fori(1, npass) as w:
                    with pool.Fori(0, 2 * E) as b:
                        gather_body(w * ET + b * BODY, b * BODY, w * (4 * E) + b * 2)

            def dx(c):
                pool.wait_ge(s_tanh, c + 1)
                pool.wait_ge(s_dxg, c + 1)
                pool.tensor_tensor(DX, AT[:, :, ds(c * CH, CH)], BT[:, :, ds(c * CH, CH)], ALU.subtract).then_inc(s_dx, 1)
            pool.wait_ge(s_xlc, NCH)
            with pool.Fori(0, NCH) as c:
                dx(c)
            pool.wait_ge(s_h, NCH)
            pool.memset(BR[:, NT - 1, :], 0.0).then_inc(s_xpad2, 1)
            pool.wait_ge(s_hn, NT)
            pool.affine_select(out=tri, in_=ones[:], compare_op=ALU.is_gt, fill=0.0, base=0,
                               pattern=[[1, P]], channel_multiplier=-1).then_inc(s_tri, 1)
            pool.affine_select(out=valid, in_=ones[:, 0:NT], compare_op=ALU.is_ge, fill=0.0, base=N - 1,
                               pattern=[[-P, NT]], channel_multiplier=-1).then_inc(s_tri, 1)
            slot_id = A[:, 21 * 256 + 64:21 * 256 + 64 + ST]
            pool.iota(slot_id, pattern=[[P, ST]], base=DUMP, channel_multiplier=1,
                      allow_small_or_imprecise_dtypes=True).then_inc(s_tri, 1)

            pool.wait_ge(s_routed, 1)
            pool.wait_ge(s_xh_st[0], 16 * (NT - NT // 2))
            pool.wait_ge(s_xh_st[1], 16 * (NT // 2))

            def gather_x(n, j, count):
                if not (isinstance(n, int) and n < U):
                    pool.wait_ge(s_xgT, n - (U - 1))
                pool.tensor_copy(gi[:, j:j + 1], gidx[:, ds(n, 1)]).then_inc(s_gcopy, 1)
                pool.wait_ge(s_gcopy, count)
                pool.sem_inc(s_hold, 1)
                pool.indirect_dma_start(out=XGr[j], out_offset=None, in_=xn_dram[:, :],
                                        in_offset=bass.IndirectOffsetOnAxis(ap=gi[:, j:j + 1], axis=0)
                                        ).then_inc(s_xg[j], 16)

            def scatter_y(n, b, j, count, first):
                if not first:
                    pool.wait_ge(s_sc[j], b * 16)
                pool.tensor_copy(si[:, j:j + 1], sidx[:, ds(n, 1)]).then_inc(s_gcopy, 1)
                pool.wait_ge(s_gcopy, count)
                pool.wait_ge(s_yr, n + 1)
                pool.sem_inc(s_hold, 1)
                pool.indirect_dma_start(out=y_dram[:, :],
                                        out_offset=bass.IndirectOffsetOnAxis(ap=si[:, j:j + 1], axis=0),
                                        in_=Y[j], in_offset=None).then_inc(s_sc[j], 16)

            def turn(b, first, last):
                for j in range(U):
                    n = b * U + j
                    ahead = not last or j < U - 3
                    if ahead:
                        gather_x(n + 3, (j + 3) % U, n * 2 + 4)
                        scatter_y(n, b, j, n * 2 + 5, first)
                    else:
                        scatter_y(n, b, j, n + (ST - 3) + 4, first)
            for n in range(3):
                gather_x(n, n, n + 1)
            turn(0, True, False)
            with pool.Fori(1, NB - 1) as b:
                turn(b, False, False)
            turn(NB - 1, False, True)

        @block.scalar
        def _(act):
            rows = [(b1.rearrange("e (c p) -> (e c) p", p=P), E * KH), (ln_g.rearrange("e (k p) -> (e k) p", p=P), E * KD),
                    (ln_b.rearrange("e (k p) -> (e k) p", p=P), E * KD)]
            rows += [(v.rearrange("(k p) -> k p", p=P), KD) for v in (gcn_b, lin_b, gate_b, bn_gamma, bn_beta)]
            r0 = 0
            for v, n in rows:
                act.dma_start(prow[r0:r0 + n, :], v).then_inc(s_par, 16)
                r0 += n
            act.wait_ge(s_mean, 1)
            act.activation(nst[:, 3, :], nst[:, 2, :], ACT.Sqrt, bias=epst, scale=1.0 / D).then_inc(s_sq, 1)
            act.wait_ge(s_hist, 1)
            act.activation(nst[:, 4, :], Q[0][:, 0:NT], ACT.Sqrt, bias=ones[:, 0:1]).then_inc(s_degsq, 1)
            act.wait_ge(s_edges_done, 1)
            act.wait_ge(s_span_T, 1)

            def tile(t, i, first):
                act.wait_ge(s_xT, t + 1)
                if not first:
                    g = (t - i) // 2 if isinstance(t, int) else None
                    act.wait_ge(s_xs_st[i], xs_count(t, i))
                    act.wait_ge(s_xw, t - 1)
                act.activation(XS[i], PA[i][:, 0:D], ACT.Copy).then_inc(s_xTc, 1)
                act.wait_ge(s_xw, t + 1)
                if not first:
                    act.wait_ge(s_t_st[i], xs_count(t, i))
                    act.wait_ge(s_tT, t - 1)
                act.activation(TS[i], PA[i][:, D:2 * D], ACT.Copy, scale=dinv[:, ds(t, 1)]).then_inc(s_ts, 1)

            def xs_count(t, i):
                return (t - i) * 8
            act.wait_ge(s_dinv, 1)
            for i in range(2):
                tile(i, i, True)
            with act.Fori(1, NT // 2) as g:
                for i in range(2):
                    tile(g * 2 + i, i, False)
            tile(NT - 1, 0, False)

            def hi_part(u, e, dest, k0):
                act.wait_ge(s_w_sc, k0)
                act.activation(dest, S[:].rearrange("p (a n) -> p a n", a=dest.shape[1]), ACT.Copy, scale=wsc).then_inc(s_w_hi, 1)
            act.wait_ge(s_params, 1)
            with act.Fori(0, E) as e:
                act.wait_ge(s_xl, e + 1)
                for m in range(KD):
                    last = act.activation(BT[:, m, ds(e * CH, CH)], PH[1][:, m * 512:m * 512 + CH], ACT.Identity,
                                          bias=params[:, CV + KD + m:CV + KD + m + 1])
                last.then_inc(s_xlc, 1)
                act.wait_ge(s_w_sc, e + 1)
                act.activation(W1hi[:, ds(e, 1), :, :].rearrange("p a k h -> p (a k h)"), S[:], ACT.Copy,
                               scale=wsc).then_inc(s_w_hi, 1)
            with act.Fori(0, E) as e:
                act.wait_ge(s_w_sc, e + (E + 1))
                act.activation(W2hi[:, ds(e, 1), :, :].rearrange("p a c d -> p (a c d)"), S[:], ACT.Copy,
                               scale=wsc).then_inc(s_w_hi, 1)

            def tanh(c):
                act.wait_ge(s_zs, c + 1)
                for m in range(KD):
                    last = act.activation(AT[:, m, ds(c * CH, CH)], AT[:, m, ds(c * CH, CH)], ACT.Tanh,
                                          bias=params[:, CV + m:CV + m + 1])
                last.then_inc(s_tanh, 1)
            with act.Fori(0, NCH) as c:
                tanh(c)
            with act.Fori(0, NCH // 2) as g:
                for i in range(2):
                    act.wait_ge(s_gate, g * 2 + i + 1)
                    for m in range(KD):
                        last = act.activation(PH[i][:, m * 512:m * 512 + CH], PH[i][:, m * 512:m * 512 + CH], ACT.Sigmoid,
                                              bias=params[:, CV + 2 * KD + m:CV + 2 * KD + m + 1])
                    last.then_inc(s_sig, 1)
            act.wait_ge(s_bnsq, 1)
            act.activation(bsq, bmv[:, :, 1:2].rearrange("p k a -> p (k a)"), ACT.Sqrt, bias=epst).then_inc(s_bnsq, 1)
            act.wait_ge(s_bn, 1)

            def norm_tile(t, i, first):
                if not first:
                    act.wait_ge(s_hT, t - 1)
                for m in range(KD):
                    last = act.activation(HN[i][:, m * P:(m + 1) * P], AT[:, m, ds(t * P, P)], ACT.Identity,
                                          bias=bbi[:, m:m + 1], scale=bsc[:, m:m + 1])
                last.then_inc(s_hn, 1)
            for i in range(2):
                norm_tile(i, i, True)
            with act.Fori(1, NT // 2) as g:
                for i in range(2):
                    norm_tile(g * 2 + i, i, False)
            norm_tile(NT - 1, 0, False)
            act.wait_ge(s_var, 1)
            act.activation(nst[:, 3, :], nst[:, 2, :], ACT.Sqrt, bias=epst, scale=1.0 / D).then_inc(s_sq1, 1)
            act.wait_ge(s_v2, 1)
            act.activation(nst[:, 5, :], nst[:, 4, :], ACT.Sqrt, bias=epst, scale=1.0 / D).then_inc(s_sq2, 1)

            def token(t, i, first):
                act.wait_ge(s_v, t + 1)
                if not first:
                    act.wait_ge(s_xh_st[i], (t - i) * 8)
                act.activation(XH[i][:, 0:D], V[i], ACT.Copy).then_inc(s_xhi, 1)
                act.wait_ge(s_vT, t + 1)
                if not first:
                    act.wait_ge(s_log, t - 1)
                act.activation(VT[i], PA[i][:, 0:D], ACT.Copy).then_inc(s_vTc, 1)
            for i in range(2):
                token(i, i, True)
            with act.Fori(1, NT // 2) as g:
                for i in range(2):
                    token(g * 2 + i, i, False)
            token(NT - 1, 0, False)
            act.wait_ge(s_sh, 1)
            act.activation(rt(1), rt(1), ACT.Exp).then_inc(s_exp, 1)

            act.wait_ge(s_routed, 1)

            def turn(b, first, last):
                for j in range(U):
                    n, i = b * U + j, j % 2
                    e = act.value_load(exp_i[0:1, ds(n, 1)], min_val=0, max_val=E - 1)
                    act.wait_ge(s_xgT, n + 1)
                    if not (first and j < 2):
                        act.wait_ge(s_h1, (n - 1) * 2)
                    act.activation(XT16[i].rearrange("p v k t -> p (v k t)"), P16[:, i * 512:(i + 1) * 512],
                                   ACT.Copy).then_inc(s_xt, 1)
                    for c in range(KH):
                        if c % (KH // 2) == 0:
                            act.wait_ge(s_h1, n * 2 + (1 + 2 * c // KH))
                        if c == 0 and not (first and j < 2):
                            act.wait_ge(s_hs, (n - 1) * 4)
                        act.activation(HF[i][:, c * P:(c + 1) * P], PH[i][:, c * P:(c + 1) * P], ACT.Gelu,
                                       bias=params[:, ds(e * KH + c, 1)], scale=sc1[:, ds(e, 1)]).then_inc(s_gelu, 1)
            turn(0, True, False)
            with act.Fori(1, NB) as b:
                turn(b, False, False)

        @block.tensor
        def _(pe):
            pe.wait_ge(s_const, 6)
            pe.wait_ge(s_edge_f, 2)
            for k, rows in enumerate((edge_df, edge_sf)):
                for c in range(4):
                    last = pe.transpose(Q[k][:, c * ROWS:(c + 1) * ROWS], rows[0:ROWS, c * P:(c + 1) * P],
                                        ident[0:ROWS, 0:ROWS])
                last.then_inc(s_edge_T, 1)
            pe.wait_ge(s_tmin, 5)
            for c in range(4):
                last = pe.matmul(Q[2][:, c * ROWS:(c + 1) * ROWS], tmin_w[0:ROWS, c * P:(c + 1) * P],
                                 ident[0:ROWS, 0:ROWS], start=True, stop=True)
            last.then_inc(s_tmin_bc, 1)
            pe.transpose(Q[3][0:1, 0:ROWS], tspan[0:ROWS, :], ident[0:ROWS, 0:ROWS]).then_inc(s_span_T, 1)
            pe.wait_ge(s_par, 16 * 8)
            pe.transpose(PB[:, 0:PROWS], prow[0:PROWS, :], ident[0:PROWS, 0:PROWS]).then_inc(s_par_T, 1)

            pe.wait_ge(s_masks, 1)

            def count(g, first, last):
                for j in range(8):
                    t = g * 8 + j
                    mm = pe.matmul(Q[0][:, 0:NT], mask_lo[:, :, ds(t, 1)].rearrange("p k a -> p (k a)"),
                                   mask_hi[:, :, ds(t, 1)].rearrange("p k a -> p (k a)"),
                                   start=first and j == 0, stop=last and j == 7)
                return mm
            count(0, True, False)
            with pe.Fori(1, ET // 8 - 1) as g:
                count(g, False, False)
            count(ET // 8 - 1, False, True).then_inc(s_hist, 1)

            pe.wait_ge(s_gcnw, 16)

            def tile(t, i, first):
                pe.wait_ge(s_xn, t + 1)
                if not first:
                    pe.wait_ge(s_ts, t - 1)
                for k in range(KD):
                    last = pe.transpose(PA[i][:, k * P:(k + 1) * P], XN[i][:, k * P:(k + 1) * P], ident[:])
                last.then_inc(s_xT, 1)
                pe.wait_ge(s_xTc, t + 1)
                for k in range(KD):
                    last = pe.matmul(PA[i][:, D:2 * D], XS[i][:, k * P:(k + 1) * P], gcnW[:, k, :],
                                     start=(k == 0), stop=(k == KD - 1))
                last.then_inc(s_xw, 1)
                pe.wait_ge(s_ts, t + 1)
                if not first:
                    pe.wait_ge(s_z0, t - 1)
                for k in range(KD):
                    last = pe.transpose(PH[i][:, k * P:(k + 1) * P], TS[i][:, k * P:(k + 1) * P], ident[:])
                last.then_inc(s_tT, 1)
            for i in range(2):
                tile(i, i, True)
            with pe.Fori(1, NT // 2) as g:
                for i in range(2):
                    tile(g * 2 + i, i, False)
            tile(NT - 1, 0, False)
            pe.transpose(PB[0:NT, 128:256], dinv[:], ident[:]).then_inc(s_dinv_T, 1)
            pe.wait_ge(s_z0, NT)

            def sums(n0, round0, r):
                for j in range(SLOTS):
                    k = r * SLOTS + j
                    i = k % 2
                    pe.wait_ge(s_slot[j], (round0 + r + 1) * 16)
                    pe.wait_ge(s_oh, n0 + (k + 1))
                    pe.wait_ge(s_zadd, n0 + (k + 1))
                    for m in range(KD):
                        last = pe.matmul(PA[i][:, m * WINDOW:(m + 1) * WINDOW], RS[:, j, m * P:(m + 1) * P],
                                         oh[:, i, :], start=True, stop=True)
                    last.then_inc(s_msg, 1)

            pe.sem_inc(s_msg, SLOTS)
            pe.wait_ge(s_linw, 16)
            pe.wait_ge(s_xnT_ld, 16)
            pe.wait_ge(s_params, 1)

            def top(u):
                pe.wait_ge(s_w_am, u + 1)
                pe.transpose(PB[0:1, 128:256], wam, ident[:]).then_inc(s_w_amT, 1)

            def spread(u):
                pe.wait_ge(s_w_amr, u + 1)
                pe.matmul(PB[:, 256:257], ones[0:1, :], wamr[0:1, :], start=True, stop=True).then_inc(s_w_bc, 1)
            with pe.Fori(0, E) as e:
                pe.wait_ge(s_w_ld, (e + 1) * 16)
                for c in range(KH):
                    for k in range(KD):
                        last = pe.matmul(PB[:, c:c + 1], SW1[:, k, c * P:(c + 1) * P],
                                         params[:, ds(e * KD + (CB + k), 1)], start=(k == 0), stop=(k == KD - 1))
                last.then_inc(s_w_bias, 1)
                sums(e * BODY, e * 2, 0)
                top(e)
                spread(e)
                for m in range(KD):
                    for k in range(KD):
                        last = pe.matmul(PH[1][:, m * 512:m * 512 + CH], linWv[:, k, m * P:(m + 1) * P],
                                         BT[:, k, ds(e * CH, CH)], start=(k == 0), stop=(k == KD - 1))
                last.then_inc(s_xl, 1)
                sums(e * BODY, e * 2, 1)
                pe.wait_ge(s_xlc, e + 1)
            with pe.Fori(0, E) as e:
                sums(e * BODY + E * BODY, e * 2 + 2 * E, 0)
                top(e + E)
                spread(e + E)
                sums(e * BODY + E * BODY, e * 2 + 2 * E, 1)
            npass = pe.value_load(npass_i[:, 2:3], min_val=1, max_val=NPAD // WINDOW)
            with pe.If(npass > 1):
                with pe.Fori(1, npass) as w:
                    with pe.Fori(0, 2 * E) as b:
                        for r in range(2):
                            sums(w * ET + b * BODY, w * (4 * E) + b * 2, r)

            pe.wait_ge(s_gate_ld, 16)

            def gate(c, i, first):
                pe.wait_ge(s_tanh, c + 1)
                if not first:
                    pe.wait_ge(s_dxg, c)
                for m in range(KD):
                    for k in range(KD):
                        last = pe.matmul(PH[i][:, m * 512:m * 512 + CH], gateW[:, k, m * P:(m + 1) * P],
                                         AT[:, k, ds(c * CH, CH)], start=(k == 0), stop=(k == KD - 1))
                last.then_inc(s_gate, 1)
            for i in range(2):
                gate(i, i, True)
            with pe.Fori(1, NCH // 2) as g:
                for i in range(2):
                    gate(g * 2 + i, i, False)

            def rows_of(t, i, first):
                pe.wait_ge(s_hn, t + 1)
                if not first:
                    pe.wait_ge(s_x2, t - 1)
                for k in range(KD):
                    last = pe.transpose(PA[i][:, k * P:(k + 1) * P], HN[i][:, k * P:(k + 1) * P], ident[:])
                last.then_inc(s_hT, 1)
            for i in range(2):
                rows_of(i, i, True)
            with pe.Fori(1, NT // 2) as g:
                for i in range(2):
                    rows_of(g * 2 + i, i, False)
            rows_of(NT - 1, 0, False)

            pe.wait_ge(s_wr, 32)

            def router(t, i, first):
                pe.wait_ge(s_v, t + 1)
                if not first:
                    pe.wait_ge(s_vTc, t - 1)
                for k in range(KD):
                    last = pe.transpose(PA[i][:, k * P:(k + 1) * P], V[i][:, k * P:(k + 1) * P], ident[:])
                last.then_inc(s_vT, 1)
                pe.wait_ge(s_vTc, t + 1)
                for k in range(KD):
                    last = pe.matmul(PB[:, ds(t * E, E)], VT[i][:, k * P:(k + 1) * P], WrS[:, k, :],
                                     start=(k == 0), stop=(k == KD - 1))
                last.then_inc(s_log, 1)
            pe.wait_ge(s_x2, NT)
            for i in range(2):
                router(i, i, True)
            with pe.Fori(1, NT // 2) as g:
                for i in range(2):
                    router(g * 2 + i, i, False)
            router(NT - 1, 0, False)

            pe.wait_ge(s_msum, 1)
            pe.wait_ge(s_tri, 3)
            pe.matmul(Q[0][:, 0:NE], tri, rt(6).rearrange("p t e -> p (t e)"), start=True, stop=True)
            pe.matmul(Q[1][:, 0:NE], ones[:], rt(6).rearrange("p t e -> p (t e)"), start=True, stop=True).then_inc(s_cnt, 1)

            def place(g, first, last):
                for i in range(2):
                    pe.wait_ge(s_onehots, g * 2 + i + 1)
                    mm = pe.matmul(Q[2][:, 0:2 * ST], LO[i], V2[i].rearrange("p v t -> p (v t)"),
                                   start=first and i == 0, stop=last and i == 1)
                    mm.then_inc(s_perm, 1)
            place(0, True, False)
            with pe.Fori(1, NT - 1) as g:
                place(g, False, False)
            place(NT - 1, False, True)

            pe.wait_ge(s_routed, 1)

            def tokens_T(n, b, j, first):
                pe.wait_ge(s_xg[j], (b + 1) * 16)
                if not first:
                    pe.wait_ge(s_xt, n)
                for k in range(4):
                    last = pe.transpose(P16[:, (j % 2) * 512 + k * P:(j % 2) * 512 + (k + 1) * P],
                                        XGr[j][:, k * P:(k + 1) * P], ident16)
                last.then_inc(s_xgT, 1)

            def up(n, j, first):
                i = j % 2
                e = pe.value_load(exp_i[0:1, ds(n, 1)], min_val=0, max_val=E - 1)
                pe.wait_ge(s_xt, n + 1)
                for c in range(KH):
                    if not first and c % (KH // 2) == 0:
                        pe.wait_ge(s_gelu, (n - 2) * KH + (c + KH // 2))
                    q = 0
                    for k in range(KD):
                        for w, v in ((W1hi, 0), (W1hi, 1), (W1lo, 0)):
                            last = pe.matmul(PH[i][:, c * P:(c + 1) * P],
                                             w[:, ds(e, 1), k, c * P:(c + 1) * P].rearrange("p a h -> p (a h)"),
                                             XT16[i][:, v, k, :], start=(q == 0), stop=(q == 3 * KD - 1))
                            q += 1
                    if (c + 1) % (KH // 2) == 0:
                        last.then_inc(s_h1, 1)

            def down(n, j, first):
                i = j % 2
                e = pe.value_load(exp_i[0:1, ds(n, 1)], min_val=0, max_val=E - 1)
                if not first:
                    pe.wait_ge(s_yr, n - 1)
                q = 0
                for half in range(2):
                    pe.wait_ge(s_hs, n * 4 + 2 * (half + 1))
                    for c in range(half * KH // 2, (half + 1) * KH // 2):
                        for h, w in ((HHI, W2hi), (HLO, W2hi), (HHI, W2lo)):
                            last = pe.matmul(PA[i][:, 0:D], h[i][:, c * P:(c + 1) * P],
                                             w[:, ds(e, 1), c, :].rearrange("p a d -> p (a d)"),
                                             start=(q == 0), stop=(q == 3 * KH - 1))
                            q += 1
                last.then_inc(s_y, 1)

            def turn(b, first, last):
                for j in range(U):
                    n = b * U + j
                    if not (last and j == U - 1):
                        tokens_T(n + 1, b if j < U - 1 else b + 1, (j + 1) % U, False)
                    up(n, j, first and j < 2)
                    if not (first and j == 0):
                        down(n - 1, (j - 1) % U, first and j < 3)
            tokens_T(0, 0, 0, True)
            turn(0, True, False)
            with pe.Fori(1, NB - 1) as b:
                turn(b, False, False)
            turn(NB - 1, False, True)
            down(ST - 1, U - 1, False)

        @block.vector
        def _(dve):
            made = [0]

            def link(ins):
                made[0] += 1
                ins.then_inc(s_dve, 1)
                dve.wait_ge(s_dve, made[0])

            dve.wait_ge(s_edges, 64)
            dve.tensor_copy(edge_df[0:ROWS, :], edge_d[0:ROWS, :]).then_inc(s_edge_f, 1)
            dve.tensor_copy(edge_sf[0:ROWS, :], edge_s[0:ROWS, :]).then_inc(s_edge_f, 1)
            dve.wait_ge(s_edge_f, 2)
            dve.wait_ge(s_const, 6)
            edv = edge_df[0:ROWS, :].rearrange("r (c p) -> r c p", c=4)
            dve.tensor_reduce(tmin[0:ROWS, :], edv, AX, ALU.min)
            link(dve.tensor_reduce(tmax[0:ROWS, :], edv, AX, ALU.max))
            for c in range(4):
                dve.tensor_scalar(tmin_w[0:ROWS, c * P:(c + 1) * P], ones[0:ROWS, :], tmin[0:ROWS, c:c + 1], None,
                                  ALU.mult).then_inc(s_tmin, 1)
            link(dve.tensor_tensor(tdif[0:ROWS, :], tmax[0:ROWS, :], tmin[0:ROWS, :], ALU.subtract))
            dve.tensor_reduce(tspan[0:ROWS, :], tdif[0:ROWS, :], AX, ALU.max).then_inc(s_tmin, 1)

            def tiles_of(v):
                return v.rearrange("p (q c) -> p q c", c=4)

            def rows4(q):
                return q[:, 0:ET].rearrange("p (c q) -> p q c", c=4)
            dve.wait_ge(s_edge_T, 2)
            dve.tensor_copy(tiles_of(src_i[:]), rows4(Q[1]))
            link(dve.tensor_copy(tiles_of(dst_f), rows4(Q[0])))
            dve.wait_ge(s_tmin_bc, 1)
            dve.tensor_tensor(tiles_of(dst_rel[:]), tiles_of(dst_f), rows4(Q[2]), ALU.subtract)
            dve.tensor_scalar(tiles_of(base_i[:]), rows4(Q[2])[0:1], float(NPAD - WINDOW), None, ALU.min)
            dve.wait_ge(s_span_T, 1)
            link(dve.tensor_reduce(npass_f, Q[3][0:1, 0:ROWS], AX, ALU.max))
            link(dve.tensor_copy(npass_i[:, 0:1], npass_f))
            link(dve.tensor_scalar(npass_i[:, 1:2], npass_i[:, 0:1], WINDOW.bit_length() - 1, None, ALU.arith_shift_right))
            link(dve.tensor_scalar(npass_i[:, 2:3], npass_i[:, 1:2], 1.0, None, ALU.add))
            link(dve.tensor_copy(dst_i, dst_f))
            link(dve.tensor_scalar(lohi_i, dst_i, P - 1, None, ALU.bitwise_and))
            link(dve.tensor_copy(lo16, lohi_i))
            link(dve.tensor_scalar(lohi_i, dst_i, P.bit_length() - 1, None, ALU.arith_shift_right))
            link(dve.tensor_copy(hi16, lohi_i))
            dve.wait_ge(s_par_T, 1)
            dve.tensor_copy(params[:], PB[:, 0:PROWS]).then_inc(s_params, 1)
            dve.sem_inc(s_edges_done, 1)

            def combine(sv):
                m_e, q_e, m_o, q_o = (sv[:, :, v:v + 1].rearrange("p t a -> p (t a)") for v in (1, 2, 4, 5))
                dve.tensor_tensor(nst[:, 0, :], m_e, m_o, ALU.add)
                dve.tensor_tensor(nst[:, 2, :], q_e, q_o, ALU.add)
                link(dve.tensor_tensor(nst[:, 1, :], m_e, m_o, ALU.subtract))
                link(dve.tensor_tensor(nst[:, 1, :], nst[:, 1, :], nst[:, 1, :], ALU.mult))
                dve.tensor_scalar(nst[:, 0, :], nst[:, 0, :], 0.5, None, ALU.mult)
                return dve.scalar_tensor_tensor(out=nst[:, 2, :], in0=nst[:, 1, :], scalar=D / 4.0, in1=nst[:, 2, :],
                                                op0=ALU.mult, op1=ALU.add)
            for i in range(4):
                dve.wait_ge(s_x[i], 16)
                with dve.Fori(i * XG, (i + 1) * XG) as t:
                    dve.bn_stats(svx[:, ds(t, 1), :].rearrange("p a v -> p (a v)"),
                                 BR[:, ds(t, 1), :].rearrange("p a d -> p (a d)"))
            dve.wait_ge(s_xlast, 16)
            link(dve.bn_stats(svx[:, NT - 1, :], BR[:, NT - 1, :]))
            combine(svx).then_inc(s_mean, 1)

            with dve.Fori(0, P // 8) as g:
                for j in range(8):
                    dve.tensor_scalar(mask_lo[:, ds(g * 8 + j, 1), :].rearrange("p a t -> p (a t)"), lo16,
                                      iota[:, ds(g * 8 + j, 1)], None, ALU.is_equal)
            for j in range(NT):
                last = dve.tensor_scalar(mask_hi[:, j, :], hi16, float(j), None, ALU.is_equal)
            last.then_inc(s_masks, 1)
            dve.wait_ge(s_sq, 1)
            dve.reciprocal(nst[:, 6, :], nst[:, 3, :]).then_inc(s_sq, 1)
            dve.wait_ge(s_degsq, 1)
            dve.reciprocal(dinv[:], nst[:, 4, :]).then_inc(s_dinv, 1)
            dve.wait_ge(s_sq, 2)

            def xn_tile(t, i, first):
                if not first:
                    dve.wait_ge(s_xT, t - 1)
                dve.tensor_scalar(XN[i], BR[:, ds(t, 1), :].rearrange("p a d -> p (a d)"), nst[:, 0, ds(t, 1)],
                                  nst[:, 6, ds(t, 1)], ALU.subtract, ALU.mult).then_inc(s_xn, 1)

            def z0_tile(t, i):
                dve.wait_ge(s_tT, t + 1)
                dve.tensor_copy(AT[:, :, ds(t * P, P)], PH[i][:, 0:D].rearrange("p (k n) -> p k n", k=KD)).then_inc(s_z0, 1)
            for i in range(2):
                xn_tile(i, i, True)
            with dve.Fori(1, NT // 2) as g:
                for i in range(2):
                    xn_tile(g * 2 + i, i, False)
                    z0_tile(g * 2 + (i - 2), i)
            xn_tile(NT - 1, 0, False)
            for t in range(NT - 3, NT):
                z0_tile(t, t % 2)
            dve.wait_ge(s_dinv_T, 1)
            dve.wait_ge(s_xT, NT)
            dve.tensor_copy(XN[1][0:NT, 0:P], PB[0:NT, 128:256]).then_inc(s_dinv_Tc, 1)

            def onehot(n0, c0, k):
                dve.wait_ge(s_msg, n0 + (SLOTS - 1 + k))
                dve.tensor_scalar(oh[:, k % 2, :], iota_w[:], dst_rel[:, ds(c0 + k, 1)], None, ALU.is_equal).then_inc(s_oh, 1)

            def add(n0, c0, k):
                base = dve.value_load(base_i[0:1, ds(c0 + k, 1)], min_val=0, max_val=NPAD - WINDOW)
                dve.wait_ge(s_msg, n0 + (SLOTS + k + 1))
                dve.wait_ge(s_zadd, n0 + (k + 2))
                z = AT[:, :, ds(base, WINDOW)]
                dve.tensor_tensor(z, z, PA[k % 2][:, 0:KD * WINDOW].rearrange("p (m w) -> p m w", m=KD),
                                  ALU.add).then_inc(s_zadd, 1)

            def adds(n0, c0, r):
                if r == 0:
                    onehot(n0, c0, 0)
                for k in range(r * SLOTS, (r + 1) * SLOTS):
                    if k + 1 < BODY:
                        onehot(n0, c0, k + 1)
                    add(n0, c0, k)

            def scale(u, sum2):
                dve.wait_ge(s_w_amT, u + 1)
                dve.tensor_reduce(wamr[0:1, :], PB[0:1, 128:256], AX, ALU.max).then_inc(s_w_amr, 1)
                dve.wait_ge(s_w_bc, u + 1)
                dve.tensor_scalar(wmax, PB[:, 256:257], 1e-30, None, ALU.max).then_inc(s_w_sc0, 1)
                dve.wait_ge(s_w_sc0, u * 3 + 1)
                dve.tensor_scalar(wp2.bitcast(I32), wmax.bitcast(I32), EXPONENT, None, ALU.bitwise_and).then_inc(s_w_sc0, 1)
                dve.wait_ge(s_w_sc0, u * 3 + 2)
                dve.reciprocal(wmax, wp2).then_inc(s_w_sc0, 1)
                dve.wait_ge(s_w_sc0, u * 3 + 3)

            def low_part(u, dest, hi):
                dve.wait_ge(s_w_hi, u + 1)
                dve.scalar_tensor_tensor(out=dest, in0=S[:], scalar=wsc, in1=hi, op0=ALU.mult,
                                         op1=ALU.subtract).then_inc(s_w_lo, 1)

            dve.sem_inc(s_zadd, 2)
            dve.wait_ge(s_z0, NT)
            dve.sem_inc(s_w_lo, 1)
            with dve.Fori(0, E) as e:
                dve.wait_ge(s_w_bias, e + 1)
                bcol = params[:, ds(e * KH, KH)]
                dve.tensor_tensor(bcol, bcol, PB[:, 0:KH], ALU.add).then_inc(s_w_fold, 1)
                for k in range(KD):
                    dve.tensor_scalar(SW1[:, k, :], SW1[:, k, :], params[:, ds(e * KD + (CG + k), 1)], None,
                                      ALU.mult).then_inc(s_w_fold, 1)
                dve.wait_ge(s_w_fold, e * 3 + 3)
                dve.tensor_reduce(wam, S[:], AX, ALU.max, apply_absolute_value=True).then_inc(s_w_am0, 1)
                dve.tensor_reduce(wam2, bcol, AX, ALU.max, apply_absolute_value=True).then_inc(s_w_am0, 1)
                dve.wait_ge(s_w_am0, e * 2 + 2)
                dve.scalar_tensor_tensor(out=wam, in0=wam, scalar=float(D), in1=wam2, op0=ALU.mult,
                                         op1=ALU.max).then_inc(s_w_am, 1)
                adds(e * BODY, e * BODY, 0)
                scale(e, True)
                dve.tensor_scalar(sc1[:, ds(e, 1)], wp2, 2.0 ** -21 / XN_SCALE, None, ALU.mult)
                dve.tensor_scalar(shs[:, ds(e, 1)], wmax, 2.0 ** 13, None, ALU.mult)
                dve.tensor_scalar(sc2[:, ds(e, 1)], wp2, 2.0 ** -13, None, ALU.mult)
                dve.tensor_scalar(wsc, wmax, 2.0 ** 21, None, ALU.mult).then_inc(s_w_sc, 1)
                adds(e * BODY, e * BODY, 1)
                low_part(e, W1lo[:, ds(e, 1), :, :].rearrange("p a k h -> p (a k h)"),
                         W1hi[:, ds(e, 1), :, :].rearrange("p a k h -> p (a k h)"))
            with dve.Fori(0, E) as e:
                dve.wait_ge(s_w_ld, (e + (E + 1)) * 16)
                dve.tensor_reduce(wam, S[:], AX, ALU.max, apply_absolute_value=True).then_inc(s_w_am, 1)
                adds((e + E) * BODY, (e + E) * BODY, 0)
                scale(e + E, False)
                dve.scalar_tensor_tensor(out=sc2[:, ds(e, 1)], in0=sc2[:, ds(e, 1)], scalar=2.0 ** -13, in1=wp2,
                                         op0=ALU.mult, op1=ALU.mult)
                dve.tensor_scalar(wsc, wmax, 2.0 ** 13, None, ALU.mult).then_inc(s_w_sc, 1)
                adds((e + E) * BODY, (e + E) * BODY, 1)
                low_part(e + E, W2lo[:, ds(e, 1), :, :].rearrange("p a c d -> p (a c d)"),
                         W2hi[:, ds(e, 1), :, :].rearrange("p a c d -> p (a c d)"))
            npass = dve.value_load(npass_i[:, 2:3], min_val=1, max_val=NPAD // WINDOW)
            with dve.If(npass > 1):
                with dve.Fori(1, npass) as w:
                    dve.wait_ge(s_zadd, w * ET + 2)
                    dve.tensor_scalar(iota_w[:], iota_w[:], float(WINDOW), None, ALU.add).then_inc(s_passb, 1)
                    dve.tensor_scalar(base_i[:], base_i[:], float(WINDOW), float(NPAD - WINDOW), ALU.add,
                                      ALU.min).then_inc(s_passb, 1)
                    dve.wait_ge(s_passb, w * 2)
                    dve.sem_inc(s_passgo, 1)
                    with dve.Fori(0, 2 * E) as b:
                        for r in range(2):
                            adds(w * ET + b * BODY, b * BODY, r)
            dve.wait_ge(s_zadd, npass * ET + 2)
            dve.sem_inc(s_gathered, 1)
            dve.tensor_copy(ident16, ident[:])

            for c in range(NCH):
                dve.wait_ge(s_dbc[c], 16)
                for m in range(KD):
                    z = AT[:, m, c * CH:(c + 1) * CH]
                    last = dve.tensor_tensor(z, z, R[:, c * CH:(c + 1) * CH], ALU.mult)
                last.then_inc(s_zs, 1)
            dve.sem_inc(s_dxg, 1)

            def mix(c, i):
                h = AT[:, :, ds(c * CH, CH)]
                dve.wait_ge(s_sig, c + 1)
                dve.wait_ge(s_dx, c + 1)
                dve.tensor_tensor(h, DX, PH[i][:].rearrange("p (m n) -> p m n", m=KD)[:, :, 0:CH],
                                  ALU.mult).then_inc(s_dxg, 1)
                dve.wait_ge(s_dxg, c + 2)
                dve.tensor_tensor(h, h, BT[:, :, ds(c * CH, CH)], ALU.add).then_inc(s_mix, 1)
                dve.wait_ge(s_mix, c + 1)
                dve.tensor_scalar(h, h, 0.0, None, ALU.max).then_inc(s_h, 1)
                dve.wait_ge(s_h, c + 1)

            def node_stats(c, n):
                for m in range(KD):
                    last = dve.bn_stats(bsv[:, m, ds(c, 1), :].rearrange("p a v -> p (a v)"), AT[:, m, ds(c * CH, n)])
                return last
            with dve.Fori(0, NCH // 2 - 1) as g:
                for i in range(2):
                    mix(g * 2 + i, i)
                    node_stats(g * 2 + i, CH)
            mix(NCH - 2, 0)
            node_stats(NCH - 2, CH)
            mix(NCH - 1, 1)
            link(node_stats(NCH - 1, N - (NCH - 1) * CH))
            for m in range(KD):
                last = dve.bn_aggr(bmv[:, m, :], bsv[:, m, :, :].rearrange("p c v -> p (c v)"))
            last.then_inc(s_bnsq, 1)
            dve.wait_ge(s_bnsq, 2)
            link(dve.reciprocal(brs, bsq))
            link(dve.tensor_tensor(bsc, brs, params[:, CV + 3 * KD:CV + 4 * KD], ALU.mult))
            link(dve.tensor_tensor(brs, bmv[:, :, 0:1].rearrange("p k a -> p (k a)"), bsc, ALU.mult))
            dve.tensor_tensor(bbi, params[:, CV + 4 * KD:CV + 5 * KD], brs, ALU.subtract).then_inc(s_bn, 1)

            def x2_tile(t, i):
                v = BR[:, ds(t, 1), :].rearrange("p a d -> p (a d)")
                dve.wait_ge(s_hT, t + 1)
                dve.tensor_tensor(v, v, PA[i][:, 0:D], ALU.add).then_inc(s_x2, 1)
                dve.wait_ge(s_x2, t + 1)
                return dve.bn_stats(svh[:, ds(t, 1), :].rearrange("p a v -> p (a v)"), v)
            for q in range(4):
                dve.wait_ge(s_xr[q], 16)
                with dve.Fori(q * XG // 2, (q + 1) * XG // 2) as g:
                    for i in range(2):
                        x2_tile(g * 2 + i, i)
            dve.wait_ge(s_xr[4], 16)
            link(x2_tile(NT - 1, 0))
            combine(svh).then_inc(s_var, 1)
            dve.wait_ge(s_sq1, 1)
            link(dve.reciprocal(nst[:, 6, :], nst[:, 3, :]))
            link(dve.tensor_tensor(nst[:, 1, :], nst[:, 6, :], nst[:, 6, :], ALU.mult))
            dve.tensor_tensor(nst[:, 4, :], nst[:, 2, :], nst[:, 1, :], ALU.mult).then_inc(s_v2, 1)
            dve.wait_ge(s_sq2, 1)
            link(dve.reciprocal(nst[:, 7, :], nst[:, 5, :]))
            link(dve.scalar_tensor_tensor(out=nst[:, 7, :], in0=nst[:, 7, :], scalar=XN_SCALE, in1=nst[:, 6, :],
                                          op0=ALU.mult, op1=ALU.mult))

            def token(t, i, first):
                if not first:
                    dve.wait_ge(s_vT, t - 1)
                    dve.wait_ge(s_xlo, t - 1)
                dve.tensor_scalar(V[i], BR[:, ds(t, 1), :].rearrange("p a d -> p (a d)"), nst[:, 0, ds(t, 1)],
                                  nst[:, 7, ds(t, 1)], ALU.subtract, ALU.mult).then_inc(s_v, 1)

            def token_low(t, i):
                dve.wait_ge(s_xhi, t + 1)
                dve.tensor_tensor(XH[i][:, D:2 * D], V[i], XH[i][:, 0:D], ALU.subtract).then_inc(s_xlo, 1)
            token(0, 0, True)
            token(1, 1, True)
            token_low(0, 0)
            with dve.Fori(1, NT // 2) as g:
                token(g * 2, 0, False)
                token_low(g * 2 - 1, 1)
                token(g * 2 + 1, 1, False)
                token_low(g * 2, 0)
            token(NT - 1, 0, False)
            token_low(NT - 2, 1)
            token_low(NT - 1, 0)

            def bc_e(v):
                return v.rearrange("p (t a) -> p t a", a=1).to_broadcast([P, NT, E])

            def bc_t(v, n=E):
                return v.rearrange("p (a e) -> p a e", a=1).to_broadcast([P, NT, n])
            m1, zs, p1, p2 = nst[:, 1, :], nst[:, 2, :], nst[:, 3, :], nst[:, 4, :]
            i1, i2, pos = nst[:, 6, :], nst[:, 7, :], nst[:, 0, :]
            L, EX, PR, EQ, O1, O2, MS = (rt(i) for i in range(7))
            TOT, INC, SL, TMP = rt(7), rt(8), rt(9), rt(10)
            dve.wait_ge(s_log, NT)
            dve.wait_ge(s_wr, 32)
            dve.wait_ge(s_tri, 3)
            link(dve.tensor_scalar(nst[:, 5, :], nst[:, 5, :], 1.0 / XN_SCALE, None, ALU.mult))
            link(dve.tensor_tensor(L, PB[:, 0:NE].rearrange("p (t e) -> p t e", e=E), bc_e(nst[:, 5, :]), ALU.mult))
            link(dve.tensor_tensor(L, L, bc_t(brS), ALU.add))
            link(dve.tensor_reduce(m1, L, AX, ALU.max))
            dve.tensor_tensor(EX, L, bc_e(m1), ALU.subtract).then_inc(s_sh, 1)
            dve.wait_ge(s_exp, 1)
            link(dve.tensor_reduce(zs, EX, AX, ALU.add))
            link(dve.reciprocal(zs, zs))
            link(dve.tensor_tensor(PR, EX, bc_e(zs), ALU.mult))

            def choose(one, best, index):
                link(dve.tensor_reduce(best, PR, AX, ALU.max))
                link(dve.tensor_tensor(EQ, PR, bc_e(best), ALU.is_equal))
                link(dve.scalar_tensor_tensor(out=EQ, in0=EQ, scalar=-float(E), in1=bc_t(iota[:, E:2 * E]),
                                              op0=ALU.mult, op1=ALU.add))
                link(dve.tensor_reduce(index, EQ, AX, ALU.min))
                link(dve.tensor_tensor(one, bc_t(iota[:, 0:E]), bc_e(index), ALU.is_equal))
            choose(O1, p1, i1)
            link(dve.scalar_tensor_tensor(out=PR, in0=O1, scalar=-2.0, in1=PR, op0=ALU.mult, op1=ALU.add))
            choose(O2, p2, i2)
            link(dve.tensor_tensor(zs, p1, p2, ALU.add))
            link(dve.reciprocal(zs, zs))
            dve.tensor_tensor(wts[:, 0, :], p1, zs, ALU.mult)
            dve.tensor_tensor(wts[:, 1, :], p2, zs, ALU.mult)
            link(dve.tensor_tensor(MS, O1, O2, ALU.add))
            dve.tensor_tensor(MS, MS, bc_e(valid), ALU.mult).then_inc(s_msum, 1)
            dve.wait_ge(s_cnt, 1)
            link(dve.tensor_copy(TOT.rearrange("p t e -> p (t e)").rearrange("p (e t) -> p e t", e=E),
                                 Q[1][:, 0:NE].rearrange("p (t e) -> p e t", e=E)))
            tot = TOT.rearrange("p t e -> p (t e)").rearrange("p (e t) -> p e t", e=E)
            inc = INC.rearrange("p t e -> p (t e)").rearrange("p (e t) -> p e t", e=E)
            for e in range(E):
                last = dve.tensor_tensor_scan(inc[:, e, :], ones[:, 0:NT], tot[:, e, :], 0.0, ALU.mult, ALU.add)
            link(last)
            ct, ci, ti, te, tend = (small[:, a:a + E] for a in (56, 4, 4, 56, 24))
            work = A[:, 23 * 256:23 * 256 + 8 * E]
            cf, ci, ti, te, tend, tst = (work[:, E * a:E * (a + 1)] for a in range(6))
            link(dve.tensor_scalar(cf, inc[:, :, NT - 1:NT].rearrange("p e a -> p (e a)"), float(P - 1), None, ALU.add))
            link(dve.tensor_copy(ci.bitcast(I32), cf))
            link(dve.tensor_scalar(ti.bitcast(I32), ci.bitcast(I32), P.bit_length() - 1, None, ALU.arith_shift_right))
            link(dve.tensor_copy(te, ti.bitcast(I32)))
            link(dve.tensor_tensor_scan(tend, ones[:, 0:E], te, 0.0, ALU.mult, ALU.add))
            link(dve.tensor_tensor(tst, tend, te, ALU.subtract))
            link(dve.tensor_scalar(tst, tst, float(P), None, ALU.mult))
            link(dve.tensor_tensor(SL, inc.rearrange("p e t -> p t e"), tot.rearrange("p e t -> p t e"), ALU.subtract))
            link(dve.tensor_tensor(SL, SL, Q[0][:, 0:NE].rearrange("p (t e) -> p t e", e=E), ALU.add))
            link(dve.tensor_tensor(SL, SL, bc_t(tst), ALU.add))
            link(dve.tensor_scalar(far, valid, -float(P * P * P), float(P * P * P), ALU.mult, ALU.add))
            lane = rt(11).rearrange("p t e -> p (t e)")[:, 0:2 * NT]
            tile_of = rt(12).rearrange("p t e -> p (t e)")[:, 0:2 * NT]
            posi = rt(13).rearrange("p t e -> p (t e)")[:, 0:2 * NT].bitcast(I32)
            pi2 = rt(14).rearrange("p t e -> p (t e)")[:, 0:2 * NT].bitcast(I32)
            for k, one in enumerate((O1, O2)):
                link(dve.tensor_tensor(TMP, SL, one, ALU.mult))
                link(dve.tensor_reduce(pos, TMP, AX, ALU.add))
                link(dve.tensor_tensor(pos, pos, far, ALU.add))
                link(dve.tensor_copy(posi.rearrange("p (t k) -> p t k", k=2)[:, :, k:k + 1],
                                     pos.rearrange("p (t a) -> p t a", a=1)))
            link(dve.tensor_scalar(pi2, posi, P - 1, None, ALU.bitwise_and))
            link(dve.tensor_copy(lane, pi2))
            link(dve.tensor_scalar(pi2, posi, P.bit_length() - 1, None, ALU.arith_shift_right))
            link(dve.tensor_copy(tile_of, pi2))

            def onehots(g, first):
                for i in range(2):
                    n = g * 2 + i
                    if not first:
                        dve.wait_ge(s_perm, n - 1)
                    dve.tensor_scalar(LO[i], iota[:], lane[:, ds(n, 1)], None, ALU.is_equal)
                    dve.tensor_scalar(V2[i][:, 0, :], iota[:, 0:ST], tile_of[:, ds(n, 1)], iota[:, ds(n + 1, 1)],
                                      ALU.is_equal, ALU.mult)
                    dve.tensor_scalar(V2[i][:, 1, :], iota[:, 0:ST], tile_of[:, ds(n, 1)], iota_p,
                                      ALU.is_equal, ALU.mult).then_inc(s_onehots, 1)
            onehots(0, True)
            with dve.Fori(1, NT) as g:
                onehots(g, False)
            ef = rt(15).rearrange("p t e -> p (t e)")[:, 0:ST]
            link(dve.tensor_scalar(ef, iota[:, 0:ST], tend[:, 0:1], None, ALU.is_ge))
            for e in range(1, E):
                link(dve.scalar_tensor_tensor(out=ef, in0=iota[:, 0:ST], scalar=tend[:, e:e + 1], in1=ef,
                                              op0=ALU.is_ge, op1=ALU.add))
            dve.tensor_scalar(exp_i, ef, float(E - 1), None, ALU.min)
            dve.wait_ge(s_perm, 2 * NT)
            v1, lane_s = Q[2][:, 0:ST], Q[2][:, ST:2 * ST]
            sf = [rt(16 + a).rearrange("p t e -> p (t e)")[:, 0:ST] for a in range(4)]
            slot_id = A[:, 21 * 256 + 64:21 * 256 + 64 + ST]
            filled, vi, vh, tok = sf
            link(dve.tensor_scalar(filled, v1, 0.0, None, ALU.is_gt))
            link(dve.tensor_scalar(vi.bitcast(I32), v1, -1.0, 0.0, ALU.add, ALU.max))
            link(dve.tensor_scalar(vh.bitcast(I32), vi.bitcast(I32), 1, None, ALU.arith_shift_right))
            link(dve.tensor_copy(tok, vh.bitcast(I32)))
            link(dve.scalar_tensor_tensor(out=tok, in0=tok, scalar=float(P), in1=lane_s, op0=ALU.mult, op1=ALU.add))
            dve.tensor_copy(gidx, tok)
            link(dve.tensor_scalar(vh.bitcast(I32), vi.bitcast(I32), 1, None, ALU.bitwise_and))
            link(dve.tensor_copy(vi, vh.bitcast(I32)))
            link(dve.scalar_tensor_tensor(out=vi, in0=tok, scalar=2.0, in1=vi, op0=ALU.mult, op1=ALU.add))
            link(dve.tensor_tensor(vi, vi, slot_id, ALU.subtract))
            link(dve.tensor_tensor(vi, vi, filled, ALU.mult))
            link(dve.tensor_tensor(vi, vi, slot_id, ALU.add))
            dve.tensor_copy(sidx, vi).then_inc(s_routed, 1)

            dve.wait_ge(s_b2, 16)
            dve.wait_ge(s_routed, 1)

            def result(n, b, j, first):
                i = j % 2
                e = dve.value_load(exp_i[0:1, ds(n, 1)], min_val=0, max_val=E - 1)
                dve.wait_ge(s_y, n + 1)
                if not first:
                    dve.wait_ge(s_sc[j], b * 16)
                dve.scalar_tensor_tensor(out=Y[j], in0=PA[i][:, 0:D], scalar=sc2[:, ds(e, 1)],
                                         in1=b2bc[:, ds(e, 1), :].rearrange("p a d -> p (a d)"),
                                         op0=ALU.mult, op1=ALU.add).then_inc(s_yr, 1)

            def split(n, j, first):
                i = j % 2
                e = dve.value_load(exp_i[0:1, ds(n, 1)], min_val=0, max_val=E - 1)
                for half in range(2):
                    c0, c1 = half * H // 2, (half + 1) * H // 2
                    dve.wait_ge(s_gelu, n * KH + (half + 1) * KH // 2)
                    if not first and half == 0:
                        dve.wait_ge(s_y, n - 1)
                    dve.tensor_scalar(HHI[i][:, c0:c1], HF[i][:, c0:c1], shs[:, ds(e, 1)], None,
                                      ALU.mult).then_inc(s_hs, 1)
                    dve.wait_ge(s_hs, n * 4 + (2 * half + 1))
                    dve.scalar_tensor_tensor(out=HLO[i][:, c0:c1], in0=HF[i][:, c0:c1], scalar=shs[:, ds(e, 1)],
                                             in1=HHI[i][:, c0:c1], op0=ALU.mult, op1=ALU.subtract).then_inc(s_hs, 1)

            def turn(b, first):
                for j in range(U):
                    n = b * U + j
                    split(n, j, first and j < 2)
                    if not (first and j == 0):
                        result(n - 1, b if j else b - 1, (j - 1) % U, first)
            turn(0, True)
            split(U, 0, False)
            result(U - 1, 0, U - 1, True)
            for j in range(1, U):
                split(U + j, j, False)
                result(U + j - 1, 1, j - 1, False)
            with dve.Fori(2, NB) as b:
                turn(b, False)
            result(ST - 1, NB - 1, U - 1, False)

            def final(t, g, i, rows):
                dve.wait_ge(s_yload[i], (g + 1) * 16)
                o = BR[0:rows, ds(t, 1), :].rearrange("p a d -> p (a d)")
                dve.scalar_tensor_tensor(out=o, in0=FIN[i][0:rows, 0, :], scalar=wts[0:rows, 0, ds(t, 1)], in1=o,
                                         op0=ALU.mult, op1=ALU.add).then_inc(s_fin0, 1)
                dve.wait_ge(s_fin0, t + 1)
                dve.scalar_tensor_tensor(out=o, in0=FIN[i][0:rows, 1, :], scalar=wts[0:rows, 1, ds(t, 1)], in1=o,
                                         op0=ALU.mult, op1=ALU.add).then_inc(s_fin, 1)
            with dve.Fori(0, (NT - 1) // 4) as g:
                for i in range(4):
                    final(g * 4 + i, g, i, P)
            final(NT - 1, (NT - 1) // 4, 0, LAST)


_INS = ['x', 'src', 'dst', 'L0_gnn_gcn_W', 'L0_gnn_gcn_b', 'L0_gnn_lin_W', 'L0_gnn_lin_b', 'L0_gnn_gate_W',
        'L0_gnn_gate_b', 'L0_gnn_bn_gamma', 'L0_gnn_bn_beta', 'L0_ffn_Wr', 'L0_ffn_br', 'L0_ffn_ln_g', 'L0_ffn_ln_b',
        'L0_ffn_W1', 'L0_ffn_b1', 'L0_ffn_W2', 'L0_ffn_b2']


def kernel(**inputs):
    import numpy as _np
    import concourse.bacc as _bacc
    from concourse import mybir as _mybir
    from concourse.bass_utils import run_bass_kernel_spmd as _run

    nc = _bacc.Bacc("TRN2", target_bir_lowering=False, num_devices=1)
    arrays, args = {}, []
    for name in _INS:
        a = _np.ascontiguousarray(inputs[name])
        arrays[f"in_{name}"] = a
        args.append(nc.dram_tensor(f"in_{name}", a.shape, _mybir.dt.from_np(a.dtype), kind="ExternalInput").ap())
    args.append(nc.dram_tensor("out_0", inputs["x"].shape, _mybir.dt.float32, kind="ExternalOutput").ap())
    build_gnn_moe(nc, *args)
    r = _run(nc, [arrays], core_ids=[0])
    return r.results[0]["out_0"]
```

```python
from contextlib import ExitStack

import concourse.bass as bass
from concourse import mybir

P = 128
F32, F16, I32 = mybir.dt.float32, mybir.dt.float16, mybir.dt.int32
ALU = mybir.AluOpType
ACT = mybir.ActivationFunctionType
AX = mybir.AxisListType.X

EPS = 1e-5
WINDOW = 64
SLOTS = 13
BASES = 8
PART = 10
OH = 6
SLOT_ROWS = 256
U = 2
LOW = 64
XN_SCALE = 1024.0
EXPONENT = 0x7F800000


def build_gnn_moe(nc, x, src, dst, gcn_W, gcn_b, lin_W, lin_b, gate_W, gate_b, bn_gamma, bn_beta,
                  Wr, br, ln_g, ln_b, W1, b1, W2, b2, out):
    N, D = x.shape
    E, _, H = W1.shape
    EDGES = src.shape[0]
    NT = -(-N // P)
    NPAD = NT * P
    KD, KH = D // P, H // P
    LAST = N - (NT - 1) * P
    BODY = 2 * SLOTS
    ET = BODY * 2 * E
    ROWS = ET // 4
    FULL = EDGES // (4 * P)
    TAIL = EDGES - FULL * 4 * P
    XG = (NT - 1) // 4
    CH = 400
    NCH = NPAD // CH
    ST = (2 * N + E * (SLOT_ROWS - 1)) // SLOT_ROWS
    SC = ST * SLOT_ROWS // P
    NB = ST // U
    HIGH = NPAD // LOW
    DUMP = 2 * NPAD
    EW = E * KD * H
    assert KD == 2 and ET * P >= EDGES and FULL == ROWS - 1 and 0 < TAIL <= 4 * P and ROWS <= P
    assert ST % U == 0 and NPAD % CH == 0 and (LOW + HIGH) * ET <= 4 * EW - 2 * KD * D and NPAD < 2 ** 15
    assert 2 * LOW == P and SLOT_ROWS == 2 * P
    CB1, CG = 0, E * KH
    CB = CG + E * KD
    CV = CB + E * KD
    PROWS = CV + 5 * KD

    t_dram = nc.dram_tensor("message_table", (NPAD, 2 * D), F16, kind="Internal").ap()
    xnT_dram = nc.dram_tensor("xnT_table", (P, KD, NPAD), F32, kind="Internal").ap()
    dinv_dram = nc.dram_tensor("dinv_row", (NT, P), F32, kind="Internal").ap()
    xn_dram = nc.dram_tensor("token_table", (NPAD, 2 * D), F16, kind="Internal").ap()
    y_dram = nc.dram_tensor("expert_rows", (DUMP + SC * P, D), F32, kind="Internal").ap()

    with ExitStack() as ctx:
        def sb(name, shape, dt):
            return ctx.enter_context(nc.sbuf_tensor(name, shape, dt))

        def sem(name):
            return ctx.enter_context(nc.semaphore(name))

        WALL = sb("WALL", [P, 4 * EW], F16)
        W1hi = WALL[:, 0:EW].rearrange("p (e k h) -> p e k h", e=E, k=KD)
        W1lo = WALL[:, EW:2 * EW].rearrange("p (e k h) -> p e k h", e=E, k=KD)
        W2hi = WALL[:, 2 * EW:3 * EW].rearrange("p (e c d) -> p e c d", e=E, c=KH)
        W2lo = WALL[:, 3 * EW:4 * EW].rearrange("p (e c d) -> p e c d", e=E, c=KH)
        mask_lo = WALL[:, 0:LOW * ET].rearrange("p (k t) -> p k t", t=ET)
        mask_hi = WALL[:, LOW * ET:(LOW + HIGH) * ET].rearrange("p (k t) -> p k t", t=ET)
        brow = WALL[0:1, 3 * EW:3 * EW + 2 * H].bitcast(F32)

        A = sb("A", [P, KD * NPAD], F32)
        B = sb("B", [P, KD * NPAD], F32)
        R = sb("R", [P, SLOTS * D], F32)
        S = sb("S", [P, KD * H], F32)

        AT = A[:].rearrange("p (k n) -> p k n", k=KD)
        BT = B[:].rearrange("p (k n) -> p k n", k=KD)
        BR = B[:].rearrange("p (t d) -> p t d", d=D)
        RS = R[:].rearrange("p (s d) -> p s d", d=D)

        edge_d = A[:, 0:4 * P].bitcast(I32)
        edge_s = A[:, 4 * P:8 * P].bitcast(I32)
        edge_df = A[:, 8 * P:12 * P]
        edge_sf = A[:, 12 * P:16 * P]
        tmin_w = A[:, 16 * P:20 * P]
        prow = A[:, 20 * P:21 * P]
        tmin = A[:, 21 * P:21 * P + 4]
        tmax = A[:, 21 * P + 4:21 * P + 8]
        tdif = A[:, 21 * P + 8:21 * P + 12]
        tspan = A[:, 21 * P + 12:21 * P + 13]
        dst_f = R[:, 0:ET]
        dst_i = R[:, ET:2 * ET].bitcast(I32)
        lohi_i = R[:, 2 * ET:3 * ET].bitcast(I32)
        lo16 = R[:, 3 * ET:3 * ET + ET // 2].bitcast(F16)
        hi16 = R[:, 3 * ET + ET // 2:4 * ET].bitcast(F16)
        XN = [RS[:, 7, :], RS[:, 8, :]]
        XS = [RS[:, 9, :], RS[:, 10, :]]
        TS = [RS[:, 11, :], RS[:, 12, :]]
        TH = [RS[:, 0, :].bitcast(F16), RS[:, 1, :].bitcast(F16)]
        gcnW = S[:, 0:KD * D].rearrange("p (k n) -> p k n", k=KD)
        linWv = WALL[:, 4 * EW - 2 * KD * D:4 * EW].bitcast(F32).rearrange("p (k n) -> p k n", k=KD)
        gateW = gcnW
        DX = S[:, KD * D:KD * D + KD * CH].rearrange("p (k n) -> p k n", k=KD)
        SW1 = S[:].rearrange("p (k h) -> p k h", k=KD)
        b2bc = S[:].rearrange("p (e d) -> p e d", e=E)

        ident = sb("ident", [P, P], F32)
        ones = sb("ones", [P, P], F32)
        iota = sb("iota", [P, P], F32)
        iota_w = sb("iota_w", [P, WINDOW], F32)
        src_i = sb("src_i", [P, ET], I32)
        dst_rel = sb("dst_rel", [P, ET], F32)
        route = sb("route", [P, 2 * E * (BODY + 2)], F32)
        base_i = route[0:1, :].bitcast(I32).rearrange("p (b k) -> p b k", b=2 * E)
        base_f = A[0:1, 4096:4096 + ET]
        params = sb("params", [P, PROWS], F32)
        ident16 = sb("ident16", [P, P], F16)
        idx_ring = sb("idx_ring", [P, BODY], I32)
        dinv = sb("dinv", [P, NT], F32)
        small = sb("small", [P, 64], F32)
        npass_f, npass_i = small[0:1, 0:1], small[0:1, 1:4].bitcast(I32)
        wam, wmax = small[:, 4:5], small[:, 5:6]
        wp2 = small[:, 6:7]
        wsc = small[:, 7:8]
        epst = small[:, 8:9]
        bmv = small[:, 12:16].rearrange("p (k v) -> p k v", k=KD)
        bsq, brs, bsc, bbi = small[:, 16:18], small[:, 18:20], small[:, 20:22], small[:, 22:24]
        iota_p = small[:, 24:25]
        zsc, zinv = small[:, 27:28], small[:, 28:29]
        lnb = small[:, 29:31]
        bnew = small[:, 56:56 + KH]
        wam2 = small[:, 25:26]
        wamr = small[:, 26:27]
        sc1, shs, sc2 = small[:, 32:32 + E], small[:, 40:40 + E], small[:, 48:48 + E]
        svx = A[:, 22 * P:22 * P + 6 * NT].rearrange("p (t v) -> p t v", v=6)
        bsv = R[:, NPAD:NPAD + KD * NCH * 6].rearrange("p (k c v) -> p k c v", k=KD, v=6)
        svh = RS[:, 10, 0:6 * NT].rearrange("p (t v) -> p t v", v=6)
        nst = sb("nst", [P, 8, NT], F32)
        oh = nst[:].rearrange("p a t -> p (a t)")[:, 0:OH * WINDOW // 2].bitcast(F16).rearrange("p (i w) -> p i w", i=OH)

        HN = [RS[:, 0, :], RS[:, 1, :]]
        V = [RS[:, 2, :], RS[:, 3, :]]
        VT = [RS[:, 4, :], RS[:, 5, :]]
        XH = [RS[:, 6, :].bitcast(F16), RS[:, 7, :].bitcast(F16)]
        WrS = RS[:, 8, 0:KD * E].rearrange("p (k e) -> p k e", k=KD)
        brS = RS[:, 8, 16:16 + E]
        NE = NT * E

        def rt(i):
            return A[:, i * 256:i * 256 + NE].rearrange("p (t e) -> p t e", e=E)
        tri = A[:, 20 * 256:20 * 256 + P]
        valid = A[:, 21 * 256:21 * 256 + NT]
        far = A[:, 21 * 256 + 32:21 * 256 + 32 + NT]
        iota16 = A[:, 22 * 256:22 * 256 + P // 2].bitcast(F16)
        LO = R[:, 0:NT * P].bitcast(F16).rearrange("p (t n) -> p t n", n=P)
        V2 = A[:, 0:2 * NT * SC].bitcast(F16).rearrange("p (v t n) -> p v t n", v=2, n=SC)
        lt16 = A[:, 22 * 256 + 64:22 * 256 + 64 + 2 * NT].bitcast(F16).rearrange("p (v t) -> p v t", v=2)
        wts = route[:, 0:2 * NT].rearrange("p (k t) -> p k t", k=2)
        gidx = route[:, 2 * NT:2 * NT + SC].bitcast(I32)
        sidx = route[:, 2 * NT + SC:2 * NT + 2 * SC].bitcast(I32)
        exp_i = route[:, 2 * NT + 2 * SC:2 * NT + 2 * SC + ST].bitcast(I32)
        g0 = 2 * NT + 2 * SC + ST
        gi = route[:, g0:g0 + 4].bitcast(I32)
        si = route[:, g0 + 4:g0 + 8].bitcast(I32)
        XT16 = [A[:, 512 * i:512 * (i + 1)].bitcast(F16).rearrange("p (v k t) -> p v k t", v=2, k=KD) for i in range(2)]
        HF = A[:, 1024:3072]
        HHI = A[:, 3072:4096].bitcast(F16)
        HLO = A[:, 4096:5120].bitcast(F16)
        XGr = [RS[:, i, :].bitcast(F16) for i in range(4)]
        Y = [RS[:, 4 + i, :] for i in range(4)]
        FIN = [A[:, 2048 * i:2048 * (i + 1)].rearrange("p (t k d) -> p t k d", t=4, k=2) for i in range(3)]

        def ps(name, shape, dt=F32):
            return ctx.enter_context(nc.psum_tensor(name, shape, dt))
        PH = ps("ph", [P, 2048])
        Q = [PH[:, 512 * i:512 * (i + 1)] for i in range(4)]
        G = [PH[:, 0:1024].rearrange("p (m n) -> p m n", m=KD), PH[:, 1024:2048].rearrange("p (m n) -> p m n", m=KD)]
        PA = [ps("pa0", [P, 512]), ps("pa1", [P, 512])]
        PB = ps("pb", [P, 512])
        P16 = ps("p16", [P, 1024], F16)
        MS = [PA[0], PA[1], Q[1], Q[2]]

        s_const0, s_const, s_pads = sem("const0"), sem("const"), sem("pads")
        s_edges, s_xlast, s_par, s_gcnw, s_linw = (sem(n) for n in ("edges", "xlast", "par", "gcnw", "linw"))
        s_x = [sem(f"xin{i}") for i in range(4)]
        s_edge_f, s_tmin, s_edge_T, s_tmin_bc, s_span_T = (
            sem(n) for n in ("edge_f", "tmin", "edge_T", "tmin_bc", "span_T"))
        s_dve = sem("dve_chain")
        s_edges_done, s_masks, s_hist, s_degsq, s_dinv = (
            sem(n) for n in ("edges_done", "masks", "hist", "degsq", "dinv"))
        s_par_T, s_params, s_mean, s_sq = (sem(n) for n in ("par_T", "params", "mean", "sq"))
        s_xn, s_xT, s_xTc, s_xw, s_ts, s_thi, s_tlo, s_tT, s_z0 = (
            sem(n) for n in ("xn", "xT", "xTc", "xw", "ts", "thi", "tlo", "tT", "z0"))
        s_hi_masks = sem("hi_masks")
        s_gmax, s_gmax_pe = sem("gmax"), sem("gmax_pe")
        s_t_st = [sem(f"t_st{i}") for i in range(2)]
        s_xs_st = [sem(f"xs_st{i}") for i in range(2)]
        s_dinv_T, s_dinv_Tc, s_dinv_st = (sem(n) for n in ("dinv_T", "dinv_Tc", "dinv_st"))
        s_slot = [sem(f"slot{i}") for i in range(SLOTS)]
        s_idx, s_hold, s_oh, s_msg, s_zadd, s_passb, s_passgo = (
            sem(n) for n in ("idx", "hold", "oh", "msg", "zadd", "passb", "passgo"))
        s_xnT_ld, s_xl, s_xlc = (sem(n) for n in ("xnT_ld", "xl", "xlc"))
        s_w_ld, s_w_bias, s_w_fold, s_w_am, s_w_amT, s_w_amr, s_w_bc, s_w_sc, s_w_hi, s_w_lo, s_w_sc0, s_w_am0, s_lnb, s_brow, s_browT = (
            sem(n) for n in ("w_ld", "w_bias", "w_fold", "w_am", "w_amT", "w_amr", "w_bc", "w_sc", "w_hi", "w_lo",
                             "w_sc0", "w_am0", "lnb", "brow", "browT"))
        s_gathered, s_gate_ld = sem("gathered"), sem("gate_ld")
        s_dbc = [sem(f"dbc{i}") for i in range(NCH // 2)]
        s_zs, s_tanh, s_gate, s_sig, s_dx, s_dxg, s_mix, s_h = (
            sem(n) for n in ("zs", "tanh", "gate", "sig", "dx", "dxg", "mix", "h"))
        s_bnsq, s_bn = sem("bnsq"), sem("bn")
        s_hn, s_hT, s_x2 = (sem(n) for n in ("hn", "hT", "x2"))
        s_xr = [sem(f"xr{i}") for i in range(5)]
        s_xpad2, s_wr = sem("xpad2"), sem("wr")
        s_var, s_sq1, s_v2, s_sq2 = (sem(n) for n in ("var", "sq1", "v2", "sq2"))
        s_v, s_vT, s_vTc, s_log, s_xhi, s_xlo = (sem(n) for n in ("v", "vT", "vTc", "log", "xhi", "xlo"))
        s_xh_st = [sem(f"xh_st{i}") for i in range(2)]
        s_tri, s_sh, s_exp, s_msum, s_cnt, s_onehots, s_perm, s_routed = (
            sem(n) for n in ("tri", "sh", "exp", "msum", "cnt", "onehots", "perm", "routed"))
        s_b2 = sem("b2")
        s_xg = [sem(f"xg{i}") for i in range(4)]
        s_sc = [sem(f"sc{i}") for i in range(4)]
        s_gcopy, s_xgT, s_xt, s_h1, s_gelu, s_hs, s_y, s_yr = (
            sem(n) for n in ("gcopy", "xgT", "xt", "h1", "gelu", "hs", "y", "yr"))
        s_yload = [sem(f"yload{i}") for i in range(3)]
        s_fin0, s_fin, s_out = sem("fin0"), sem("fin"), sem("out")

        block = ctx.enter_context(nc.Block())
        ds = bass.ds

        @block.sync
        def _(sp):
            sp.wait_ge(s_pads, 3)
            for rows, v in ((edge_d, dst), (edge_s, src)):
                sp.dma_start(rows[0:FULL, :], v[0:FULL * 4 * P].rearrange("(r c) -> r c", c=4 * P)).then_inc(s_edges, 16)
                sp.dma_start(rows[FULL:FULL + 1, 0:TAIL],
                             v[FULL * 4 * P:EDGES].rearrange("(r c) -> r c", r=1)).then_inc(s_edges, 16)
            for i in range(4):
                sp.dma_start(BR[:, i * XG:(i + 1) * XG, :],
                             x[i * XG * P:(i + 1) * XG * P, :].rearrange("(t p) d -> p t d", p=P)).then_inc(s_x[i], 16)
            sp.dma_start(BR[0:LAST, NT - 1, :], x[(NT - 1) * P:N, :]).then_inc(s_xlast, 16)
            sp.dma_start(gcnW, gcn_W.rearrange("(k p) n -> p k n", p=P)).then_inc(s_gcnw, 16)
            sp.dma_start(linWv, lin_W.rearrange("(k p) n -> p k n", p=P)).then_inc(s_linw, 16)

            def store_tile(t, i):
                sp.wait_ge(s_xTc, t + 1)
                sp.dma_start(xnT_dram[:, :, ds(t * P, P)], XS[i].rearrange("p (k n) -> p k n", k=KD)).then_inc(s_xs_st[i], 16)
                sp.wait_ge(s_tlo, t + 1)
                sp.dma_start(t_dram[ds(t * P, P), :], TH[i]).then_inc(s_t_st[i], 16)
            with sp.Fori(0, NT // 2) as g:
                for i in range(2):
                    store_tile(g * 2 + i, i)
            store_tile(NT - 1, 0)
            sp.wait_ge(s_dinv_Tc, 1)
            sp.dma_start(dinv_dram[:, :], XN[1][0:NT, 0:P]).then_inc(s_dinv_st, 16)
            sp.wait_ge(s_xs_st[0], 16 * (NT - NT // 2))
            sp.wait_ge(s_xs_st[1], 16 * (NT // 2))
            sp.wait_ge(s_xn, NT)
            sp.dma_start(BT, xnT_dram[:, :, :]).then_inc(s_xnT_ld, 16)

            sp.wait_ge(s_xw, NT)
            with sp.Fori(0, E) as e:
                sp.wait_ge(s_w_lo, e + 1)
                sp.dma_start(SW1, W1[ds(e, 1), :, :].rearrange("a (k p) h -> p (a k) h", p=P)).then_inc(s_w_ld, 16)
            with sp.Fori(0, E) as e:
                sp.wait_ge(s_w_lo, e + (E + 1))
                sp.dma_start(S[:].rearrange("p (c d) -> p c d", c=KH),
                             W2[ds(e, 1), :, :].rearrange("a (c p) d -> p (a c) d", p=P)).then_inc(s_w_ld, 16)
            sp.wait_ge(s_w_lo, 2 * E + 1)
            sp.dma_start(gateW, gate_W.rearrange("(k p) n -> p k n", p=P)).then_inc(s_gate_ld, 16)
            sp.wait_ge(s_gathered, 1)
            sp.wait_ge(s_dinv_st, 16)
            for c in range(NCH // 2):
                sp.dma_start(R[:, 2 * c * CH:2 * (c + 1) * CH],
                             dinv_dram.rearrange("t p -> (t p)")[2 * c * CH:2 * (c + 1) * CH].rearrange("(a n) -> a n", a=1)
                             .to_broadcast([P, 2 * CH])).then_inc(s_dbc[c], 16)
            sp.wait_ge(s_h, NCH)
            sp.wait_ge(s_xpad2, 1)
            for i in range(4):
                sp.dma_start(BR[:, i * XG:(i + 1) * XG, :],
                             x[i * XG * P:(i + 1) * XG * P, :].rearrange("(t p) d -> p t d", p=P)).then_inc(s_xr[i], 16)
            sp.dma_start(BR[0:LAST, NT - 1, :], x[(NT - 1) * P:N, :]).then_inc(s_xr[4], 16)
            sp.dma_start(WrS, Wr.rearrange("(k p) e -> p k e", p=P)).then_inc(s_wr, 16)
            sp.dma_start(brS, br.rearrange("(a e) -> a e", a=1).to_broadcast([P, E])).then_inc(s_wr, 16)
            sp.dma_start(S[:], b2.rearrange("(a e) d -> a (e d)", a=1).to_broadcast([P, E * D])).then_inc(s_b2, 16)

            def store_token(t, i):
                sp.wait_ge(s_xlo, t + 1)
                sp.dma_start(xn_dram[ds(t * P, P), :], XH[i]).then_inc(s_xh_st[i], 16)
            with sp.Fori(0, NT // 2) as g:
                for i in range(2):
                    store_token(g * 2 + i, i)
            store_token(NT - 1, 0)

            for i in range(4):
                sp.wait_ge(s_sc[i], 16 * NB)

            def load_y(g, i):
                sp.dma_start(FIN[i], y_dram[ds(g * 8 * P, 8 * P), :].rearrange("(t p k) d -> p t k d", p=P, k=2)
                             ).then_inc(s_yload[i], 16)

            def store_out(g):
                sp.wait_ge(s_fin, g * 4 + 4)
                sp.dma_start(out[ds(g * 4 * P, 4 * P), :].rearrange("(t p) d -> p t d", p=P),
                             BR[:, ds(g * 4, 4), :]).then_inc(s_out, 16)
            for g in range(3):
                load_y(g, g)
            for g in range(NT // 4):
                store_out(g)
                if g + 3 < NT // 4:
                    load_y(g + 3, g % 3)
                elif g + 3 == NT // 4:
                    sp.dma_start(FIN[g % 3][0:LAST, 0, :, :], y_dram[(NT - 1) * 2 * P:(NT - 1) * 2 * P + 2 * LAST, :]
                                 .rearrange("(p k) d -> p k d", k=2)).then_inc(s_yload[g % 3], 16)
            sp.wait_ge(s_fin, NT)
            sp.dma_start(out[(NT - 1) * P:N, :], BR[0:LAST, NT - 1, :]).then_inc(s_out, 16)
            sp.wait_ge(s_out, 16 * (NT // 4 + 1))
            for i in range(2):
                sp.wait_ge(s_t_st[i], 16)

        @block.gpsimd
        def _(pool):
            pool.memset(edge_d, N).then_inc(s_pads, 1)
            pool.memset(edge_s, N).then_inc(s_pads, 1)
            pool.memset(BR[:, NT - 1, :], 0.0).then_inc(s_pads, 1)
            pool.memset(ident[:], 0.0).then_inc(s_const0, 1)
            pool.memset(ones[:], 1.0).then_inc(s_const, 1)
            pool.memset(epst, EPS).then_inc(s_const, 1)
            pool.iota(iota[:], pattern=[[1, P]], base=0, channel_multiplier=0,
                      allow_small_or_imprecise_dtypes=True).then_inc(s_const, 1)
            pool.iota(iota_w[:], pattern=[[1, WINDOW]], base=0, channel_multiplier=0,
                      allow_small_or_imprecise_dtypes=True).then_inc(s_const, 1)
            pool.iota(iota_p, pattern=[[1, 1]], base=0, channel_multiplier=1,
                      allow_small_or_imprecise_dtypes=True).then_inc(s_const, 1)
            pool.wait_ge(s_const0, 1)
            pool.affine_select(out=ident[:], in_=ident[:], compare_op=ALU.not_equal, fill=1.0, base=0,
                               pattern=[[-1, P]], channel_multiplier=1).then_inc(s_const, 1)

            pool.wait_ge(s_edges_done, 1)
            for half in range(2):
                a, b = half * ET // 2, (half + 1) * ET // 2
                for j in range(HIGH // 2):
                    last = pool.tensor_scalar(mask_hi[:, j, a:b], hi16[:, a:b], float(j), None, ALU.is_equal)
                last.then_inc(s_hi_masks, 1)

            pool.wait_ge(s_t_st[0], 16 * (NT - NT // 2))
            pool.wait_ge(s_t_st[1], 16 * (NT // 2))
            pool.wait_ge(s_edges_done, 1)
            pool.wait_ge(s_tT, NT)
            pool.wait_ge(s_dinv_st, 16)
            pool.wait_ge(s_xs_st[0], 16 * (NT - NT // 2))
            pool.wait_ge(s_xs_st[1], 16 * (NT // 2))

            def gather_body(n0, c0, round0):
                for r in range(2):
                    pool.tensor_copy(idx_ring[:, r * SLOTS:(r + 1) * SLOTS],
                                     src_i[:, ds(c0 + r * SLOTS, SLOTS)]).then_inc(s_idx, 1)
                    pool.wait_ge(s_idx, round0 + (r + 1))
                    for j in range(SLOTS):
                        pool.wait_ge(s_msg, n0 + (r * SLOTS + j + 1))
                        pool.sem_inc(s_hold, 1)
                        pool.indirect_dma_start(
                            out=RS[:, j, :].bitcast(F16), out_offset=None, in_=t_dram[:, :],
                            in_offset=bass.IndirectOffsetOnAxis(ap=idx_ring[:, r * SLOTS + j:r * SLOTS + j + 1], axis=0),
                        ).then_inc(s_slot[j], 16)

            with pool.Fori(0, 2 * E) as b:
                gather_body(b * BODY, b * BODY, b * 2)
            pool.wait_ge(s_edges_done, 1)
            npass = pool.value_load(npass_i[:, 2:3], min_val=1, max_val=NPAD // WINDOW)
            with pool.If(npass > 1):
                with pool.Fori(1, npass) as w:
                    with pool.Fori(0, 2 * E) as b:
                        gather_body(w * ET + b * BODY, b * BODY, w * (4 * E) + b * 2)

            def dx(c):
                pool.wait_ge(s_tanh, c + 1)
                pool.wait_ge(s_dxg, c + 1)
                pool.tensor_tensor(DX, AT[:, :, ds(c * CH, CH)], BT[:, :, ds(c * CH, CH)], ALU.subtract).then_inc(s_dx, 1)
            pool.wait_ge(s_xlc, KD * NCH)
            with pool.Fori(0, NCH) as c:
                dx(c)
            pool.wait_ge(s_h, NCH)
            pool.memset(BR[:, NT - 1, :], 0.0).then_inc(s_xpad2, 1)
            pool.wait_ge(s_hn, NT)
            pool.affine_select(out=tri, in_=ones[:], compare_op=ALU.is_gt, fill=0.0, base=0,
                               pattern=[[1, P]], channel_multiplier=-1).then_inc(s_tri, 1)
            pool.affine_select(out=valid, in_=ones[:, 0:NT], compare_op=ALU.is_ge, fill=0.0, base=N - 1,
                               pattern=[[-P, NT]], channel_multiplier=-1).then_inc(s_tri, 1)
            slot_id = A[:, 21 * 256 + 64:21 * 256 + 64 + SC]
            pool.iota(slot_id, pattern=[[P, SC]], base=DUMP, channel_multiplier=1,
                      allow_small_or_imprecise_dtypes=True).then_inc(s_tri, 1)

            pool.iota(iota16, pattern=[[1, P]], base=0, channel_multiplier=0,
                      allow_small_or_imprecise_dtypes=True).then_inc(s_tri, 1)

            pool.wait_ge(s_routed, 1)
            pool.wait_ge(s_xh_st[0], 16 * (NT - NT // 2))
            pool.wait_ge(s_xh_st[1], 16 * (NT // 2))

            def gather_x(n, i, count, first):
                if not first:
                    pool.wait_ge(s_xgT, n - 1)
                pool.tensor_copy(gi[:, 2 * i:2 * i + 2], gidx[:, ds(n * 2, 2)]).then_inc(s_gcopy, 1)
                pool.wait_ge(s_gcopy, count)
                pool.sem_inc(s_hold, 1)
                for h in range(2):
                    j = 2 * i + h
                    pool.indirect_dma_start(out=XGr[j], out_offset=None, in_=xn_dram[:, :],
                                            in_offset=bass.IndirectOffsetOnAxis(ap=gi[:, j:j + 1], axis=0)
                                            ).then_inc(s_xg[j], 16)

            def scatter_y(n, b, i, count, first):
                if not first:
                    for h in range(2):
                        pool.wait_ge(s_sc[2 * i + h], b * 16)
                pool.tensor_copy(si[:, 2 * i:2 * i + 2], sidx[:, ds(n * 2, 2)]).then_inc(s_gcopy, 1)
                pool.wait_ge(s_gcopy, count)
                for h in range(2):
                    j = 2 * i + h
                    pool.wait_ge(s_yr, n * 2 + h + 1)
                    pool.sem_inc(s_hold, 1)
                    pool.indirect_dma_start(out=y_dram[:, :],
                                            out_offset=bass.IndirectOffsetOnAxis(ap=si[:, j:j + 1], axis=0),
                                            in_=Y[j], in_offset=None).then_inc(s_sc[j], 16)

            def turn(b, first, gathers):
                for i in range(U):
                    n = b * U + i
                    if i < gathers:
                        gather_x(n + 3, 1 - i, n * 2 + 4, False)
                        scatter_y(n, b, i, n * 2 + 5, first)
                    else:
                        scatter_y(n, b, i, n + ST + 1, first)
            for n in range(3):
                gather_x(n, n % 2, n + 1, n < 2)
            turn(0, True, U)
            with pool.Fori(1, NB - 2) as b:
                turn(b, False, U)
            turn(NB - 2, False, U - 1)
            turn(NB - 1, False, 0)

        @block.scalar
        def _(act):
            rows = [(b1.rearrange("e (c p) -> (e c) p", p=P), E * KH), (ln_g.rearrange("e (k p) -> (e k) p", p=P), E * KD),
                    (ln_b.rearrange("e (k p) -> (e k) p", p=P), E * KD)]
            rows += [(v.rearrange("(k p) -> k p", p=P), KD) for v in (gcn_b, lin_b, gate_b, bn_gamma, bn_beta)]
            r0 = 0
            for v, n in rows:
                act.dma_start(prow[r0:r0 + n, :], v).then_inc(s_par, 16)
                r0 += n
            act.wait_ge(s_mean, 1)
            act.activation(nst[:, 3, :], nst[:, 2, :], ACT.Sqrt, bias=epst, scale=1.0 / D).then_inc(s_sq, 1)
            act.wait_ge(s_hist, 1)
            for h in range(2):
                last = act.activation(nst[h * LOW:(h + 1) * LOW, 4, :],
                                      Q[0][0:LOW, 0:HIGH].rearrange("p (t h) -> p h t", h=2)[:, h, :], ACT.Sqrt,
                                      bias=ones[0:LOW, 0:1])
            last.then_inc(s_degsq, 1)
            act.wait_ge(s_edges_done, 1)
            act.wait_ge(s_span_T, 1)

            def copy_xT(t, i, first):
                act.wait_ge(s_xT, t + 1)
                if not first:
                    act.wait_ge(s_xs_st[i], (t - i) * 8)
                    act.wait_ge(s_xw, t - 1)
                act.activation(XS[i], Q[i][:, 0:D], ACT.Copy).then_inc(s_xTc, 1)

            def messages(t, i, first):
                act.wait_ge(s_xw, t + 1)
                if not first:
                    act.wait_ge(s_tT, t - 1)
                    act.wait_ge(s_tlo, t - 1)
                act.activation(TS[i], PA[i][:, 0:D], ACT.Copy, scale=nst[:, 5, ds(t, 1)]).then_inc(s_ts, 1)
                if not first:
                    act.wait_ge(s_t_st[i], (t - i) * 8)
                act.wait_ge(s_ts, t + 1)
                act.activation(TH[i][:, 0:D], TS[i], ACT.Copy).then_inc(s_thi, 1)
            act.wait_ge(s_dinv, 1)
            copy_xT(0, 0, True)
            copy_xT(1, 1, True)
            messages(0, 0, True)
            copy_xT(2, 0, False)
            messages(1, 1, True)
            with act.Fori(1, NT // 2) as g:
                for i in range(2):
                    copy_xT(g * 2 + i + 1, 1 - i, False)
                    messages(g * 2 + i, i, False)
            messages(NT - 1, 0, False)

            act.wait_ge(s_params, 1)
            with act.Fori(0, E) as e:
                act.wait_ge(s_xl, e * 2 + 2)
                for m in range(KD):
                    act.activation(BT[:, m, ds(e * CH, CH)], Q[3 - 3 * m][:, 0:CH], ACT.Identity,
                                   bias=params[:, CV + KD + m:CV + KD + m + 1]).then_inc(s_xlc, 1)
                for h in range(2):
                    act.wait_ge(s_w_bias, e * 2 + h + 1)
                    act.activation(brow[:, h * 512:(h + 1) * 512], Q[3 - 3 * h][0:1, :], ACT.Copy).then_inc(s_brow, 1)
                for kk in range(KD):
                    act.activation(SW1[:, kk, :], SW1[:, kk, :], ACT.Copy,
                                   scale=params[:, ds(e * KD + (CG + kk), 1)]).then_inc(s_w_fold, 1)
                act.wait_ge(s_w_sc, e + 1)
                act.activation(W1hi[:, ds(e, 1), :, :].rearrange("p a k h -> p (a k h)"), S[:], ACT.Copy,
                               scale=wsc).then_inc(s_w_hi, 1)
            with act.Fori(0, E) as e:
                act.wait_ge(s_w_sc, e + (E + 1))
                act.activation(W2hi[:, ds(e, 1), :, :].rearrange("p a c d -> p (a c d)"), S[:], ACT.Copy,
                               scale=wsc).then_inc(s_w_hi, 1)

            def tanh(c):
                act.wait_ge(s_zs, c + 1)
                for m in range(KD):
                    last = act.activation(AT[:, m, ds(c * CH, CH)], AT[:, m, ds(c * CH, CH)], ACT.Tanh,
                                          bias=params[:, CV + m:CV + m + 1], scale=zinv)
                last.then_inc(s_tanh, 1)
            with act.Fori(0, NCH) as c:
                tanh(c)
            with act.Fori(0, NCH // 2) as g:
                for i in range(2):
                    act.wait_ge(s_gate, g * 2 + i + 1)
                    for m in range(KD):
                        last = act.activation(G[i][:, m, 0:CH], G[i][:, m, 0:CH], ACT.Sigmoid,
                                              bias=params[:, CV + 2 * KD + m:CV + 2 * KD + m + 1])
                    last.then_inc(s_sig, 1)
            act.wait_ge(s_bnsq, 1)
            act.activation(bsq, bmv[:, :, 1:2].rearrange("p k a -> p (k a)"), ACT.Sqrt, bias=epst).then_inc(s_bnsq, 1)
            act.wait_ge(s_bn, 1)

            def norm_tile(t, i, first):
                if not first:
                    act.wait_ge(s_hT, t - 1)
                for m in range(KD):
                    last = act.activation(HN[i][:, m * P:(m + 1) * P], AT[:, m, ds(t * P, P)], ACT.Identity,
                                          bias=bbi[:, m:m + 1], scale=bsc[:, m:m + 1])
                last.then_inc(s_hn, 1)
            for i in range(2):
                norm_tile(i, i, True)
            with act.Fori(1, NT // 2) as g:
                for i in range(2):
                    norm_tile(g * 2 + i, i, False)
            norm_tile(NT - 1, 0, False)
            act.wait_ge(s_var, 1)
            act.activation(nst[:, 3, :], nst[:, 2, :], ACT.Sqrt, bias=epst, scale=1.0 / D).then_inc(s_sq1, 1)
            act.wait_ge(s_v2, 1)
            act.activation(nst[:, 5, :], nst[:, 4, :], ACT.Sqrt, bias=epst, scale=1.0 / D).then_inc(s_sq2, 1)

            def token(t, i, first):
                act.wait_ge(s_vT, t + 1)
                if not first:
                    act.wait_ge(s_log, t - 1)
                act.activation(VT[i], PA[i][:, 0:D], ACT.Copy).then_inc(s_vTc, 1)
                if not first:
                    act.wait_ge(s_xh_st[i], (t - i) * 8)
                act.activation(XH[i][:, 0:D], V[i], ACT.Copy).then_inc(s_xhi, 1)
            for i in range(2):
                token(i, i, True)
            with act.Fori(1, NT // 2) as g:
                for i in range(2):
                    token(g * 2 + i, i, False)
            token(NT - 1, 0, False)
            act.wait_ge(s_sh, 1)
            act.activation(rt(1), rt(1), ACT.Exp).then_inc(s_exp, 1)

            act.wait_ge(s_routed, 1)

            def turn(b, first):
                for i in range(U):
                    n = b * U + i
                    e = act.value_load(exp_i[0:1, ds(n, 1)], min_val=0, max_val=E - 1)
                    act.wait_ge(s_xgT, n + 1)
                    if not first:
                        act.wait_ge(s_h1, (n - 1) * 4)
                    act.activation(XT16[i].rearrange("p v k t -> p (v k t)"), P16[:], ACT.Copy).then_inc(s_xt, 1)
                    for c in range(KH):
                        if c % 2 == 0:
                            act.wait_ge(s_h1, n * 4 + (c // 2 + 1))
                        if c % 4 == 0 and not (first and i == 0):
                            act.wait_ge(s_hs, n * 4 + (c // 2 - 2))
                        act.activation(HF[:, c * SLOT_ROWS:(c + 1) * SLOT_ROWS], PH[:, c * SLOT_ROWS:(c + 1) * SLOT_ROWS],
                                       ACT.Gelu, bias=params[:, ds(e * KH + c, 1)],
                                       scale=sc1[:, ds(e, 1)]).then_inc(s_gelu, 1)
            turn(0, True)
            with act.Fori(1, NB) as b:
                turn(b, False)

        @block.tensor
        def _(pe):
            pe.wait_ge(s_const, 6)
            pe.wait_ge(s_edge_f, 2)
            for k, rows in enumerate((edge_df, edge_sf)):
                for c in range(4):
                    last = pe.transpose(Q[k][:, c * ROWS:(c + 1) * ROWS], rows[0:ROWS, c * P:(c + 1) * P],
                                        ident[0:ROWS, 0:ROWS])
                last.then_inc(s_edge_T, 1)
            pe.wait_ge(s_tmin, 5)
            for c in range(4):
                last = pe.matmul(Q[2][:, c * ROWS:(c + 1) * ROWS], tmin_w[0:ROWS, c * P:(c + 1) * P],
                                 ident[0:ROWS, 0:ROWS], start=True, stop=True)
            last.then_inc(s_tmin_bc, 1)
            pe.transpose(Q[3][0:1, 0:ROWS], tspan[0:ROWS, :], ident[0:ROWS, 0:ROWS]).then_inc(s_span_T, 1)
            pe.wait_ge(s_par, 16 * 8)
            pe.transpose(PB[:, 0:PROWS], prow[0:PROWS, :], ident[0:PROWS, 0:PROWS]).then_inc(s_par_T, 1)

            pe.wait_ge(s_gmax, 1)
            pe.transpose(PA[0][0:1, 0:P], wam, ident[:]).then_inc(s_gmax_pe, 1)
            pe.wait_ge(s_gmax, 2)
            pe.matmul(PA[1][:, 0:1], ones[0:1, :], wamr[0:1, :], start=True, stop=True).then_inc(s_gmax_pe, 1)

            for half in range(2):
                pe.wait_ge(s_masks, half + 1)
                pe.wait_ge(s_hi_masks, half + 1)
                if half == 0:
                    pe.wait_ge(s_edges_done, 1)
                for t in range(half * ET // 2, (half + 1) * ET // 2):
                    mm = pe.matmul(Q[0][0:LOW, 0:HIGH], mask_lo[:, :, t], mask_hi[:, :, t],
                                   start=(t == 0), stop=(t == ET - 1))
            mm.then_inc(s_hist, 1)

            pe.wait_ge(s_gcnw, 16)

            def x_T(t, i, first):
                pe.wait_ge(s_xn, t + 1)
                if not first:
                    pe.wait_ge(s_xTc, t - 1)
                for k in range(KD):
                    last = pe.transpose(Q[i][:, k * P:(k + 1) * P], XN[i][:, k * P:(k + 1) * P], ident[:])
                last.then_inc(s_xT, 1)

            def times_gcn(t, i, first):
                pe.wait_ge(s_xTc, t + 1)
                if not first:
                    pe.wait_ge(s_ts, t - 1)
                for k in range(KD):
                    last = pe.matmul(PA[i][:, 0:D], XS[i][:, k * P:(k + 1) * P], gcnW[:, k, :],
                                     start=(k == 0), stop=(k == KD - 1))
                last.then_inc(s_xw, 1)

            def t_T(t, i, first):
                pe.wait_ge(s_ts, t + 1)
                if not first:
                    pe.wait_ge(s_z0, t - 1)
                for k in range(KD):
                    last = pe.transpose(Q[2 + i][:, k * P:(k + 1) * P], TS[i][:, k * P:(k + 1) * P], ident[:])
                last.then_inc(s_tT, 1)
            pe.wait_ge(s_degsq, 1)
            x_T(0, 0, True)
            x_T(1, 1, True)
            times_gcn(0, 0, True)
            x_T(2, 0, False)
            times_gcn(1, 1, True)
            t_T(0, 0, True)
            x_T(3, 1, False)
            times_gcn(2, 0, False)
            t_T(1, 1, True)
            with pe.Fori(1, NT // 2 - 1) as g:
                for i in range(2):
                    x_T(g * 2 + i + 2, i, False)
                    times_gcn(g * 2 + i + 1, 1 - i, False)
                    t_T(g * 2 + i, i, False)
            x_T(NT - 1, 0, False)
            times_gcn(NT - 2, 1, False)
            t_T(NT - 3, 0, False)
            times_gcn(NT - 1, 0, False)
            t_T(NT - 2, 1, False)
            t_T(NT - 1, 0, False)
            pe.transpose(PB[0:NT, 128:256], dinv[:], ident[:]).then_inc(s_dinv_T, 1)
            pe.wait_ge(s_z0, NT)

            def sums(n0, round0, step=None):
                for k in range(BODY):
                    if step:
                        step(k)
                    r, j = divmod(k, SLOTS)
                    pe.wait_ge(s_slot[j], (round0 + r + 1) * 16)
                    pe.wait_ge(s_oh, n0 + (k + 1))
                    pe.wait_ge(s_zadd, n0 + (k + (3 if k < BODY % 4 else 1)))
                    for m in range(KD):
                        for v in range(2):
                            last = pe.matmul(MS[k % 4][:, m * WINDOW:(m + 1) * WINDOW],
                                             RS[:, j, :].bitcast(F16)[:, v * D + m * P:v * D + (m + 1) * P],
                                             oh[:, k % OH, :], start=(v == 0), stop=(v == 1))
                    last.then_inc(s_msg, 1)

            pe.sem_inc(s_msg, SLOTS)
            pe.wait_ge(s_linw, 16)
            pe.wait_ge(s_xnT_ld, 16)
            pe.wait_ge(s_params, 1)

            def top(u):
                pe.wait_ge(s_w_am, u + 1)
                pe.transpose(PB[0:1, 128:256], wam, ident[:]).then_inc(s_w_amT, 1)

            def spread(u):
                pe.wait_ge(s_w_amr, u + 1)
                pe.matmul(PB[:, 256:257], ones[0:1, :], wamr[0:1, :], start=True, stop=True).then_inc(s_w_bc, 1)
            with pe.Fori(0, E) as e:
                def step(k):
                    if k in (2, 4):
                        m = k // 4
                        for kk in range(KD):
                            last = pe.matmul(Q[3 - 3 * m][:, 0:CH], linWv[:, kk, m * P:(m + 1) * P],
                                             BT[:, kk, ds(e * CH, CH)], start=(kk == 0), stop=(kk == KD - 1))
                        last.then_inc(s_xl, 1)
                    if k in (7, 9):
                        h = k // 9
                        if not h:
                            pe.wait_ge(s_w_ld, (e + 1) * 16)
                            pe.wait_ge(s_lnb, e + 1)
                        pe.wait_ge(s_xlc, e * 2 + h + 1)
                        for kk in range(KD):
                            last = pe.matmul(Q[3 - 3 * h][0:1, :], lnb[:, kk:kk + 1],
                                             SW1[:, kk, h * 512:(h + 1) * 512], start=(kk == 0), stop=(kk == KD - 1))
                        last.then_inc(s_w_bias, 1)
                    if k == 12:
                        pe.wait_ge(s_brow, e * 2 + 2)
                        for c in range(KH):
                            last = pe.matmul(PB[:, c:c + 1], brow[:, c * P:(c + 1) * P], ones[0:1, 0:1],
                                             start=True, stop=True)
                        last.then_inc(s_browT, 1)
                    if k == 17:
                        top(e)
                    if k == 20:
                        spread(e)
                sums(e * BODY, e * 2, step)
            with pe.Fori(0, E) as e:
                def step(k):
                    if k == 9:
                        top(e + E)
                    if k == 12:
                        spread(e + E)
                sums(e * BODY + E * BODY, e * 2 + 2 * E, step)
            npass = pe.value_load(npass_i[:, 2:3], min_val=1, max_val=NPAD // WINDOW)
            with pe.If(npass > 1):
                with pe.Fori(1, npass) as w:
                    with pe.Fori(0, 2 * E) as b:
                        sums(w * ET + b * BODY, w * (4 * E) + b * 2)

            pe.wait_ge(s_gate_ld, 16)

            def gate(c, i, first):
                pe.wait_ge(s_tanh, c + 1)
                if not first:
                    pe.wait_ge(s_dxg, c)
                for m in range(KD):
                    for k in range(KD):
                        last = pe.matmul(G[i][:, m, 0:CH], gateW[:, k, m * P:(m + 1) * P],
                                         AT[:, k, ds(c * CH, CH)], start=(k == 0), stop=(k == KD - 1))
                last.then_inc(s_gate, 1)
            for i in range(2):
                gate(i, i, True)
            with pe.Fori(1, NCH // 2) as g:
                for i in range(2):
                    gate(g * 2 + i, i, False)

            def rows_of(t, i, first):
                pe.wait_ge(s_hn, t + 1)
                if not first:
                    pe.wait_ge(s_x2, t - 1)
                for k in range(KD):
                    last = pe.transpose(PA[i][:, k * P:(k + 1) * P], HN[i][:, k * P:(k + 1) * P], ident[:])
                last.then_inc(s_hT, 1)
            for i in range(2):
                rows_of(i, i, True)
            with pe.Fori(1, NT // 2) as g:
                for i in range(2):
                    rows_of(g * 2 + i, i, False)
            rows_of(NT - 1, 0, False)

            pe.wait_ge(s_wr, 32)

            def v_T(t, i, first):
                pe.wait_ge(s_v, t + 1)
                if not first:
                    pe.wait_ge(s_vTc, t - 1)
                for k in range(KD):
                    last = pe.transpose(PA[i][:, k * P:(k + 1) * P], V[i][:, k * P:(k + 1) * P], ident[:])
                last.then_inc(s_vT, 1)

            def router(t, i):
                pe.wait_ge(s_vTc, t + 1)
                for k in range(KD):
                    last = pe.matmul(PB[:, ds(t * E, E)], VT[i][:, k * P:(k + 1) * P], WrS[:, k, :],
                                     start=(k == 0), stop=(k == KD - 1))
                last.then_inc(s_log, 1)
            pe.wait_ge(s_x2, NT)
            v_T(0, 0, True)
            v_T(1, 1, True)
            router(0, 0)
            with pe.Fori(1, NT // 2) as g:
                v_T(g * 2, 0, False)
                router(g * 2 - 1, 1)
                v_T(g * 2 + 1, 1, False)
                router(g * 2, 0)
            v_T(NT - 1, 0, False)
            router(NT - 2, 1)
            router(NT - 1, 0)

            pe.wait_ge(s_msum, 1)
            pe.wait_ge(s_tri, 4)
            pe.matmul(Q[0][:, 0:NE], tri, rt(6).rearrange("p t e -> p (t e)"), start=True, stop=True)
            pe.matmul(Q[1][:, 0:NE], ones[:], rt(6).rearrange("p t e -> p (t e)"), start=True, stop=True).then_inc(s_cnt, 1)

            for n in range(2 * NT):
                if n % PART == 0:
                    pe.wait_ge(s_onehots, n // PART + 1)
                mm = pe.matmul(Q[2][:, 0:2 * SC].rearrange("p (v t) -> p v t", v=2), LO[:, n, :], V2[:, :, n, :],
                               start=(n == 0), stop=(n == 2 * NT - 1))
            mm.then_inc(s_perm, 1)

            pe.wait_ge(s_routed, 1)

            def tokens_T(n, b, i, first):
                for h in range(2):
                    pe.wait_ge(s_xg[2 * i + h], (b + 1) * 16)
                if not first:
                    pe.wait_ge(s_xt, n)
                for h in range(2):
                    for q in range(4):
                        last = pe.transpose(P16[:, q * SLOT_ROWS + h * P:q * SLOT_ROWS + (h + 1) * P],
                                            XGr[2 * i + h][:, q * P:(q + 1) * P], ident16[:])
                last.then_inc(s_xgT, 1)

            def up(n, e, i, first):
                pe.wait_ge(s_xt, n + 1)
                for c in range(KH):
                    if not first and c % 2 == 0:
                        pe.wait_ge(s_gelu, (n - 1) * KH + (c + 2))
                    q = 0
                    for k in range(KD):
                        for w, v in ((W1hi, 0), (W1hi, 1), (W1lo, 0)):
                            last = pe.matmul(PH[:, c * SLOT_ROWS:(c + 1) * SLOT_ROWS],
                                             w[:, ds(e, 1), k, c * P:(c + 1) * P].rearrange("p a h -> p (a h)"),
                                             XT16[i][:, v, k, :], start=(q == 0), stop=(q == 3 * KD - 1))
                            q += 1
                    if c % 2 == 1:
                        last.then_inc(s_h1, 1)

            def down(n, e, first):
                if not first:
                    pe.wait_ge(s_yr, n * 2)
                for half in range(2):
                    pe.wait_ge(s_hs, n * 4 + 2 * (half + 1))
                    for c in range(half * KH // 2, (half + 1) * KH // 2):
                        for hv, w in ((HHI, W2hi), (HHI, W2lo), (HLO, W2hi)):
                            for h in range(2):
                                last = pe.matmul(PA[h][:, 0:D], hv[:, c * SLOT_ROWS + h * P:c * SLOT_ROWS + (h + 1) * P],
                                                 w[:, ds(e, 1), c, :].rearrange("p a d -> p (a d)"),
                                                 start=(c == 0 and w is W2hi and hv is HHI),
                                                 stop=(c == KH - 1 and hv is HLO))
                    last.then_inc(s_y, 1)

            def expert(n):
                return pe.value_load(exp_i[0:1, ds(n, 1)], min_val=0, max_val=E - 1)

            def turn(b, first, last):
                before = None if first else expert(b * U - 1)
                es = [expert(b * U + i) for i in range(U)]
                for i in range(U):
                    n = b * U + i
                    if not (last and i == U - 1):
                        tokens_T(n + 1, b if i < U - 1 else b + 1, 1 - i, False)
                    up(n, es[i], i, first and i == 0)
                    if i or not first:
                        down(n - 1, es[i - 1] if i else before, first)
            tokens_T(0, 0, 0, True)
            turn(0, True, False)
            with pe.Fori(1, NB - 1) as b:
                turn(b, False, False)
            turn(NB - 1, False, True)
            down(ST - 1, expert(ST - 1), False)

        @block.vector
        def _(dve):
            made = [0]

            def link(ins):
                made[0] += 1
                ins.then_inc(s_dve, 1)
                dve.wait_ge(s_dve, made[0])

            dve.wait_ge(s_edges, 64)
            dve.tensor_copy(edge_df[0:ROWS, :], edge_d[0:ROWS, :]).then_inc(s_edge_f, 1)
            dve.tensor_copy(edge_sf[0:ROWS, :], edge_s[0:ROWS, :]).then_inc(s_edge_f, 1)
            dve.wait_ge(s_edge_f, 2)
            dve.wait_ge(s_const, 6)
            edv = edge_df[0:ROWS, :].rearrange("r (c p) -> r c p", c=4)
            dve.tensor_reduce(tmin[0:ROWS, :], edv, AX, ALU.min)
            link(dve.tensor_reduce(tmax[0:ROWS, :], edv, AX, ALU.max))
            for c in range(4):
                dve.tensor_scalar(tmin_w[0:ROWS, c * P:(c + 1) * P], ones[0:ROWS, :], tmin[0:ROWS, c:c + 1], None,
                                  ALU.mult).then_inc(s_tmin, 1)
            link(dve.tensor_tensor(tdif[0:ROWS, :], tmax[0:ROWS, :], tmin[0:ROWS, :], ALU.subtract))
            dve.tensor_reduce(tspan[0:ROWS, :], tdif[0:ROWS, :], AX, ALU.max).then_inc(s_tmin, 1)

            def tiles_of(v):
                return v.rearrange("p (q c) -> p q c", c=4)

            def rows4(q):
                return q[:, 0:ET].rearrange("p (c q) -> p q c", c=4)
            dve.wait_ge(s_edge_T, 2)
            dve.tensor_copy(tiles_of(src_i[:]), rows4(Q[1]))
            link(dve.tensor_copy(tiles_of(dst_f), rows4(Q[0])))
            dve.wait_ge(s_tmin_bc, 1)
            dve.tensor_tensor(tiles_of(dst_rel[:]), tiles_of(dst_f), rows4(Q[2]), ALU.subtract)
            link(dve.tensor_scalar(tiles_of(base_f), rows4(Q[2])[0:1], float(NPAD - WINDOW), None, ALU.min))
            dve.tensor_copy(base_i[:, :, 0:BODY], base_f.rearrange("p (b k) -> p b k", b=2 * E))
            dve.wait_ge(s_span_T, 1)
            link(dve.tensor_reduce(npass_f, Q[3][0:1, 0:ROWS], AX, ALU.max))
            link(dve.tensor_copy(npass_i[:, 0:1], npass_f))
            link(dve.tensor_scalar(npass_i[:, 1:2], npass_i[:, 0:1], WINDOW.bit_length() - 1, None, ALU.arith_shift_right))
            link(dve.tensor_scalar(npass_i[:, 2:3], npass_i[:, 1:2], 1.0, None, ALU.add))
            link(dve.tensor_copy(dst_i, dst_f))
            link(dve.tensor_scalar(lohi_i, dst_i, LOW - 1, None, ALU.bitwise_and))
            link(dve.tensor_copy(lo16, lohi_i))
            link(dve.tensor_scalar(lohi_i, dst_i, LOW.bit_length() - 1, None, ALU.arith_shift_right))
            link(dve.tensor_copy(hi16, lohi_i))
            dve.wait_ge(s_par_T, 1)
            dve.tensor_copy(params[:], PB[:, 0:PROWS]).then_inc(s_params, 1)
            dve.sem_inc(s_edges_done, 1)
            dve.tensor_copy(ident16[:], ident[:])

            def combine(sv):
                m_e, q_e, m_o, q_o = (sv[:, :, v:v + 1].rearrange("p t a -> p (t a)") for v in (1, 2, 4, 5))
                dve.tensor_tensor(nst[:, 0, :], m_e, m_o, ALU.add)
                dve.tensor_tensor(nst[:, 2, :], q_e, q_o, ALU.add)
                link(dve.tensor_tensor(nst[:, 1, :], m_e, m_o, ALU.subtract))
                link(dve.tensor_tensor(nst[:, 1, :], nst[:, 1, :], nst[:, 1, :], ALU.mult))
                dve.tensor_scalar(nst[:, 0, :], nst[:, 0, :], 0.5, None, ALU.mult)
                return dve.scalar_tensor_tensor(out=nst[:, 2, :], in0=nst[:, 1, :], scalar=D / 4.0, in1=nst[:, 2, :],
                                                op0=ALU.mult, op1=ALU.add)
            for half in range(2):
                a, b = half * ET // 2, (half + 1) * ET // 2
                for j in range(LOW):
                    dve.tensor_scalar(mask_lo[:, j, a:b], lo16[:, a:b], float(j), None, ALU.is_equal)
                for j in range(HIGH // 2, HIGH):
                    last = dve.tensor_scalar(mask_hi[:, j, a:b], hi16[:, a:b], float(j), None, ALU.is_equal)
                last.then_inc(s_masks, 1)
                if half == 0:
                    dve.wait_ge(s_gcnw, 16)
                    dve.tensor_reduce(wam, S[:, 0:KD * D], AX, ALU.max, apply_absolute_value=True).then_inc(s_gmax, 1)
                    dve.wait_ge(s_gmax_pe, 1)
                    dve.tensor_reduce(wamr[0:1, :], PA[0][0:1, 0:P], AX, ALU.max).then_inc(s_gmax, 1)
            for t in range(NT):
                if t % XG == 0:
                    dve.wait_ge(s_x[t // XG] if t < 4 * XG else s_xlast, 16)
                last = dve.bn_stats(svx[:, t, :], BR[:, t, :])
            link(last)
            combine(svx).then_inc(s_mean, 1)
            dve.wait_ge(s_gmax_pe, 2)
            link(dve.tensor_scalar(wmax, PA[1][:, 0:1], 1e-30, None, ALU.max))
            link(dve.tensor_scalar(wp2.bitcast(I32), wmax.bitcast(I32), EXPONENT, None, ALU.bitwise_and))
            link(dve.reciprocal(zsc, wp2))
            dve.tensor_scalar(zinv, wp2, (2 * D) / 2.0 ** 15, None, ALU.mult)
            link(dve.tensor_scalar(zsc, zsc, 2.0 ** 15 / (2 * D), None, ALU.mult))
            dve.wait_ge(s_sq, 1)
            dve.reciprocal(nst[:, 6, :], nst[:, 3, :]).then_inc(s_sq, 1)
            dve.wait_ge(s_degsq, 1)
            link(dve.reciprocal(dinv[:], nst[:, 4, :]))
            dve.tensor_scalar(nst[:, 5, :], dinv[:], zsc, None, ALU.mult).then_inc(s_dinv, 1)
            dve.wait_ge(s_sq, 2)

            def xn_tile(t, i, first):
                if not first:
                    dve.wait_ge(s_xT, t - 1)
                dve.tensor_scalar(XN[i], BR[:, ds(t, 1), :].rearrange("p a d -> p (a d)"), nst[:, 0, ds(t, 1)],
                                  nst[:, 6, ds(t, 1)], ALU.subtract, ALU.mult).then_inc(s_xn, 1)

            def t_low(t, i, first):
                dve.wait_ge(s_thi, t + 1)
                dve.tensor_tensor(TH[i][:, D:2 * D], TS[i], TH[i][:, 0:D], ALU.subtract).then_inc(s_tlo, 1)

            def z0_tile(t, i):
                dve.wait_ge(s_tT, t + 1)
                dve.tensor_copy(AT[:, :, ds(t * P, P)],
                                Q[2 + i][:, 0:D].rearrange("p (k n) -> p k n", k=KD)).then_inc(s_z0, 1)
            for i in range(2):
                xn_tile(i, i, True)
            xn_tile(2, 0, False)
            t_low(0, 0, True)
            with dve.Fori(1, NT // 2 - 1) as g:
                for i in range(2):
                    xn_tile(g * 2 + i + 1, 1 - i, False)
                    t_low(g * 2 + (i - 1), 1 - i, False)
                    z0_tile(g * 2 + (i - 2), i)
            for t in range(NT - 3, NT + 2):
                if t + 1 < NT:
                    xn_tile(t + 1, (t + 1) % 2, False)
                if t - 1 < NT:
                    t_low(t - 1, (t - 1) % 2, False)
                z0_tile(t - 2, t % 2)
            dve.wait_ge(s_dinv_T, 1)
            dve.wait_ge(s_xT, NT)
            dve.tensor_copy(XN[1][0:NT, 0:P], PB[0:NT, 128:256]).then_inc(s_dinv_Tc, 1)

            def onehot(n0, c0, k):
                dve.wait_ge(s_msg, n0 + (SLOTS - OH + 1 + k))
                dve.tensor_scalar(oh[:, k % OH, :], iota_w[:], dst_rel[:, ds(c0 + k, 1)], None, ALU.is_equal).then_inc(s_oh, 1)

            def add(n0, base, k):
                dve.wait_ge(s_msg, n0 + (SLOTS + k + 1))
                dve.wait_ge(s_zadd, n0 + (k + 4))
                z = AT[:, :, ds(base, WINDOW)]
                dve.tensor_tensor(z, z, MS[k % 4][:, 0:KD * WINDOW].rearrange("p (m w) -> p m w", m=KD),
                                  ALU.add).then_inc(s_zadd, 1)

            def adds(n0, b, step=None):
                c0 = b * BODY
                for k in range(OH):
                    onehot(n0, c0, k)
                for k in range(BODY):
                    if step:
                        step(k)
                    if k % BASES == 0:
                        _, bases = nc.values_load_multi_w_load_instructions(
                            base_i[0:1, ds(b, 1), k:min(k + BASES, BODY)].rearrange("p a k -> p (a k)"),
                            engines={mybir.EngineType.DVE}, min_val=0, max_val=NPAD - WINDOW,
                            skip_runtime_bounds_check_because="clamped to this range where they are made")
                    add(n0, bases[k % BASES], k)
                    if k + OH < BODY:
                        onehot(n0, c0, k + OH)

            def row_max(u):
                dve.wait_ge(s_w_amT, u + 1)
                dve.tensor_reduce(wamr[0:1, :], PB[0:1, 128:256], AX, ALU.max).then_inc(s_w_amr, 1)

            def scale(u):
                dve.wait_ge(s_w_bc, u + 1)
                dve.tensor_scalar(wmax, PB[:, 256:257], 1e-30, None, ALU.max).then_inc(s_w_sc0, 1)
                dve.wait_ge(s_w_sc0, u * 3 + 1)
                dve.tensor_scalar(wp2.bitcast(I32), wmax.bitcast(I32), EXPONENT, None, ALU.bitwise_and).then_inc(s_w_sc0, 1)
                dve.wait_ge(s_w_sc0, u * 3 + 2)
                dve.reciprocal(wmax, wp2).then_inc(s_w_sc0, 1)
                dve.wait_ge(s_w_sc0, u * 3 + 3)

            def low_part(u, dest, hi):
                dve.wait_ge(s_w_hi, u + 1)
                dve.scalar_tensor_tensor(out=dest, in0=S[:], scalar=wsc, in1=hi, op0=ALU.mult,
                                         op1=ALU.subtract).then_inc(s_w_lo, 1)

            dve.sem_inc(s_zadd, 4)
            dve.wait_ge(s_z0, NT)
            dve.sem_inc(s_w_lo, 1)
            with dve.Fori(0, E) as e:
                bcol = params[:, ds(e * KH, KH)]

                def step(k):
                    if k == 0:
                        dve.tensor_copy(lnb, params[:, ds(e * KD + CB, KD)]).then_inc(s_lnb, 1)
                    if k == 14:
                        dve.wait_ge(s_w_fold, e * 2 + 2)
                        dve.tensor_reduce(wam, S[:], AX, ALU.max, apply_absolute_value=True).then_inc(s_w_am0, 1)
                        dve.wait_ge(s_browT, e + 1)
                        dve.tensor_tensor(bnew, bcol, PB[:, 0:KH], ALU.add).then_inc(s_w_am0, 1)
                    if k == 15:
                        dve.wait_ge(s_w_am0, e * 3 + 2)
                        dve.tensor_reduce(wam2, bnew, AX, ALU.max, apply_absolute_value=True).then_inc(s_w_am0, 1)
                        dve.tensor_copy(bcol, bnew)
                    if k == 16:
                        dve.wait_ge(s_w_am0, e * 3 + 3)
                        dve.scalar_tensor_tensor(out=wam, in0=wam, scalar=float(D), in1=wam2, op0=ALU.mult,
                                                 op1=ALU.max).then_inc(s_w_am, 1)
                    if k == 19:
                        row_max(e)
                    if k == 22:
                        scale(e)
                        dve.tensor_scalar(sc1[:, ds(e, 1)], wp2, 2.0 ** -21 / XN_SCALE, None, ALU.mult)
                        dve.tensor_scalar(shs[:, ds(e, 1)], wmax, 2.0 ** 13, None, ALU.mult)
                        dve.tensor_scalar(sc2[:, ds(e, 1)], wp2, 2.0 ** -13, None, ALU.mult)
                        dve.tensor_scalar(wsc, wmax, 2.0 ** 21, None, ALU.mult).then_inc(s_w_sc, 1)
                    if k == 25:
                        low_part(e, W1lo[:, ds(e, 1), :, :].rearrange("p a k h -> p (a k h)"),
                                 W1hi[:, ds(e, 1), :, :].rearrange("p a k h -> p (a k h)"))
                adds(e * BODY, e, step)
            with dve.Fori(0, E) as e:
                def step(k):
                    if k == 6:
                        dve.wait_ge(s_w_ld, (e + (E + 1)) * 16)
                        dve.tensor_reduce(wam, S[:], AX, ALU.max, apply_absolute_value=True).then_inc(s_w_am, 1)
                    if k == 11:
                        row_max(e + E)
                    if k == 14:
                        scale(e + E)
                        dve.scalar_tensor_tensor(out=sc2[:, ds(e, 1)], in0=sc2[:, ds(e, 1)], scalar=2.0 ** -13, in1=wp2,
                                                 op0=ALU.mult, op1=ALU.mult)
                        dve.tensor_scalar(wsc, wmax, 2.0 ** 13, None, ALU.mult).then_inc(s_w_sc, 1)
                    if k == 20:
                        low_part(e + E, W2lo[:, ds(e, 1), :, :].rearrange("p a c d -> p (a c d)"),
                                 W2hi[:, ds(e, 1), :, :].rearrange("p a c d -> p (a c d)"))
                adds((e + E) * BODY, e + E, step)
            npass = dve.value_load(npass_i[:, 2:3], min_val=1, max_val=NPAD // WINDOW)
            with dve.If(npass > 1):
                with dve.Fori(1, npass) as w:
                    dve.wait_ge(s_zadd, w * ET + 4)
                    dve.tensor_scalar(iota_w[:], iota_w[:], float(WINDOW), None, ALU.add).then_inc(s_passb, 1)
                    dve.tensor_scalar(base_i[:, :, 0:BODY], base_i[:, :, 0:BODY], float(WINDOW), float(NPAD - WINDOW), ALU.add,
                                      ALU.min).then_inc(s_passb, 1)
                    dve.wait_ge(s_passb, w * 2)
                    dve.sem_inc(s_passgo, 1)
                    with dve.Fori(0, 2 * E) as b:
                        adds(w * ET + b * BODY, b)
            dve.wait_ge(s_zadd, npass * ET + 4)
            dve.sem_inc(s_gathered, 1)

            for c in range(NCH):
                dve.wait_ge(s_dbc[c // 2], 16)
                for m in range(KD):
                    z = AT[:, m, c * CH:(c + 1) * CH]
                    last = dve.tensor_tensor(z, z, R[:, c * CH:(c + 1) * CH], ALU.mult)
                last.then_inc(s_zs, 1)
            dve.sem_inc(s_dxg, 1)

            def mix(c, i):
                h = AT[:, :, ds(c * CH, CH)]
                dve.wait_ge(s_sig, c + 1)
                dve.wait_ge(s_dx, c + 1)
                dve.tensor_tensor(h, DX, G[i][:, :, 0:CH],
                                  ALU.mult).then_inc(s_dxg, 1)
                dve.wait_ge(s_dxg, c + 2)
                dve.tensor_tensor(h, h, BT[:, :, ds(c * CH, CH)], ALU.add).then_inc(s_mix, 1)
                dve.wait_ge(s_mix, c + 1)
                dve.tensor_scalar(h, h, 0.0, None, ALU.max).then_inc(s_h, 1)
                dve.wait_ge(s_h, c + 1)

            def node_stats(c, n):
                for m in range(KD):
                    last = dve.bn_stats(bsv[:, m, ds(c, 1), :].rearrange("p a v -> p (a v)"), AT[:, m, ds(c * CH, n)])
                return last
            with dve.Fori(0, NCH // 2 - 1) as g:
                for i in range(2):
                    mix(g * 2 + i, i)
                    node_stats(g * 2 + i, CH)
            mix(NCH - 2, 0)
            node_stats(NCH - 2, CH)
            mix(NCH - 1, 1)
            link(node_stats(NCH - 1, N - (NCH - 1) * CH))
            for m in range(KD):
                last = dve.bn_aggr(bmv[:, m, :], bsv[:, m, :, :].rearrange("p c v -> p (c v)"))
            last.then_inc(s_bnsq, 1)
            dve.wait_ge(s_bnsq, 2)
            link(dve.reciprocal(brs, bsq))
            link(dve.tensor_tensor(bsc, brs, params[:, CV + 3 * KD:CV + 4 * KD], ALU.mult))
            link(dve.tensor_tensor(brs, bmv[:, :, 0:1].rearrange("p k a -> p (k a)"), bsc, ALU.mult))
            dve.tensor_tensor(bbi, params[:, CV + 4 * KD:CV + 5 * KD], brs, ALU.subtract).then_inc(s_bn, 1)

            def x2_tile(t, i):
                v = BR[:, ds(t, 1), :].rearrange("p a d -> p (a d)")
                dve.wait_ge(s_hT, t + 1)
                dve.tensor_tensor(v, v, PA[i][:, 0:D], ALU.add).then_inc(s_x2, 1)
                dve.wait_ge(s_x2, t + 1)
                return dve.bn_stats(svh[:, ds(t, 1), :].rearrange("p a v -> p (a v)"), v)
            for q in range(4):
                dve.wait_ge(s_xr[q], 16)
                with dve.Fori(q * XG // 2, (q + 1) * XG // 2) as g:
                    for i in range(2):
                        x2_tile(g * 2 + i, i)
            dve.wait_ge(s_xr[4], 16)
            link(x2_tile(NT - 1, 0))
            combine(svh).then_inc(s_var, 1)
            dve.wait_ge(s_sq1, 1)
            link(dve.reciprocal(nst[:, 6, :], nst[:, 3, :]))
            link(dve.tensor_tensor(nst[:, 1, :], nst[:, 6, :], nst[:, 6, :], ALU.mult))
            dve.tensor_tensor(nst[:, 4, :], nst[:, 2, :], nst[:, 1, :], ALU.mult).then_inc(s_v2, 1)
            dve.wait_ge(s_sq2, 1)
            link(dve.reciprocal(nst[:, 7, :], nst[:, 5, :]))
            link(dve.scalar_tensor_tensor(out=nst[:, 7, :], in0=nst[:, 7, :], scalar=XN_SCALE, in1=nst[:, 6, :],
                                          op0=ALU.mult, op1=ALU.mult))

            def token(t, i, first):
                if not first:
                    dve.wait_ge(s_vT, t - 1)
                    dve.wait_ge(s_xlo, t - 1)
                dve.tensor_scalar(V[i], BR[:, ds(t, 1), :].rearrange("p a d -> p (a d)"), nst[:, 0, ds(t, 1)],
                                  nst[:, 7, ds(t, 1)], ALU.subtract, ALU.mult).then_inc(s_v, 1)

            def token_low(t, i):
                dve.wait_ge(s_xhi, t + 1)
                dve.tensor_tensor(XH[i][:, D:2 * D], V[i], XH[i][:, 0:D], ALU.subtract).then_inc(s_xlo, 1)
            token(0, 0, True)
            token(1, 1, True)
            token_low(0, 0)
            with dve.Fori(1, NT // 2) as g:
                token(g * 2, 0, False)
                token_low(g * 2 - 1, 1)
                token(g * 2 + 1, 1, False)
                token_low(g * 2, 0)
            token(NT - 1, 0, False)
            token_low(NT - 2, 1)
            token_low(NT - 1, 0)

            def bc_e(v):
                return v.rearrange("p (t a) -> p t a", a=1).to_broadcast([P, NT, E])

            def bc_t(v, n=E):
                return v.rearrange("p (a e) -> p a e", a=1).to_broadcast([P, NT, n])
            m1, zs, p1, p2 = nst[:, 1, :], nst[:, 2, :], nst[:, 3, :], nst[:, 4, :]
            i1, i2, pos = nst[:, 6, :], nst[:, 7, :], nst[:, 0, :]
            L, EX, PR, EQ, O1, O2, CHOSEN = (rt(i) for i in range(7))
            TOT, INC, SL, TMP = rt(7), rt(8), rt(9), rt(10)
            dve.wait_ge(s_log, NT)
            dve.wait_ge(s_wr, 32)
            dve.wait_ge(s_tri, 4)
            link(dve.tensor_scalar(nst[:, 5, :], nst[:, 5, :], 1.0 / XN_SCALE, None, ALU.mult))
            link(dve.tensor_tensor(L, PB[:, 0:NE].rearrange("p (t e) -> p t e", e=E), bc_e(nst[:, 5, :]), ALU.mult))
            link(dve.tensor_tensor(L, L, bc_t(brS), ALU.add))
            link(dve.tensor_reduce(m1, L, AX, ALU.max))
            dve.tensor_tensor(EX, L, bc_e(m1), ALU.subtract).then_inc(s_sh, 1)
            dve.wait_ge(s_exp, 1)
            link(dve.tensor_reduce(zs, EX, AX, ALU.add))
            link(dve.reciprocal(zs, zs))
            link(dve.tensor_tensor(PR, EX, bc_e(zs), ALU.mult))

            def choose(one, best, index):
                link(dve.tensor_reduce(best, PR, AX, ALU.max))
                link(dve.tensor_tensor(EQ, PR, bc_e(best), ALU.is_equal))
                link(dve.scalar_tensor_tensor(out=EQ, in0=EQ, scalar=-float(E), in1=bc_t(iota[:, E:2 * E]),
                                              op0=ALU.mult, op1=ALU.add))
                link(dve.tensor_reduce(index, EQ, AX, ALU.min))
                link(dve.tensor_tensor(one, bc_t(iota[:, 0:E]), bc_e(index), ALU.is_equal))
            choose(O1, p1, i1)
            link(dve.scalar_tensor_tensor(out=PR, in0=O1, scalar=-2.0, in1=PR, op0=ALU.mult, op1=ALU.add))
            choose(O2, p2, i2)
            link(dve.tensor_tensor(zs, p1, p2, ALU.add))
            link(dve.reciprocal(zs, zs))
            dve.tensor_tensor(wts[:, 0, :], p1, zs, ALU.mult)
            dve.tensor_tensor(wts[:, 1, :], p2, zs, ALU.mult)
            link(dve.tensor_tensor(CHOSEN, O1, O2, ALU.add))
            dve.tensor_tensor(CHOSEN, CHOSEN, bc_e(valid), ALU.mult).then_inc(s_msum, 1)
            dve.wait_ge(s_cnt, 1)
            link(dve.tensor_copy(TOT.rearrange("p t e -> p (t e)").rearrange("p (e t) -> p e t", e=E),
                                 Q[1][:, 0:NE].rearrange("p (t e) -> p e t", e=E)))
            tot = TOT.rearrange("p t e -> p (t e)").rearrange("p (e t) -> p e t", e=E)
            inc = INC.rearrange("p t e -> p (t e)").rearrange("p (e t) -> p e t", e=E)
            for e in range(E):
                last = dve.tensor_tensor_scan(inc[:, e, :], ones[:, 0:NT], tot[:, e, :], 0.0, ALU.mult, ALU.add)
            link(last)
            work = A[:, 24 * 256:24 * 256 + 8 * E]
            cf, ci, ti, te, tend, tst = (work[:, E * a:E * (a + 1)] for a in range(6))
            link(dve.tensor_scalar(cf, inc[:, :, NT - 1:NT].rearrange("p e a -> p (e a)"), float(SLOT_ROWS - 1), None, ALU.add))
            link(dve.tensor_copy(ci.bitcast(I32), cf))
            link(dve.tensor_scalar(ti.bitcast(I32), ci.bitcast(I32), SLOT_ROWS.bit_length() - 1, None,
                                   ALU.arith_shift_right))
            link(dve.tensor_copy(te, ti.bitcast(I32)))
            link(dve.tensor_tensor_scan(tend, ones[:, 0:E], te, 0.0, ALU.mult, ALU.add))
            link(dve.tensor_tensor(tst, tend, te, ALU.subtract))
            link(dve.tensor_scalar(tst, tst, float(SLOT_ROWS), None, ALU.mult))
            link(dve.tensor_tensor(SL, inc.rearrange("p e t -> p t e"), tot.rearrange("p e t -> p t e"), ALU.subtract))
            link(dve.tensor_tensor(SL, SL, Q[0][:, 0:NE].rearrange("p (t e) -> p t e", e=E), ALU.add))
            link(dve.tensor_tensor(SL, SL, bc_t(tst), ALU.add))
            link(dve.tensor_scalar(far, valid, -float(P * P * P), float(P * P * P), ALU.mult, ALU.add))
            lane = rt(11).rearrange("p t e -> p (t e)")[:, 0:2 * NT]
            tile_of = rt(12).rearrange("p t e -> p (t e)")[:, 0:2 * NT]
            posi = rt(13).rearrange("p t e -> p (t e)")[:, 0:2 * NT].bitcast(I32)
            pi2 = rt(14).rearrange("p t e -> p (t e)")[:, 0:2 * NT].bitcast(I32)
            for k, one in enumerate((O1, O2)):
                link(dve.tensor_tensor(TMP, SL, one, ALU.mult))
                link(dve.tensor_reduce(pos, TMP, AX, ALU.add))
                link(dve.tensor_tensor(pos, pos, far, ALU.add))
                link(dve.tensor_copy(posi.rearrange("p (t k) -> p t k", k=2)[:, :, k:k + 1],
                                     pos.rearrange("p (t a) -> p t a", a=1)))
            link(dve.tensor_scalar(pi2, posi, P - 1, None, ALU.bitwise_and))
            link(dve.tensor_copy(lane, pi2))
            link(dve.tensor_scalar(pi2, posi, P.bit_length() - 1, None, ALU.arith_shift_right))
            link(dve.tensor_copy(tile_of, pi2))

            link(dve.tensor_copy(lt16[:, 0, :], lane))
            link(dve.tensor_copy(lt16[:, 1, :], tile_of))

            dve.wait_ge(s_xh_st[0], 16 * (NT - NT // 2))
            dve.wait_ge(s_xh_st[1], 16 * (NT // 2))

            def spread_to(v, n):
                return v.rearrange("p (t a) -> p t a", a=1).to_broadcast([P, PART, n])
            for c in range(2 * NT // PART):
                r = slice(c * PART, (c + 1) * PART)
                dve.tensor_tensor(LO[:, r, :], spread_to(lt16[:, 0, r], P),
                                  iota16.rearrange("p (a n) -> p a n", a=1).to_broadcast([P, PART, P]), ALU.is_equal)
                link(dve.tensor_tensor(V2[:, 1, r, :], spread_to(lt16[:, 1, r], SC),
                                       iota16[:, 0:SC].rearrange("p (a n) -> p a n", a=1).to_broadcast([P, PART, SC]),
                                       ALU.is_equal))
                link(dve.tensor_tensor(V2[:, 0, r, :], V2[:, 1, r, :], spread_to(iota16[:, c * PART + 1:(c + 1) * PART + 1], SC),
                                       ALU.mult))
                dve.tensor_scalar(V2[:, 1, r, :], V2[:, 1, r, :], iota_p, None, ALU.mult).then_inc(s_onehots, 1)
            ef = rt(15).rearrange("p t e -> p (t e)")[:, 0:ST]
            link(dve.tensor_scalar(ef, iota[:, 0:ST], tend[:, 0:1], None, ALU.is_ge))
            for e in range(1, E):
                link(dve.scalar_tensor_tensor(out=ef, in0=iota[:, 0:ST], scalar=tend[:, e:e + 1], in1=ef,
                                              op0=ALU.is_ge, op1=ALU.add))
            dve.tensor_scalar(exp_i, ef, float(E - 1), None, ALU.min)
            dve.wait_ge(s_perm, 1)
            v1, lane_s = Q[2][:, 0:SC], Q[2][:, SC:2 * SC]
            sf = [rt(16 + a).rearrange("p t e -> p (t e)")[:, 0:SC] for a in range(4)]
            slot_id = A[:, 21 * 256 + 64:21 * 256 + 64 + SC]
            filled, vi, vh, tok = sf
            link(dve.tensor_scalar(filled, v1, 0.0, None, ALU.is_gt))
            link(dve.tensor_scalar(vi.bitcast(I32), v1, -1.0, 0.0, ALU.add, ALU.max))
            link(dve.tensor_scalar(vh.bitcast(I32), vi.bitcast(I32), 1, None, ALU.arith_shift_right))
            link(dve.tensor_copy(tok, vh.bitcast(I32)))
            link(dve.scalar_tensor_tensor(out=tok, in0=tok, scalar=float(P), in1=lane_s, op0=ALU.mult, op1=ALU.add))
            dve.tensor_copy(gidx, tok)
            link(dve.tensor_scalar(vh.bitcast(I32), vi.bitcast(I32), 1, None, ALU.bitwise_and))
            link(dve.tensor_copy(vi, vh.bitcast(I32)))
            link(dve.scalar_tensor_tensor(out=vi, in0=tok, scalar=2.0, in1=vi, op0=ALU.mult, op1=ALU.add))
            link(dve.tensor_tensor(vi, vi, slot_id, ALU.subtract))
            link(dve.tensor_tensor(vi, vi, filled, ALU.mult))
            link(dve.tensor_tensor(vi, vi, slot_id, ALU.add))
            dve.tensor_copy(sidx, vi).then_inc(s_routed, 1)

            dve.wait_ge(s_b2, 16)
            dve.wait_ge(s_routed, 1)

            def expert(n):
                return dve.value_load(exp_i[0:1, ds(n, 1)], min_val=0, max_val=E - 1)

            def result(n, e, b, i, first):
                for h in range(2):
                    j = 2 * i + h
                    if h == 0:
                        dve.wait_ge(s_y, n * 2 + 2)
                    if not first:
                        dve.wait_ge(s_sc[j], b * 16)
                    dve.scalar_tensor_tensor(out=Y[j], in0=PA[h][:, 0:D], scalar=sc2[:, ds(e, 1)],
                                             in1=b2bc[:, ds(e, 1), :].rearrange("p a d -> p (a d)"),
                                             op0=ALU.mult, op1=ALU.add).then_inc(s_yr, 1)

            def split(n, e, half, first):
                c0, c1 = half * KH // 2 * SLOT_ROWS, (half + 1) * KH // 2 * SLOT_ROWS
                dve.wait_ge(s_gelu, n * KH + (half + 1) * KH // 2)
                if not first:
                    dve.wait_ge(s_y, n * 2 + (half - 1))
                dve.tensor_scalar(HHI[:, c0:c1], HF[:, c0:c1], shs[:, ds(e, 1)], None, ALU.mult).then_inc(s_hs, 1)
                dve.wait_ge(s_hs, n * 4 + (2 * half + 1))
                dve.scalar_tensor_tensor(out=HLO[:, c0:c1], in0=HF[:, c0:c1], scalar=shs[:, ds(e, 1)],
                                         in1=HHI[:, c0:c1], op0=ALU.mult, op1=ALU.subtract).then_inc(s_hs, 1)

            def step(n, e, before, b, i, first_tile, first_turn):
                split(n, e, 0, first_tile)
                if not first_tile:
                    result(n - 1, before, b, 1 - i, first_turn)
                split(n, e, 1, first_tile)

            e0, e1, e2, e3 = (expert(n) for n in range(4))
            step(0, e0, None, 0, 0, True, True)
            step(1, e1, e0, 0, 1, False, True)
            step(2, e2, e1, 0, 0, False, True)
            step(3, e3, e2, 1, 1, False, False)
            with dve.Fori(2, NB) as b:
                before, ea, eb = (expert(b * U + d) for d in (-1, 0, 1))
                step(b * U, ea, before, b - 1, 0, False, False)
                step(b * U + 1, eb, ea, b, 1, False, False)
            result(ST - 1, expert(ST - 1), NB - 1, 1, False)

            def final(t, y, rows):
                o = BR[0:rows, ds(t, 1), :].rearrange("p a d -> p (a d)")
                dve.scalar_tensor_tensor(out=o, in0=y[0:rows, 0, :], scalar=wts[0:rows, 0, ds(t, 1)], in1=o,
                                         op0=ALU.mult, op1=ALU.add).then_inc(s_fin0, 1)
                dve.wait_ge(s_fin0, t + 1)
                dve.scalar_tensor_tensor(out=o, in0=y[0:rows, 1, :], scalar=wts[0:rows, 1, ds(t, 1)], in1=o,
                                         op0=ALU.mult, op1=ALU.add).then_inc(s_fin, 1)
            for g in range(NT // 4):
                dve.wait_ge(s_yload[g % 3], (g // 3 + 1) * 16)
                for a in range(4):
                    final(g * 4 + a, FIN[g % 3][:, a], P)
            dve.wait_ge(s_yload[NT // 4 % 3], (NT // 12 + 1) * 16)
            final(NT - 1, FIN[NT // 4 % 3][:, 0], LAST)


_INS = ['x', 'src', 'dst', 'L0_gnn_gcn_W', 'L0_gnn_gcn_b', 'L0_gnn_lin_W', 'L0_gnn_lin_b', 'L0_gnn_gate_W',
        'L0_gnn_gate_b', 'L0_gnn_bn_gamma', 'L0_gnn_bn_beta', 'L0_ffn_Wr', 'L0_ffn_br', 'L0_ffn_ln_g', 'L0_ffn_ln_b',
        'L0_ffn_W1', 'L0_ffn_b1', 'L0_ffn_W2', 'L0_ffn_b2']


def kernel(**inputs):
    import numpy as _np
    import concourse.bacc as _bacc
    from concourse import mybir as _mybir
    from concourse.bass_utils import run_bass_kernel_spmd as _run

    nc = _bacc.Bacc("TRN2", target_bir_lowering=False, num_devices=1)
    arrays, args = {}, []
    for name in _INS:
        a = _np.ascontiguousarray(inputs[name])
        arrays[f"in_{name}"] = a
        args.append(nc.dram_tensor(f"in_{name}", a.shape, _mybir.dt.from_np(a.dtype), kind="ExternalInput").ap())
    args.append(nc.dram_tensor("out_0", inputs["x"].shape, _mybir.dt.float32, kind="ExternalOutput").ap())
    build_gnn_moe(nc, *args)
    r = _run(nc, [arrays], core_ids=[0])
    return r.results[0]["out_0"]
```

```python
from contextlib import ExitStack

import concourse.bass as bass
from concourse import mybir

P = 128
F32, F16, I32 = mybir.dt.float32, mybir.dt.float16, mybir.dt.int32
ALU = mybir.AluOpType
ACT = mybir.ActivationFunctionType
AX = mybir.AxisListType.X

EPS = 1e-5
WINDOW = 64
SLOTS = 13
BASES = 8
PART = 10
LO_DVE = 3
OH = 6
SLOT_ROWS = 256
U = 2
LOW = 64
XN_SCALE = 1024.0
EXPONENT = 0x7F800000


def build_gnn_moe(nc, x, src, dst, gcn_W, gcn_b, lin_W, lin_b, gate_W, gate_b, bn_gamma, bn_beta,
                  Wr, br, ln_g, ln_b, W1, b1, W2, b2, out):
    N, D = x.shape
    E, _, H = W1.shape
    EDGES = src.shape[0]
    NT = -(-N // P)
    NPAD = NT * P
    KD, KH = D // P, H // P
    LAST = N - (NT - 1) * P
    BODY = 2 * SLOTS
    ET = BODY * 2 * E
    ROWS = ET // 4
    FULL = EDGES // (4 * P)
    TAIL = EDGES - FULL * 4 * P
    XG = (NT - 1) // 4
    CH = 400
    NCH = NPAD // CH
    ST = (2 * N + E * (SLOT_ROWS - 1)) // SLOT_ROWS
    SC = ST * SLOT_ROWS // P
    NB = ST // U
    HIGH = NPAD // LOW
    HIGH_POOL = 16
    DUMP = 2 * NPAD
    EW = E * KD * H
    assert KD == 2 and ET * P >= EDGES and FULL == ROWS - 1 and 0 < TAIL <= 4 * P and ROWS <= P
    assert ST % U == 0 and NPAD % CH == 0 and (LOW + HIGH) * ET <= 4 * EW - 2 * KD * D and NPAD < 2 ** 15
    assert 2 * LOW == P and SLOT_ROWS == 2 * P
    CB1, CG = 0, E * KH
    CB = CG + E * KD
    CV = CB + E * KD
    PROWS = CV + 5 * KD
    SPAN0 = 384

    t_dram = nc.dram_tensor("message_table", (NPAD, 2 * D), F16, kind="Internal").ap()
    xnT_dram = nc.dram_tensor("xnT_table", (P, KD, NPAD), F32, kind="Internal").ap()
    dinv_dram = nc.dram_tensor("dinv_row", (NT, P), F32, kind="Internal").ap()
    xn_dram = nc.dram_tensor("token_table", (NPAD, 2 * D), F16, kind="Internal").ap()
    y_dram = nc.dram_tensor("expert_rows", (DUMP + SC * P, D), F32, kind="Internal").ap()

    with ExitStack() as ctx:
        def sb(name, shape, dt):
            return ctx.enter_context(nc.sbuf_tensor(name, shape, dt))

        def sem(name):
            return ctx.enter_context(nc.semaphore(name))

        WALL = sb("WALL", [P, 4 * EW], F16)
        W1hi = WALL[:, 0:EW].rearrange("p (e k h) -> p e k h", e=E, k=KD)
        W1lo = WALL[:, EW:2 * EW].rearrange("p (e k h) -> p e k h", e=E, k=KD)
        W2hi = WALL[:, 2 * EW:3 * EW].rearrange("p (e c d) -> p e c d", e=E, c=KH)
        W2lo = WALL[:, 3 * EW:4 * EW].rearrange("p (e c d) -> p e c d", e=E, c=KH)
        mask_lo = WALL[:, 0:LOW * ET].rearrange("p (k t) -> p k t", t=ET)
        mask_hi = WALL[:, LOW * ET:(LOW + HIGH) * ET].rearrange("p (k t) -> p k t", t=ET)
        brow = WALL[0:1, 3 * EW:3 * EW + 2 * H].bitcast(F32)

        A = sb("A", [P, KD * NPAD], F32)
        B = sb("B", [P, KD * NPAD], F32)
        R = sb("R", [P, SLOTS * D], F32)
        S = sb("S", [P, KD * H], F32)

        AT = A[:].rearrange("p (k n) -> p k n", k=KD)
        BT = B[:].rearrange("p (k n) -> p k n", k=KD)
        BR = B[:].rearrange("p (t d) -> p t d", d=D)
        RS = R[:].rearrange("p (s d) -> p s d", d=D)

        edge_d = A[:, 0:4 * P].bitcast(I32)
        edge_s = A[:, 4 * P:8 * P].bitcast(I32)
        edge_df = A[:, 8 * P:12 * P]
        edge_sf = A[:, 12 * P:16 * P]
        tmin_w = A[:, 16 * P:20 * P]
        prow = A[:, 20 * P:21 * P]
        tmin = A[:, 21 * P:21 * P + 4]
        tmax = A[:, 21 * P + 4:21 * P + 8]
        tdif = A[:, 21 * P + 8:21 * P + 12]
        tspan = A[:, 21 * P + 12:21 * P + 13]
        dst_f = R[:, 0:ET]
        dst_i = R[:, ET:2 * ET].bitcast(I32)
        lohi_i = R[:, 2 * ET:3 * ET].bitcast(I32)
        lo16 = R[:, 3 * ET:3 * ET + ET // 2].bitcast(F16)
        hi16 = R[:, 3 * ET + ET // 2:4 * ET].bitcast(F16)
        XN = [RS[:, 7, :], RS[:, 8, :]]
        XS = [RS[:, i, :] for i in (9, 10, 2, 3)]
        TS = [RS[:, 11, :], RS[:, 12, :]]
        TH = [RS[:, i, :].bitcast(F16) for i in (0, 1, 4, 5)]
        gcnW = S[:, 0:KD * D].rearrange("p (k n) -> p k n", k=KD)
        linWv = WALL[:, 4 * EW - 2 * KD * D:4 * EW].bitcast(F32).rearrange("p (k n) -> p k n", k=KD)
        gateW = gcnW
        SW1 = S[:].rearrange("p (k h) -> p k h", k=KD)
        b2bc = S[:].rearrange("p (e d) -> p e d", e=E)

        ident = sb("ident", [P, P], F32)
        ones = sb("ones", [P, P], F32)
        iota = sb("iota", [P, P], F32)
        iota_w = sb("iota_w", [P, WINDOW], F32)
        src_i = sb("src_i", [P, ET + SLOTS], I32)
        dst_rel = sb("dst_rel", [P, ET], F32)
        route = sb("route", [P, 2 * E * (BODY + 2)], F32)
        base_i = route[0:1, :].bitcast(I32).rearrange("p (b k) -> p b k", b=2 * E)
        base_f = A[0:1, 4096:4096 + ET]
        params = sb("params", [P, PROWS], F32)
        ident16 = sb("ident16", [P, P], F16)
        idx_ring = sb("idx_ring", [P, BODY], I32)
        dinv = sb("dinv", [P, NT], F32)
        small = sb("small", [P, 64], F32)
        npass_f, npass_i = small[0:1, 0:1], small[0:1, 1:4].bitcast(I32)
        wam, wmax = small[:, 4:5], small[:, 5:6]
        wp2 = small[:, 6:7]
        wsc = small[:, 7:8]
        epst = small[:, 8:9]
        halfb = small[:, 9:11]
        bmv = small[:, 12:16].rearrange("p (k v) -> p k v", k=KD)
        bsq, brs, bsc, bbi = small[:, 16:18], small[:, 18:20], small[:, 20:22], small[:, 22:24]
        iota_p = small[:, 24:25]
        zsc, zinv = small[:, 27:28], small[:, 28:29]
        lnb = small[:, 29:31]
        bnew = small[:, 56:56 + KH]
        wam2 = small[:, 25:26]
        wamr = small[:, 26:27]
        sc1, shs, sc2 = small[:, 32:32 + E], small[:, 40:40 + E], small[:, 48:48 + E]
        svx = A[:, 22 * P:22 * P + 6 * NT].rearrange("p (t v) -> p t v", v=6)
        bsv = R[:, NPAD:NPAD + KD * NCH * 6].rearrange("p (k c v) -> p k c v", k=KD, v=6)
        svh = RS[:, 10, 0:6 * NT].rearrange("p (t v) -> p t v", v=6)
        nst = sb("nst", [P, 8, NT], F32)
        oh = nst[:].rearrange("p a t -> p (a t)")[:, 0:OH * WINDOW // 2].bitcast(F16).rearrange("p (i w) -> p i w", i=OH)

        HN = [RS[:, 0, :], RS[:, 1, :]]
        V = [RS[:, 2, :], RS[:, 3, :]]
        VT = [RS[:, 4, :], RS[:, 5, :]]
        XH = [RS[:, i, :].bitcast(F16) for i in (6, 7, 0, 1)]
        WrS = RS[:, 8, 0:KD * E].rearrange("p (k e) -> p k e", k=KD)
        brS = RS[:, 8, 16:16 + E]
        NE = NT * E

        def rt(i):
            return A[:, i * 256:i * 256 + NE].rearrange("p (t e) -> p t e", e=E)
        tri = A[:, 20 * 256:20 * 256 + P]
        valid = A[:, 21 * 256:21 * 256 + NT]
        far = A[:, 21 * 256 + 32:21 * 256 + 32 + NT]
        iota16 = A[:, 22 * 256:22 * 256 + P // 2].bitcast(F16)
        lane = A[:, 15 * 256 + 64:15 * 256 + 64 + 2 * NT]
        LO = R[:, 0:NT * P].bitcast(F16).rearrange("p (t n) -> p t n", n=P)
        V2 = A[:, 0:2 * NT * SC].bitcast(F16).rearrange("p (v t n) -> p v t n", v=2, n=SC)
        lt16 = A[:, 22 * 256 + 64:22 * 256 + 64 + 2 * NT].bitcast(F16).rearrange("p (v t) -> p v t", v=2)
        wts = route[:, 0:2 * NT].rearrange("p (k t) -> p k t", k=2)
        gidx = route[:, 2 * NT:2 * NT + SC].bitcast(I32)
        sidx = route[:, 2 * NT + SC:2 * NT + 2 * SC].bitcast(I32)
        exp_i = route[:, 2 * NT + 2 * SC:2 * NT + 2 * SC + ST].bitcast(I32)
        g0 = 2 * NT + 2 * SC + ST
        gi = route[:, g0:g0 + 4].bitcast(I32)
        si = route[:, g0 + 4:g0 + 8].bitcast(I32)
        XT16 = [A[:, 512 * i:512 * (i + 1)].bitcast(F16).rearrange("p (v k t) -> p v k t", v=2, k=KD) for i in range(2)]
        HF = A[:, 1024:3072]
        HHI = A[:, 3072:4096].bitcast(F16)
        HLO = A[:, 4096:5120].bitcast(F16)
        XGr = [RS[:, i, :].bitcast(F16) for i in range(4)]
        Y = [RS[:, 4 + i, :] for i in range(4)]
        FIN = [A[:, 2048 * i:2048 * (i + 1)].rearrange("p (t k d) -> p t k d", t=4, k=2) for i in range(3)]

        def ps(name, shape, dt=F32):
            return ctx.enter_context(nc.psum_tensor(name, shape, dt))
        PH = ps("ph", [P, 2048])
        Q = [PH[:, 512 * i:512 * (i + 1)] for i in range(4)]
        PA = [ps("pa0", [P, 512]), ps("pa1", [P, 512])]
        PB = ps("pb", [P, 512])
        P16 = ps("p16", [P, 1024], F16)
        GATE = [[Q[0], Q[1]], [Q[2], Q[3]], PA]
        MS = [PA[0], PA[1], Q[1], Q[2]]

        SPANS = ((0, 3), (3, 5), (5, 7), (7, 8))

        def dbc(c0, c1):
            return S[:, KD * D + c0 * CH:KD * D + c1 * CH] if c1 <= 3 else R[:, c0 * CH:c1 * CH]

        s_const0, s_const, s_pads = sem("const0"), sem("const"), sem("pads")
        s_edges, s_xlast, s_par, s_gcnw, s_linw = (sem(n) for n in ("edges", "xlast", "par", "gcnw", "linw"))
        s_x = [sem(f"xin{i}") for i in range(4)]
        s_edge_f, s_tmin, s_edge_T, s_tmin_bc, s_span_T = (
            sem(n) for n in ("edge_f", "tmin", "edge_T", "tmin_bc", "span_T"))
        s_dve = sem("dve_chain")
        s_edges_done, s_masks, s_hist, s_degsq, s_dinv = (
            sem(n) for n in ("edges_done", "masks", "hist", "degsq", "dinv"))
        s_par_T, s_params, s_mean, s_sq = (sem(n) for n in ("par_T", "params", "mean", "sq"))
        s_xn, s_xT, s_xTc, s_xw, s_ts, s_thi, s_tlo, s_tT, s_z0 = (
            sem(n) for n in ("xn", "xT", "xTc", "xw", "ts", "thi", "tlo", "tT", "z0"))
        s_hi_masks = sem("hi_masks")
        s_gmax, s_gmax_pe = sem("gmax"), sem("gmax_pe")
        s_t_st = [sem(f"t_st{i}") for i in range(4)]
        s_xs_st = [sem(f"xs_st{i}") for i in range(4)]
        s_dinv_T, s_dinv_Tc, s_dinv_st = (sem(n) for n in ("dinv_T", "dinv_Tc", "dinv_st"))
        s_slot = [sem(f"slot{i}") for i in range(SLOTS)]
        s_idx, s_hold, s_oh, s_msg, s_zadd, s_passb, s_passgo = (
            sem(n) for n in ("idx", "hold", "oh", "msg", "zadd", "passb", "passgo"))
        s_xnT_ld, s_xl, s_xlc = (sem(n) for n in ("xnT_ld", "xl", "xlc"))
        s_w_ld, s_w_bias, s_w_fold, s_w_am, s_w_amT, s_w_amr, s_w_bc, s_w_sc, s_w_hi, s_w_lo, s_w_sc0, s_w_am0, s_lnb, s_brow, s_browT = (
            sem(n) for n in ("w_ld", "w_bias", "w_fold", "w_am", "w_amT", "w_amr", "w_bc", "w_sc", "w_hi", "w_lo",
                             "w_sc0", "w_am0", "lnb", "brow", "browT"))
        s_gathered, s_gate_ld = sem("gathered"), sem("gate_ld")
        s_dbc = {c0: sem(f"dbc{c0}") for c0, c1 in SPANS}
        s_zs, s_tanh, s_gate, s_sig, s_dx, s_dxg, s_mix, s_h = (
            sem(n) for n in ("zs", "tanh", "gate", "sig", "dx", "dxg", "mix", "h"))
        s_bnsq, s_bn = sem("bnsq"), sem("bn")
        s_hn, s_hT, s_x2 = (sem(n) for n in ("hn", "hT", "x2"))
        s_xpad2, s_wr = sem("xpad2"), sem("wr")
        s_var, s_sq1, s_v2, s_sq2 = (sem(n) for n in ("var", "sq1", "v2", "sq2"))
        s_v, s_vT, s_vTc, s_log, s_xhi, s_xlo = (sem(n) for n in ("v", "vT", "vTc", "log", "xhi", "xlo"))
        s_xh_st = [sem(f"xh_st{i}") for i in range(4)]
        s_tri, s_sh, s_exp, s_msum, s_cnt, s_onehots, s_perm, s_routed = (
            sem(n) for n in ("tri", "sh", "exp", "msum", "cnt", "onehots", "perm", "routed"))
        s_b2 = sem("b2")
        s_lanes = sem("lanes")
        s_xg = [sem(f"xg{i}") for i in range(4)]
        s_sc = [sem(f"sc{i}") for i in range(4)]
        s_gcopy, s_xgT, s_xt, s_h1, s_gelu, s_hs, s_y, s_yr = (
            sem(n) for n in ("gcopy", "xgT", "xt", "h1", "gelu", "hs", "y", "yr"))
        s_yload = [sem(f"yload{i}") for i in range(3)]
        s_fin0, s_fin, s_out = sem("fin0"), sem("fin"), sem("out")

        block = ctx.enter_context(nc.Block())
        ds = bass.ds

        def over_tiles(engine, step):
            for t in range(4):
                step(lambda d: t - d, t)
            with engine.Fori(1, NT // 4) as g:
                for i in range(4):
                    step(lambda d: g * 4 + (i - d), i)
            for t in range(NT // 4 * 4, NT + 3):
                step(lambda d: t - d, t % 4)

        def exists(t):
            return not isinstance(t, int) or 0 <= t < NT

        def since(t, n):
            return not isinstance(t, int) or t >= n

        def spread_to(v, n):
            return v.rearrange("p (t a) -> p t a", a=1).to_broadcast([P, PART, n])

        def ring_full(engine, sems):
            for i in range(4):
                engine.wait_ge(sems[i], 16 * ((NT - i + 3) // 4))

        @block.sync
        def _(sp):
            sp.wait_ge(s_pads, 3)
            for rows, v in ((edge_d, dst), (edge_s, src)):
                sp.dma_start(rows[0:FULL, :], v[0:FULL * 4 * P].rearrange("(r c) -> r c", c=4 * P)).then_inc(s_edges, 16)
                sp.dma_start(rows[FULL:FULL + 1, 0:TAIL],
                             v[FULL * 4 * P:EDGES].rearrange("(r c) -> r c", r=1)).then_inc(s_edges, 16)
            for i in range(4):
                sp.dma_start(BR[:, i * XG:(i + 1) * XG, :],
                             x[i * XG * P:(i + 1) * XG * P, :].rearrange("(t p) d -> p t d", p=P)).then_inc(s_x[i], 16)
            sp.dma_start(BR[0:LAST, NT - 1, :], x[(NT - 1) * P:N, :]).then_inc(s_xlast, 16)
            sp.dma_start(gcnW, gcn_W.rearrange("(k p) n -> p k n", p=P)).then_inc(s_gcnw, 16)
            sp.dma_start(linWv, lin_W.rearrange("(k p) n -> p k n", p=P)).then_inc(s_linw, 16)

            def store_tile(t, i):
                sp.wait_ge(s_xTc, t + 1)
                sp.dma_start(xnT_dram[:, :, ds(t * P, P)], XS[i].rearrange("p (k n) -> p k n", k=KD)).then_inc(s_xs_st[i], 16)
                sp.wait_ge(s_tlo, t + 1)
                sp.dma_start(t_dram[ds(t * P, P), :], TH[i]).then_inc(s_t_st[i], 16)
            with sp.Fori(0, NT // 4) as g:
                for i in range(4):
                    store_tile(g * 4 + i, i)
            store_tile(NT - 1, 0)
            sp.wait_ge(s_dinv_Tc, 1)
            sp.dma_start(dinv_dram[:, :], XN[1][0:NT, 0:P]).then_inc(s_dinv_st, 16)
            ring_full(sp, s_xs_st)
            sp.wait_ge(s_xn, NT)
            sp.dma_start(BT, xnT_dram[:, :, :]).then_inc(s_xnT_ld, 16)

            sp.wait_ge(s_xw, NT)
            with sp.Fori(0, E) as e:
                sp.wait_ge(s_w_lo, e + 1)
                sp.dma_start(SW1, W1[ds(e, 1), :, :].rearrange("a (k p) h -> p (a k) h", p=P)).then_inc(s_w_ld, 16)
            with sp.Fori(0, E) as e:
                sp.wait_ge(s_w_lo, e + (E + 1))
                sp.dma_start(S[:].rearrange("p (c d) -> p c d", c=KH),
                             W2[ds(e, 1), :, :].rearrange("a (c p) d -> p (a c) d", p=P)).then_inc(s_w_ld, 16)
            sp.wait_ge(s_w_lo, 2 * E + 1)
            sp.dma_start(gateW, gate_W.rearrange("(k p) n -> p k n", p=P)).then_inc(s_gate_ld, 16)
            sp.wait_ge(s_dinv_st, 16)
            for c0, c1 in SPANS:
                if c0:
                    sp.wait_ge(s_gathered, 1)
                sp.dma_start(dbc(c0, c1), dinv_dram.rearrange("t p -> (t p)")[c0 * CH:c1 * CH]
                             .rearrange("(a n) -> a n", a=1).to_broadcast([P, (c1 - c0) * CH])).then_inc(s_dbc[c0], 16)
            sp.wait_ge(s_h, NCH)
            sp.wait_ge(s_xpad2, 1)
            for i in range(4):
                sp.dma_start(BR[:, i * XG:(i + 1) * XG, :],
                             x[i * XG * P:(i + 1) * XG * P, :].rearrange("(t p) d -> p t d", p=P)).then_inc(s_x[i], 16)
            sp.dma_start(BR[0:LAST, NT - 1, :], x[(NT - 1) * P:N, :]).then_inc(s_xlast, 16)
            sp.dma_start(WrS, Wr.rearrange("(k p) e -> p k e", p=P)).then_inc(s_wr, 16)
            sp.dma_start(brS, br.rearrange("(a e) -> a e", a=1).to_broadcast([P, E])).then_inc(s_wr, 16)
            sp.dma_start(S[:], b2.rearrange("(a e) d -> a (e d)", a=1).to_broadcast([P, E * D])).then_inc(s_b2, 16)

            def store_token(t, i):
                sp.wait_ge(s_xlo, t + 1)
                sp.dma_start(xn_dram[ds(t * P, P), :], XH[i]).then_inc(s_xh_st[i], 16)
            with sp.Fori(0, NT // 4) as g:
                for i in range(4):
                    store_token(g * 4 + i, i)
            store_token(NT - 1, 0)

            for i in range(4):
                sp.wait_ge(s_sc[i], 16 * NB)

            def load_y(g, i):
                sp.dma_start(FIN[i], y_dram[ds(g * 8 * P, 8 * P), :].rearrange("(t p k) d -> p t k d", p=P, k=2)
                             ).then_inc(s_yload[i], 16)

            def store_out(g):
                sp.wait_ge(s_fin, g * 4 + 4)
                sp.dma_start(out[ds(g * 4 * P, 4 * P), :].rearrange("(t p) d -> p t d", p=P),
                             BR[:, ds(g * 4, 4), :]).then_inc(s_out, 16)
            for g in range(3):
                load_y(g, g)
            for g in range(NT // 4):
                store_out(g)
                if g + 3 < NT // 4:
                    load_y(g + 3, g % 3)
                elif g + 3 == NT // 4:
                    sp.dma_start(FIN[g % 3][0:LAST, 0, :, :], y_dram[(NT - 1) * 2 * P:(NT - 1) * 2 * P + 2 * LAST, :]
                                 .rearrange("(p k) d -> p k d", k=2)).then_inc(s_yload[g % 3], 16)
            sp.wait_ge(s_fin, NT)
            sp.dma_start(out[(NT - 1) * P:N, :], BR[0:LAST, NT - 1, :]).then_inc(s_out, 16)
            sp.wait_ge(s_out, 16 * (NT // 4 + 1))
            ring_full(sp, s_t_st)

        @block.gpsimd
        def _(pool):
            pool.memset(edge_d, N).then_inc(s_pads, 1)
            pool.memset(edge_s, N).then_inc(s_pads, 1)
            pool.memset(BR[:, NT - 1, :], 0.0).then_inc(s_pads, 1)
            pool.memset(ident[:], 0.0).then_inc(s_const0, 1)
            pool.memset(ones[:], 1.0).then_inc(s_const, 1)
            pool.memset(epst, EPS).then_inc(s_const, 1)
            pool.iota(iota[:], pattern=[[1, P]], base=0, channel_multiplier=0,
                      allow_small_or_imprecise_dtypes=True).then_inc(s_const, 1)
            pool.iota(iota_w[:], pattern=[[1, WINDOW]], base=0, channel_multiplier=0,
                      allow_small_or_imprecise_dtypes=True).then_inc(s_const, 1)
            pool.iota(iota_p, pattern=[[1, 1]], base=0, channel_multiplier=1,
                      allow_small_or_imprecise_dtypes=True).then_inc(s_const, 1)
            pool.wait_ge(s_const0, 1)
            pool.affine_select(out=ident[:], in_=ident[:], compare_op=ALU.not_equal, fill=1.0, base=0,
                               pattern=[[-1, P]], channel_multiplier=1).then_inc(s_const, 1)

            pool.wait_ge(s_edges_done, 1)
            for j in range(HIGH_POOL):
                last = pool.tensor_scalar(mask_hi[:, j, :], hi16, float(j), None, ALU.is_equal)
            last.then_inc(s_hi_masks, 1)

            ring_full(pool, s_t_st)
            pool.wait_ge(s_edges_done, 2)
            pool.wait_ge(s_tT, NT)
            pool.wait_ge(s_dinv_st, 16)
            ring_full(pool, s_xs_st)

            def gather_body(n0, round0):
                for r in range(2):
                    pool.wait_ge(s_idx, round0 + (r + 1))
                    for j in range(SLOTS):
                        pool.wait_ge(s_msg, n0 + (r * SLOTS + j + 1))
                        pool.sem_inc(s_hold, 1)
                        pool.indirect_dma_start(
                            out=RS[:, j, :].bitcast(F16), out_offset=None, in_=t_dram[:, :],
                            in_offset=bass.IndirectOffsetOnAxis(ap=idx_ring[:, r * SLOTS + j:r * SLOTS + j + 1], axis=0),
                        ).then_inc(s_slot[j], 16)

            with pool.Fori(0, 2 * E) as b:
                gather_body(b * BODY, b * 2)
            pool.wait_ge(s_edges_done, 2)
            npass = pool.value_load(npass_i[:, 2:3], min_val=1, max_val=NPAD // WINDOW)
            with pool.If(npass > 1):
                with pool.Fori(1, npass) as w:
                    with pool.Fori(0, 2 * E) as b:
                        gather_body(w * ET + b * BODY, w * (4 * E + 1) + b * 2)

            pool.wait_ge(s_xlc, KD * NCH)
            for c in range(NCH):
                z = AT[:, :, c * CH:(c + 1) * CH]
                pool.wait_ge(s_tanh, c + 1)
                pool.wait_ge(s_gate, c + 1)
                pool.tensor_tensor(z, z, BT[:, :, c * CH:(c + 1) * CH], ALU.subtract).then_inc(s_dx, 1)
            pool.wait_ge(s_h, NCH)
            pool.memset(BR[:, NT - 1, :], 0.0).then_inc(s_xpad2, 1)
            pool.wait_ge(s_hn, NT)
            pool.affine_select(out=tri, in_=ones[:], compare_op=ALU.is_gt, fill=0.0, base=0,
                               pattern=[[1, P]], channel_multiplier=-1).then_inc(s_tri, 1)
            pool.affine_select(out=valid, in_=ones[:, 0:NT], compare_op=ALU.is_ge, fill=0.0, base=N - 1,
                               pattern=[[-P, NT]], channel_multiplier=-1).then_inc(s_tri, 1)
            slot_id = A[:, 21 * 256 + 64:21 * 256 + 64 + SC]
            pool.iota(slot_id, pattern=[[P, SC]], base=DUMP, channel_multiplier=1,
                      allow_small_or_imprecise_dtypes=True).then_inc(s_tri, 1)

            pool.iota(iota16, pattern=[[1, P]], base=0, channel_multiplier=0,
                      allow_small_or_imprecise_dtypes=True).then_inc(s_tri, 1)

            pool.wait_ge(s_tri, 4)
            pool.wait_ge(s_lanes, 1)
            ring_full(pool, s_xh_st)
            for c in range(LO_DVE, 2 * NT // PART):
                for n in range(c * PART, (c + 1) * PART):
                    last = pool.tensor_scalar(LO[:, n, :], iota16, lane[:, n:n + 1], None, ALU.is_equal)
                last.then_inc(s_lanes, 1)

            pool.wait_ge(s_routed, 1)
            ring_full(pool, s_xh_st)

            def gather_x(n, i, count, first):
                if not first:
                    pool.wait_ge(s_xgT, n - 1)
                pool.tensor_copy(gi[:, 2 * i:2 * i + 2], gidx[:, ds(n * 2, 2)]).then_inc(s_gcopy, 1)
                pool.wait_ge(s_gcopy, count)
                pool.sem_inc(s_hold, 1)
                for h in range(2):
                    j = 2 * i + h
                    pool.indirect_dma_start(out=XGr[j], out_offset=None, in_=xn_dram[:, :],
                                            in_offset=bass.IndirectOffsetOnAxis(ap=gi[:, j:j + 1], axis=0)
                                            ).then_inc(s_xg[j], 16)

            def scatter_y(n, b, i, count, first):
                if not first:
                    for h in range(2):
                        pool.wait_ge(s_sc[2 * i + h], b * 16)
                pool.tensor_copy(si[:, 2 * i:2 * i + 2], sidx[:, ds(n * 2, 2)]).then_inc(s_gcopy, 1)
                pool.wait_ge(s_gcopy, count)
                for h in range(2):
                    j = 2 * i + h
                    pool.wait_ge(s_yr, n * 2 + h + 1)
                    pool.sem_inc(s_hold, 1)
                    pool.indirect_dma_start(out=y_dram[:, :],
                                            out_offset=bass.IndirectOffsetOnAxis(ap=si[:, j:j + 1], axis=0),
                                            in_=Y[j], in_offset=None).then_inc(s_sc[j], 16)

            def turn(b, first, gathers):
                for i in range(U):
                    n = b * U + i
                    if i < gathers:
                        gather_x(n + 3, 1 - i, n * 2 + 4, False)
                        scatter_y(n, b, i, n * 2 + 5, first)
                    else:
                        scatter_y(n, b, i, n + ST + 1, first)
            for n in range(3):
                gather_x(n, n % 2, n + 1, n < 2)
            turn(0, True, U)
            with pool.Fori(1, NB - 2) as b:
                turn(b, False, U)
            turn(NB - 2, False, U - 1)
            turn(NB - 1, False, 0)

        @block.scalar
        def _(act):
            rows = [(b1.rearrange("e (c p) -> (e c) p", p=P), E * KH), (ln_g.rearrange("e (k p) -> (e k) p", p=P), E * KD),
                    (ln_b.rearrange("e (k p) -> (e k) p", p=P), E * KD)]
            rows += [(v.rearrange("(k p) -> k p", p=P), KD) for v in (gcn_b, lin_b, gate_b, bn_gamma, bn_beta)]
            r0 = 0
            for v, n in rows:
                act.dma_start(prow[r0:r0 + n, :], v).then_inc(s_par, 16)
                r0 += n
            act.wait_ge(s_mean, 1)
            act.activation(nst[:, 3, :], nst[:, 2, :], ACT.Sqrt, bias=epst, scale=1.0 / D).then_inc(s_sq, 1)
            act.wait_ge(s_hist, 1)
            for h in range(2):
                last = act.activation(nst[h * LOW:(h + 1) * LOW, 4, :],
                                      Q[3][0:LOW, 0:HIGH].rearrange("p (t h) -> p h t", h=2)[:, h, :], ACT.Sqrt,
                                      bias=ones[0:LOW, 0:1])
            last.then_inc(s_degsq, 1)
            act.wait_ge(s_edges_done, 2)
            act.wait_ge(s_span_T, 1)

            def x_step(tile, s):
                t = tile(0)
                if exists(t):
                    act.wait_ge(s_xT, t + 1)
                    if since(t, 4):
                        act.wait_ge(s_xs_st[s], (t - s) * 4)
                        act.wait_ge(s_xw, t - 3)
                    act.activation(XS[s], Q[s % 2][:, 0:D], ACT.Copy).then_inc(s_xTc, 1)
                t, i = tile(1), (s - 1) % 2
                if exists(t):
                    if not since(t, 1):
                        act.wait_ge(s_dinv, 1)
                    act.wait_ge(s_xw, t + 1)
                    if since(t, 2):
                        act.wait_ge(s_tT, t - 1)
                        act.wait_ge(s_tlo, t - 1)
                    act.activation(TS[i], PA[i][:, 0:D], ACT.Copy, scale=nst[:, 5, ds(t, 1)]).then_inc(s_ts, 1)
                t, i = tile(2), (s - 2) % 4
                if exists(t):
                    if since(t, 4):
                        act.wait_ge(s_t_st[i], (t - i) * 4)
                    act.wait_ge(s_ts, t + 1)
                    act.activation(TH[i][:, 0:D], TS[i % 2], ACT.Copy).then_inc(s_thi, 1)
            over_tiles(act, x_step)

            act.wait_ge(s_params, 1)
            with act.Fori(0, E) as e:
                act.wait_ge(s_xl, e * 2 + 2)
                for m in range(KD):
                    act.activation(BT[:, m, ds(e * CH, CH)], Q[3 - 3 * m][:, 0:CH], ACT.Identity,
                                   bias=params[:, CV + KD + m:CV + KD + m + 1]).then_inc(s_xlc, 1)
                for h in range(2):
                    act.wait_ge(s_w_bias, e * 2 + h + 1)
                    act.activation(brow[:, h * 512:(h + 1) * 512], Q[3 - 3 * h][0:1, :], ACT.Copy).then_inc(s_brow, 1)
                for kk in range(KD):
                    act.activation(SW1[:, kk, :], SW1[:, kk, :], ACT.Copy,
                                   scale=params[:, ds(e * KD + (CG + kk), 1)]).then_inc(s_w_fold, 1)
                act.wait_ge(s_w_sc, e + 1)
                act.activation(W1hi[:, ds(e, 1), :, :].rearrange("p a k h -> p (a k h)"), S[:], ACT.Copy,
                               scale=wsc).then_inc(s_w_hi, 1)
            with act.Fori(0, E) as e:
                act.wait_ge(s_w_sc, e + (E + 1))
                act.activation(W2hi[:, ds(e, 1), :, :].rearrange("p a c d -> p (a c d)"), S[:], ACT.Copy,
                               scale=wsc).then_inc(s_w_hi, 1)

            for c in range(NCH + 4):
                if c < NCH:
                    act.wait_ge(s_zs, c + 1)
                    for m in range(KD):
                        z = AT[:, m, c * CH:(c + 1) * CH]
                        last = act.activation(z, z, ACT.Tanh, bias=params[:, CV + m:CV + m + 1], scale=zinv)
                    last.then_inc(s_tanh, 1)
                if 0 <= c - 2 < NCH:
                    act.wait_ge(s_gate, c - 2 + 1)
                    for m in range(KD):
                        g = GATE[(c - 2) % 3][m][:, 0:CH]
                        last = act.activation(g, g, ACT.Tanh, bias=halfb[:, m:m + 1], scale=0.5)
                    last.then_inc(s_sig, 1)
                if 0 <= c - 4 < NCH:
                    h = AT[:, :, (c - 4) * CH:(c - 3) * CH]
                    act.wait_ge(s_mix, c - 4 + 1)
                    act.activation(h, h, ACT.Relu).then_inc(s_h, 1)
            act.wait_ge(s_bnsq, 1)
            act.activation(bsq, bmv[:, :, 1:2].rearrange("p k a -> p (k a)"), ACT.Sqrt, bias=epst).then_inc(s_bnsq, 1)
            act.wait_ge(s_bn, 1)

            def norm_tile(t, i, first):
                if not first:
                    act.wait_ge(s_hT, t - 1)
                for m in range(KD):
                    last = act.activation(HN[i][:, m * P:(m + 1) * P], AT[:, m, ds(t * P, P)], ACT.Identity,
                                          bias=bbi[:, m:m + 1], scale=bsc[:, m:m + 1])
                last.then_inc(s_hn, 1)
            for i in range(2):
                norm_tile(i, i, True)
            with act.Fori(1, NT // 2) as g:
                for i in range(2):
                    norm_tile(g * 2 + i, i, False)
            norm_tile(NT - 1, 0, False)
            act.wait_ge(s_var, 1)
            act.activation(nst[:, 3, :], nst[:, 2, :], ACT.Sqrt, bias=epst, scale=1.0 / D).then_inc(s_sq1, 1)
            act.wait_ge(s_v2, 1)
            act.activation(nst[:, 5, :], nst[:, 4, :], ACT.Sqrt, bias=epst, scale=1.0 / D).then_inc(s_sq2, 1)

            def token_step(tile, s):
                t, i = tile(0), s % 2
                if exists(t):
                    act.wait_ge(s_v, t + 1)
                    if since(t, 4):
                        act.wait_ge(s_xh_st[s], (t - s) * 4)
                    act.activation(XH[s][:, 0:D], V[i], ACT.Copy).then_inc(s_xhi, 1)
                    act.wait_ge(s_vT, t + 1)
                    if since(t, 2):
                        act.wait_ge(s_log, t - 1)
                    act.activation(VT[i], PA[i][:, 0:D], ACT.Copy).then_inc(s_vTc, 1)
            over_tiles(act, token_step)
            act.wait_ge(s_sh, 1)
            act.activation(rt(1), rt(1), ACT.Exp).then_inc(s_exp, 1)

            act.activation(halfb, halfb, ACT.Gelu)
            act.wait_ge(s_routed, 1)

            def turn(b, first):
                for i in range(U):
                    n = b * U + i
                    e = act.value_load(exp_i[0:1, ds(n, 1)], min_val=0, max_val=E - 1)
                    act.wait_ge(s_xgT, n + 1)
                    if not first:
                        act.wait_ge(s_h1, (n - 1) * 4)
                    act.activation(XT16[i].rearrange("p v k t -> p (v k t)"), P16[:], ACT.Copy).then_inc(s_xt, 1)
                    for c in range(KH):
                        if c % 2 == 0:
                            act.wait_ge(s_h1, n * 4 + (c // 2 + 1))
                        if c % 4 == 0 and not (first and i == 0):
                            act.wait_ge(s_hs, n * 4 + (c // 2 - 2))
                        act.activation(HF[:, c * SLOT_ROWS:(c + 1) * SLOT_ROWS], PH[:, c * SLOT_ROWS:(c + 1) * SLOT_ROWS],
                                       ACT.Gelu, bias=params[:, ds(e * KH + c, 1)],
                                       scale=sc1[:, ds(e, 1)]).then_inc(s_gelu, 1)
            turn(0, True)
            with act.Fori(1, NB) as b:
                turn(b, False)

        @block.tensor
        def _(pe):
            pe.wait_ge(s_const, 6)
            pe.wait_ge(s_edge_f, 2)
            for k, rows in enumerate((edge_df, edge_sf)):
                for c in range(4):
                    last = pe.transpose(Q[k][:, c * ROWS:(c + 1) * ROWS], rows[0:ROWS, c * P:(c + 1) * P],
                                        ident[0:ROWS, 0:ROWS])
                last.then_inc(s_edge_T, 1)
            pe.wait_ge(s_tmin, 5)
            for c in range(4):
                last = pe.matmul(Q[2][:, c * ROWS:(c + 1) * ROWS], tmin_w[0:ROWS, c * P:(c + 1) * P],
                                 ident[0:ROWS, 0:ROWS], start=True, stop=True)
            last.then_inc(s_tmin_bc, 1)
            pe.transpose(PB[0:1, SPAN0:SPAN0 + ROWS], tspan[0:ROWS, :], ident[0:ROWS, 0:ROWS]).then_inc(s_span_T, 1)
            pe.wait_ge(s_par, 16 * 8)
            pe.transpose(PB[:, 0:PROWS], prow[0:PROWS, :], ident[0:PROWS, 0:PROWS]).then_inc(s_par_T, 1)

            pe.wait_ge(s_gmax, 1)
            pe.transpose(PA[0][0:1, 0:P], wam, ident[:]).then_inc(s_gmax_pe, 1)

            pe.wait_ge(s_masks, 1)
            pe.wait_ge(s_hi_masks, 1)
            for t in range(ET):
                mm = pe.matmul(Q[3][0:LOW, 0:HIGH], mask_lo[:, :, t], mask_hi[:, :, t], start=(t == 0), stop=(t == ET - 1))
            mm.then_inc(s_hist, 1)
            pe.wait_ge(s_gmax, 2)
            pe.matmul(PB[:, 256:257], ones[0:1, :], wamr[0:1, :], start=True, stop=True).then_inc(s_gmax_pe, 1)

            pe.wait_ge(s_gcnw, 16)

            def x_step(tile, s):
                t, i = tile(0), s % 2
                if exists(t):
                    pe.wait_ge(s_xn, t + 1)
                    if since(t, 2):
                        pe.wait_ge(s_xTc, t - 1)
                    for k in range(KD):
                        last = pe.transpose(Q[i][:, k * P:(k + 1) * P], XN[i][:, k * P:(k + 1) * P], ident[:])
                    last.then_inc(s_xT, 1)
                t, i = tile(1), (s - 1) % 4
                if exists(t):
                    pe.wait_ge(s_xTc, t + 1)
                    if since(t, 2):
                        pe.wait_ge(s_ts, t - 1)
                    for k in range(KD):
                        last = pe.matmul(PA[i % 2][:, 0:D], XS[i][:, k * P:(k + 1) * P], gcnW[:, k, :],
                                         start=(k == 0), stop=(k == KD - 1))
                    last.then_inc(s_xw, 1)
                t, i = tile(2), s % 2
                if exists(t):
                    pe.wait_ge(s_ts, t + 1)
                    if since(t, 2):
                        pe.wait_ge(s_z0, t - 1)
                    for k in range(KD):
                        last = pe.transpose(Q[2 + i][:, k * P:(k + 1) * P], TS[i][:, k * P:(k + 1) * P], ident[:])
                    last.then_inc(s_tT, 1)
            over_tiles(pe, x_step)
            pe.transpose(PB[0:NT, 128:256], dinv[:], ident[:]).then_inc(s_dinv_T, 1)
            pe.wait_ge(s_z0, NT)

            def sums(n0, round0, step=None):
                for k in range(BODY):
                    if step:
                        step(k)
                    r, j = divmod(k, SLOTS)
                    pe.wait_ge(s_slot[j], (round0 + r + 1) * 16)
                    pe.wait_ge(s_oh, n0 + (k + 1))
                    pe.wait_ge(s_zadd, n0 + (k + (3 if k < BODY % 4 else 1)))
                    for m in range(KD):
                        for v in range(2):
                            last = pe.matmul(MS[k % 4][:, m * WINDOW:(m + 1) * WINDOW],
                                             RS[:, j, :].bitcast(F16)[:, v * D + m * P:v * D + (m + 1) * P],
                                             oh[:, k % OH, :], start=(v == 0), stop=(v == 1))
                    last.then_inc(s_msg, 1)

            pe.sem_inc(s_msg, SLOTS)
            pe.wait_ge(s_linw, 16)
            pe.wait_ge(s_xnT_ld, 16)
            pe.wait_ge(s_params, 1)

            def top(u):
                pe.wait_ge(s_w_am, u + 1)
                pe.transpose(PB[0:1, 128:256], wam, ident[:]).then_inc(s_w_amT, 1)

            def spread(u):
                pe.wait_ge(s_w_amr, u + 1)
                pe.matmul(PB[:, 256:257], ones[0:1, :], wamr[0:1, :], start=True, stop=True).then_inc(s_w_bc, 1)
            with pe.Fori(0, E) as e:
                def step(k):
                    if k in (2, 4):
                        m = k // 4
                        for kk in range(KD):
                            last = pe.matmul(Q[3 - 3 * m][:, 0:CH], linWv[:, kk, m * P:(m + 1) * P],
                                             BT[:, kk, ds(e * CH, CH)], start=(kk == 0), stop=(kk == KD - 1))
                        last.then_inc(s_xl, 1)
                    if k in (7, 9):
                        h = k // 9
                        if not h:
                            pe.wait_ge(s_w_ld, (e + 1) * 16)
                            pe.wait_ge(s_lnb, e + 1)
                        pe.wait_ge(s_xlc, e * 2 + h + 1)
                        for kk in range(KD):
                            last = pe.matmul(Q[3 - 3 * h][0:1, :], lnb[:, kk:kk + 1],
                                             SW1[:, kk, h * 512:(h + 1) * 512], start=(kk == 0), stop=(kk == KD - 1))
                        last.then_inc(s_w_bias, 1)
                    if k == 12:
                        pe.wait_ge(s_brow, e * 2 + 2)
                        for c in range(KH):
                            last = pe.matmul(PB[:, c:c + 1], brow[:, c * P:(c + 1) * P], ones[0:1, 0:1],
                                             start=True, stop=True)
                        last.then_inc(s_browT, 1)
                    if k == 17:
                        top(e)
                    if k == 20:
                        spread(e)
                sums(e * BODY, e * 2, step)
            with pe.Fori(0, E) as e:
                def step(k):
                    if k == 9:
                        top(e + E)
                    if k == 12:
                        spread(e + E)
                sums(e * BODY + E * BODY, e * 2 + 2 * E, step)
            npass = pe.value_load(npass_i[:, 2:3], min_val=1, max_val=NPAD // WINDOW)
            with pe.If(npass > 1):
                with pe.Fori(1, npass) as w:
                    with pe.Fori(0, 2 * E) as b:
                        sums(w * ET + b * BODY, w * (4 * E) + b * 2)

            pe.wait_ge(s_gate_ld, 16)

            for c in range(NCH):
                pe.wait_ge(s_tanh, c + 1)
                if c >= 3:
                    pe.wait_ge(s_dxg, c - 2)
                for m in range(KD):
                    for k in range(KD):
                        last = pe.matmul(GATE[c % 3][m][:, 0:CH], gateW[:, k, m * P:(m + 1) * P],
                                         AT[:, k, c * CH:(c + 1) * CH], start=(k == 0), stop=(k == KD - 1))
                last.then_inc(s_gate, 1)

            def rows_of(t, i, first):
                pe.wait_ge(s_hn, t + 1)
                if not first:
                    pe.wait_ge(s_x2, t - 1)
                for k in range(KD):
                    last = pe.transpose(PA[i][:, k * P:(k + 1) * P], HN[i][:, k * P:(k + 1) * P], ident[:])
                last.then_inc(s_hT, 1)
            for i in range(2):
                rows_of(i, i, True)
            with pe.Fori(1, NT // 2) as g:
                for i in range(2):
                    rows_of(g * 2 + i, i, False)
            rows_of(NT - 1, 0, False)

            pe.wait_ge(s_wr, 32)

            def token_step(tile, s):
                t, i = tile(0), s % 2
                if exists(t):
                    pe.wait_ge(s_v, t + 1)
                    if since(t, 2):
                        pe.wait_ge(s_vTc, t - 1)
                    for k in range(KD):
                        last = pe.transpose(PA[i][:, k * P:(k + 1) * P], V[i][:, k * P:(k + 1) * P], ident[:])
                    last.then_inc(s_vT, 1)
                t, i = tile(1), (s - 1) % 2
                if exists(t):
                    pe.wait_ge(s_vTc, t + 1)
                    for k in range(KD):
                        last = pe.matmul(PB[:, ds(t * E, E)], VT[i][:, k * P:(k + 1) * P], WrS[:, k, :],
                                         start=(k == 0), stop=(k == KD - 1))
                    last.then_inc(s_log, 1)
            pe.wait_ge(s_x2, NT)
            over_tiles(pe, token_step)

            pe.wait_ge(s_msum, 1)
            pe.wait_ge(s_tri, 4)
            pe.matmul(Q[0][:, 0:NE], tri, rt(6).rearrange("p t e -> p (t e)"), start=True, stop=True)
            pe.matmul(Q[1][:, 0:NE], ones[:], rt(6).rearrange("p t e -> p (t e)"), start=True, stop=True).then_inc(s_cnt, 1)

            for n in range(2 * NT):
                if n % PART == 0:
                    pe.wait_ge(s_onehots, n // PART + 1)
                    if n // PART >= LO_DVE:
                        pe.wait_ge(s_lanes, 2 + n // PART - LO_DVE)
                mm = pe.matmul(Q[2][:, 0:2 * SC].rearrange("p (v t) -> p v t", v=2), LO[:, n, :], V2[:, :, n, :],
                               start=(n == 0), stop=(n == 2 * NT - 1))
            mm.then_inc(s_perm, 1)

            pe.wait_ge(s_routed, 1)

            def tokens_T(n, b, i, first):
                for h in range(2):
                    pe.wait_ge(s_xg[2 * i + h], (b + 1) * 16)
                if not first:
                    pe.wait_ge(s_xt, n)
                for h in range(2):
                    for q in range(4):
                        last = pe.transpose(P16[:, q * SLOT_ROWS + h * P:q * SLOT_ROWS + (h + 1) * P],
                                            XGr[2 * i + h][:, q * P:(q + 1) * P], ident16[:])
                last.then_inc(s_xgT, 1)

            def up(n, e, i, first):
                pe.wait_ge(s_xt, n + 1)
                for c in range(KH):
                    if not first and c % 2 == 0:
                        pe.wait_ge(s_gelu, (n - 1) * KH + (c + 2))
                    q = 0
                    for k in range(KD):
                        for w, v in ((W1hi, 0), (W1hi, 1), (W1lo, 0)):
                            last = pe.matmul(PH[:, c * SLOT_ROWS:(c + 1) * SLOT_ROWS],
                                             w[:, ds(e, 1), k, c * P:(c + 1) * P].rearrange("p a h -> p (a h)"),
                                             XT16[i][:, v, k, :], start=(q == 0), stop=(q == 3 * KD - 1))
                            q += 1
                    if c % 2 == 1:
                        last.then_inc(s_h1, 1)

            def down(n, e, first):
                if not first:
                    pe.wait_ge(s_yr, n * 2)
                for half in range(2):
                    pe.wait_ge(s_hs, n * 4 + 2 * (half + 1))
                    for c in range(half * KH // 2, (half + 1) * KH // 2):
                        for hv, w in ((HHI, W2hi), (HHI, W2lo), (HLO, W2hi)):
                            for h in range(2):
                                last = pe.matmul(PA[h][:, 0:D], hv[:, c * SLOT_ROWS + h * P:c * SLOT_ROWS + (h + 1) * P],
                                                 w[:, ds(e, 1), c, :].rearrange("p a d -> p (a d)"),
                                                 start=(c == 0 and w is W2hi and hv is HHI),
                                                 stop=(c == KH - 1 and hv is HLO))
                    last.then_inc(s_y, 1)

            def expert(n):
                return pe.value_load(exp_i[0:1, ds(n, 1)], min_val=0, max_val=E - 1)

            def turn(b, first, last):
                before = None if first else expert(b * U - 1)
                es = [expert(b * U + i) for i in range(U)]
                for i in range(U):
                    n = b * U + i
                    if not (last and i == U - 1):
                        tokens_T(n + 1, b if i < U - 1 else b + 1, 1 - i, False)
                    up(n, es[i], i, first and i == 0)
                    if i or not first:
                        down(n - 1, es[i - 1] if i else before, first)
            tokens_T(0, 0, 0, True)
            turn(0, True, False)
            with pe.Fori(1, NB - 1) as b:
                turn(b, False, False)
            turn(NB - 1, False, True)
            down(ST - 1, expert(ST - 1), False)

        @block.vector
        def _(dve):
            made = [0]

            def link(ins):
                made[0] += 1
                ins.then_inc(s_dve, 1)
                dve.wait_ge(s_dve, made[0])

            dve.wait_ge(s_edges, 64)
            dve.tensor_copy(edge_df[0:ROWS, :], edge_d[0:ROWS, :]).then_inc(s_edge_f, 1)
            dve.tensor_copy(edge_sf[0:ROWS, :], edge_s[0:ROWS, :]).then_inc(s_edge_f, 1)
            dve.wait_ge(s_edge_f, 2)
            dve.wait_ge(s_const, 6)
            edv = edge_df[0:ROWS, :].rearrange("r (c p) -> r c p", c=4)
            dve.tensor_reduce(tmin[0:ROWS, :], edv, AX, ALU.min)
            link(dve.tensor_reduce(tmax[0:ROWS, :], edv, AX, ALU.max))

            def tiles_of(v):
                return v.rearrange("p (q c) -> p q c", c=4)

            def rows4(q):
                return q[:, 0:ET].rearrange("p (c q) -> p q c", c=4)

            dve.wait_ge(s_edge_T, 1)
            link(dve.tensor_copy(tiles_of(dst_f), rows4(Q[0])))
            link(dve.tensor_copy(dst_i, dst_f))
            link(dve.tensor_scalar(lohi_i, dst_i, LOW - 1, None, ALU.bitwise_and))
            link(dve.tensor_copy(lo16, lohi_i))
            link(dve.tensor_scalar(lohi_i, dst_i, LOW.bit_length() - 1, None, ALU.arith_shift_right))
            link(dve.tensor_copy(hi16, lohi_i))
            dve.sem_inc(s_edges_done, 1)

            def combine(sv):
                m_e, q_e, m_o, q_o = (sv[:, :, v:v + 1].rearrange("p t a -> p (t a)") for v in (1, 2, 4, 5))
                dve.tensor_tensor(nst[:, 0, :], m_e, m_o, ALU.add)
                dve.tensor_tensor(nst[:, 2, :], q_e, q_o, ALU.add)
                link(dve.tensor_tensor(nst[:, 1, :], m_e, m_o, ALU.subtract))
                link(dve.tensor_tensor(nst[:, 1, :], nst[:, 1, :], nst[:, 1, :], ALU.mult))
                dve.tensor_scalar(nst[:, 0, :], nst[:, 0, :], 0.5, None, ALU.mult)
                return dve.scalar_tensor_tensor(out=nst[:, 2, :], in0=nst[:, 1, :], scalar=D / 4.0, in1=nst[:, 2, :],
                                                op0=ALU.mult, op1=ALU.add)

            for j in range(LOW):
                dve.tensor_scalar(mask_lo[:, j, :], lo16, float(j), None, ALU.is_equal)
            for c in range(4):
                dve.tensor_scalar(tmin_w[0:ROWS, c * P:(c + 1) * P], ones[0:ROWS, :], tmin[0:ROWS, c:c + 1], None,
                                  ALU.mult).then_inc(s_tmin, 1)
            link(dve.tensor_tensor(tdif[0:ROWS, :], tmax[0:ROWS, :], tmin[0:ROWS, :], ALU.subtract))
            dve.tensor_reduce(tspan[0:ROWS, :], tdif[0:ROWS, :], AX, ALU.max).then_inc(s_tmin, 1)
            dve.wait_ge(s_gcnw, 16)
            dve.tensor_reduce(wam, S[:, 0:KD * D], AX, ALU.max, apply_absolute_value=True).then_inc(s_gmax, 1)
            for j in range(HIGH_POOL, HIGH):
                last = dve.tensor_scalar(mask_hi[:, j, :], hi16, float(j), None, ALU.is_equal)
            last.then_inc(s_masks, 1)
            dve.wait_ge(s_edge_T, 2)
            dve.tensor_copy(tiles_of(src_i[:, 0:ET]), rows4(Q[1]))
            dve.memset(src_i[:, ET:ET + SLOTS], 0)
            dve.wait_ge(s_par_T, 1)
            dve.wait_ge(s_tmin_bc, 1)
            dve.tensor_tensor(tiles_of(dst_rel[:]), tiles_of(dst_f), rows4(Q[2]), ALU.subtract)
            link(dve.tensor_scalar(tiles_of(base_f), rows4(Q[2])[0:1], float(NPAD - WINDOW), None, ALU.min))
            dve.tensor_copy(base_i[:, :, 0:BODY], base_f.rearrange("p (b k) -> p b k", b=2 * E))
            link(dve.tensor_reduce(npass_f, PB[0:1, SPAN0:SPAN0 + ROWS], AX, ALU.max))
            link(dve.tensor_copy(npass_i[:, 0:1], npass_f))
            link(dve.tensor_scalar(npass_i[:, 1:2], npass_i[:, 0:1], WINDOW.bit_length() - 1, None, ALU.arith_shift_right))
            link(dve.tensor_scalar(npass_i[:, 2:3], npass_i[:, 1:2], 1.0, None, ALU.add))
            link(dve.tensor_copy(params[:], PB[:, 0:PROWS]))
            dve.tensor_scalar(halfb, params[:, CV + 2 * KD:CV + 3 * KD], 0.5, None, ALU.mult).then_inc(s_params, 1)
            dve.tensor_copy(ident16[:], ident[:])
            dve.sem_inc(s_edges_done, 1)
            dve.wait_ge(s_gmax_pe, 1)
            dve.tensor_reduce(wamr[0:1, :], PA[0][0:1, 0:P], AX, ALU.max).then_inc(s_gmax, 1)
            for t in range(NT):
                if t % XG == 0:
                    dve.wait_ge(s_x[t // XG] if t < 4 * XG else s_xlast, 16)
                last = dve.bn_stats(svx[:, t, :], BR[:, t, :])
            link(last)
            combine(svx).then_inc(s_mean, 1)
            dve.wait_ge(s_gmax_pe, 2)
            link(dve.tensor_scalar(wmax, PB[:, 256:257], 1e-30, None, ALU.max))
            link(dve.tensor_scalar(wp2.bitcast(I32), wmax.bitcast(I32), EXPONENT, None, ALU.bitwise_and))
            link(dve.reciprocal(zsc, wp2))
            dve.tensor_scalar(zinv, wp2, (2 * D) / 2.0 ** 15, None, ALU.mult)
            link(dve.tensor_scalar(zsc, zsc, 2.0 ** 15 / (2 * D), None, ALU.mult))
            dve.wait_ge(s_sq, 1)
            dve.reciprocal(nst[:, 6, :], nst[:, 3, :]).then_inc(s_sq, 1)
            dve.wait_ge(s_sq, 2)

            def x_step(tile, s):
                t, i = tile(0), s % 2
                if isinstance(t, int) and t == 2:
                    dve.wait_ge(s_degsq, 1)
                    link(dve.reciprocal(dinv[:], nst[:, 4, :]))
                    dve.tensor_scalar(nst[:, 5, :], dinv[:], zsc, None, ALU.mult).then_inc(s_dinv, 1)
                if exists(t):
                    if since(t, 2):
                        dve.wait_ge(s_xT, t - 1)
                    dve.tensor_scalar(XN[i], BR[:, ds(t, 1), :].rearrange("p a d -> p (a d)"), nst[:, 0, ds(t, 1)],
                                      nst[:, 6, ds(t, 1)], ALU.subtract, ALU.mult).then_inc(s_xn, 1)
                t, i = tile(3), (s - 3) % 4
                if exists(t):
                    dve.wait_ge(s_thi, t + 1)
                    dve.tensor_tensor(TH[i][:, D:2 * D], TS[i % 2], TH[i][:, 0:D], ALU.subtract).then_inc(s_tlo, 1)
                    dve.wait_ge(s_tT, t + 1)
                    dve.tensor_copy(AT[:, :, ds(t * P, P)],
                                    Q[2 + i % 2][:, 0:D].rearrange("p (k n) -> p k n", k=KD)).then_inc(s_z0, 1)
            over_tiles(dve, x_step)
            dve.wait_ge(s_dinv_T, 1)
            dve.wait_ge(s_xT, NT)
            dve.tensor_copy(XN[1][0:NT, 0:P], PB[0:NT, 128:256]).then_inc(s_dinv_Tc, 1)

            def onehot(n0, c0, k):
                dve.wait_ge(s_msg, n0 + (SLOTS - OH + 1 + k))
                dve.tensor_scalar(oh[:, k % OH, :], iota_w[:], dst_rel[:, ds(c0 + k, 1)], None, ALU.is_equal).then_inc(s_oh, 1)

            def add(n0, base, k):
                dve.wait_ge(s_msg, n0 + (SLOTS + k + 1))
                dve.wait_ge(s_zadd, n0 + (k + 4))
                z = AT[:, :, ds(base, WINDOW)]
                dve.tensor_tensor(z, z, MS[k % 4][:, 0:KD * WINDOW].rearrange("p (m w) -> p m w", m=KD),
                                  ALU.add).then_inc(s_zadd, 1)

            def indices(b, r):
                dve.tensor_copy(idx_ring[:, r * SLOTS:(r + 1) * SLOTS],
                                src_i[:, ds(b * BODY + r * SLOTS, SLOTS)]).then_inc(s_idx, 1)

            def adds(n0, b, step=None):
                c0 = b * BODY
                indices(b, 1)
                for k in range(OH):
                    onehot(n0, c0, k)
                for k in range(BODY):
                    if step:
                        step(k)
                    if k % BASES == 0:
                        _, bases = nc.values_load_multi_w_load_instructions(
                            base_i[0:1, ds(b, 1), k:min(k + BASES, BODY)].rearrange("p a k -> p (a k)"),
                            engines={mybir.EngineType.DVE}, min_val=0, max_val=NPAD - WINDOW,
                            skip_runtime_bounds_check_because="clamped to this range where they are made")
                    add(n0, bases[k % BASES], k)
                    if k == SLOTS - 1:
                        indices(b + 1, 0)
                    if k + OH < BODY:
                        onehot(n0, c0, k + OH)

            def row_max(u):
                dve.wait_ge(s_w_amT, u + 1)
                dve.tensor_reduce(wamr[0:1, :], PB[0:1, 128:256], AX, ALU.max).then_inc(s_w_amr, 1)

            def scale(u):
                dve.wait_ge(s_w_bc, u + 1)
                dve.tensor_scalar(wmax, PB[:, 256:257], 1e-30, None, ALU.max).then_inc(s_w_sc0, 1)
                dve.wait_ge(s_w_sc0, u * 3 + 1)
                dve.tensor_scalar(wp2.bitcast(I32), wmax.bitcast(I32), EXPONENT, None, ALU.bitwise_and).then_inc(s_w_sc0, 1)
                dve.wait_ge(s_w_sc0, u * 3 + 2)
                dve.reciprocal(wmax, wp2).then_inc(s_w_sc0, 1)
                dve.wait_ge(s_w_sc0, u * 3 + 3)

            def low_part(u, dest, hi):
                dve.wait_ge(s_w_hi, u + 1)
                dve.scalar_tensor_tensor(out=dest, in0=S[:], scalar=wsc, in1=hi, op0=ALU.mult,
                                         op1=ALU.subtract).then_inc(s_w_lo, 1)

            indices(0, 0)
            dve.sem_inc(s_zadd, 4)
            dve.wait_ge(s_z0, NT)
            dve.sem_inc(s_w_lo, 1)
            with dve.Fori(0, E) as e:
                bcol = params[:, ds(e * KH, KH)]

                def step(k):
                    if k == 0:
                        dve.tensor_copy(lnb, params[:, ds(e * KD + CB, KD)]).then_inc(s_lnb, 1)
                    if k == 14:
                        dve.wait_ge(s_w_fold, e * 2 + 2)
                        dve.tensor_reduce(wam, S[:], AX, ALU.max, apply_absolute_value=True).then_inc(s_w_am0, 1)
                        dve.wait_ge(s_browT, e + 1)
                        dve.tensor_tensor(bnew, bcol, PB[:, 0:KH], ALU.add).then_inc(s_w_am0, 1)
                    if k == 15:
                        dve.wait_ge(s_w_am0, e * 3 + 2)
                        dve.tensor_reduce(wam2, bnew, AX, ALU.max, apply_absolute_value=True).then_inc(s_w_am0, 1)
                        dve.tensor_copy(bcol, bnew)
                    if k == 16:
                        dve.wait_ge(s_w_am0, e * 3 + 3)
                        dve.scalar_tensor_tensor(out=wam, in0=wam, scalar=float(D), in1=wam2, op0=ALU.mult,
                                                 op1=ALU.max).then_inc(s_w_am, 1)
                    if k == 19:
                        row_max(e)
                    if k == 22:
                        scale(e)
                        dve.tensor_scalar(sc1[:, ds(e, 1)], wp2, 2.0 ** -21 / XN_SCALE, None, ALU.mult)
                        dve.tensor_scalar(shs[:, ds(e, 1)], wmax, 2.0 ** 13, None, ALU.mult)
                        dve.tensor_scalar(sc2[:, ds(e, 1)], wp2, 2.0 ** -13, None, ALU.mult)
                        dve.tensor_scalar(wsc, wmax, 2.0 ** 21, None, ALU.mult).then_inc(s_w_sc, 1)
                    if k == 25:
                        low_part(e, W1lo[:, ds(e, 1), :, :].rearrange("p a k h -> p (a k h)"),
                                 W1hi[:, ds(e, 1), :, :].rearrange("p a k h -> p (a k h)"))
                adds(e * BODY, e, step)
            with dve.Fori(0, E) as e:
                def step(k):
                    if k == 6:
                        dve.wait_ge(s_w_ld, (e + (E + 1)) * 16)
                        dve.tensor_reduce(wam, S[:], AX, ALU.max, apply_absolute_value=True).then_inc(s_w_am, 1)
                    if k == 11:
                        row_max(e + E)
                    if k == 14:
                        scale(e + E)
                        dve.scalar_tensor_tensor(out=sc2[:, ds(e, 1)], in0=sc2[:, ds(e, 1)], scalar=2.0 ** -13, in1=wp2,
                                                 op0=ALU.mult, op1=ALU.mult)
                        dve.tensor_scalar(wsc, wmax, 2.0 ** 13, None, ALU.mult).then_inc(s_w_sc, 1)
                    if k == 20:
                        low_part(e + E, W2lo[:, ds(e, 1), :, :].rearrange("p a c d -> p (a c d)"),
                                 W2hi[:, ds(e, 1), :, :].rearrange("p a c d -> p (a c d)"))
                adds((e + E) * BODY, e + E, step)
            npass = dve.value_load(npass_i[:, 2:3], min_val=1, max_val=NPAD // WINDOW)
            with dve.If(npass > 1):
                with dve.Fori(1, npass) as w:
                    dve.wait_ge(s_zadd, w * ET + 4)
                    dve.tensor_scalar(iota_w[:], iota_w[:], float(WINDOW), None, ALU.add).then_inc(s_passb, 1)
                    dve.tensor_scalar(base_i[:, :, 0:BODY], base_i[:, :, 0:BODY], float(WINDOW), float(NPAD - WINDOW), ALU.add,
                                      ALU.min).then_inc(s_passb, 1)
                    dve.wait_ge(s_passb, w * 2)
                    indices(0, 0)
                    dve.sem_inc(s_passgo, 1)
                    with dve.Fori(0, 2 * E) as b:
                        adds(w * ET + b * BODY, b)
            dve.wait_ge(s_zadd, npass * ET + 4)
            dve.sem_inc(s_gathered, 1)

            for c in range(NCH):
                if c in s_dbc:
                    dve.wait_ge(s_dbc[c], 16)
                for m in range(KD):
                    z = AT[:, m, c * CH:(c + 1) * CH]
                    last = dve.tensor_tensor(z, z, dbc(c, c + 1), ALU.mult)
                last.then_inc(s_zs, 1)
            for c in range(NCH + 3):
                if c < NCH:
                    h = AT[:, :, c * CH:(c + 1) * CH]
                    dve.wait_ge(s_sig, c + 1)
                    dve.wait_ge(s_dx, c + 1)
                    for m in range(KD):
                        last = dve.scalar_tensor_tensor(out=h[:, m, :], in0=GATE[c % 3][m][:, 0:CH], scalar=1.0,
                                                        in1=h[:, m, :], op0=ALU.add, op1=ALU.mult)
                    last.then_inc(s_dxg, 1)
                if 0 <= c - 1 < NCH:
                    h = AT[:, :, (c - 1) * CH:c * CH]
                    dve.wait_ge(s_dxg, c)
                    dve.scalar_tensor_tensor(out=h, in0=h, scalar=0.5, in1=BT[:, :, (c - 1) * CH:c * CH], op0=ALU.mult,
                                             op1=ALU.add).then_inc(s_mix, 1)
                if c >= 3:
                    n = min(CH, N - (c - 3) * CH)
                    dve.wait_ge(s_h, c - 3 + 1)
                    for m in range(KD):
                        last = dve.bn_stats(bsv[:, m, c - 3, :], AT[:, m, (c - 3) * CH:(c - 3) * CH + n])
            link(last)
            for m in range(KD):
                last = dve.bn_aggr(bmv[:, m, :], bsv[:, m, :, :].rearrange("p c v -> p (c v)"))
            last.then_inc(s_bnsq, 1)
            dve.wait_ge(s_bnsq, 2)
            link(dve.reciprocal(brs, bsq))
            link(dve.tensor_tensor(bsc, brs, params[:, CV + 3 * KD:CV + 4 * KD], ALU.mult))
            link(dve.tensor_tensor(brs, bmv[:, :, 0:1].rearrange("p k a -> p (k a)"), bsc, ALU.mult))
            dve.tensor_tensor(bbi, params[:, CV + 4 * KD:CV + 5 * KD], brs, ALU.subtract).then_inc(s_bn, 1)

            def x2_tile(t, i):
                v = BR[:, ds(t, 1), :].rearrange("p a d -> p (a d)")
                dve.wait_ge(s_hT, t + 1)
                dve.tensor_tensor(v, v, PA[i][:, 0:D], ALU.add).then_inc(s_x2, 1)
                dve.wait_ge(s_x2, t + 1)
                return dve.bn_stats(svh[:, ds(t, 1), :].rearrange("p a v -> p (a v)"), v)
            for q in range(4):
                dve.wait_ge(s_x[q], 32)
                with dve.Fori(q * XG // 2, (q + 1) * XG // 2) as g:
                    for i in range(2):
                        x2_tile(g * 2 + i, i)
            dve.wait_ge(s_xlast, 32)
            link(x2_tile(NT - 1, 0))
            combine(svh).then_inc(s_var, 1)
            dve.wait_ge(s_sq1, 1)
            link(dve.reciprocal(nst[:, 6, :], nst[:, 3, :]))
            link(dve.tensor_tensor(nst[:, 1, :], nst[:, 6, :], nst[:, 6, :], ALU.mult))
            dve.tensor_tensor(nst[:, 4, :], nst[:, 2, :], nst[:, 1, :], ALU.mult).then_inc(s_v2, 1)
            dve.wait_ge(s_sq2, 1)
            link(dve.reciprocal(nst[:, 7, :], nst[:, 5, :]))
            link(dve.scalar_tensor_tensor(out=nst[:, 7, :], in0=nst[:, 7, :], scalar=XN_SCALE, in1=nst[:, 6, :],
                                          op0=ALU.mult, op1=ALU.mult))

            def token_step(tile, s):
                t, i = tile(0), s % 2
                if exists(t):
                    if since(t, 2):
                        dve.wait_ge(s_vT, t - 1)
                        dve.wait_ge(s_xlo, t - 1)
                    dve.tensor_scalar(V[i], BR[:, ds(t, 1), :].rearrange("p a d -> p (a d)"), nst[:, 0, ds(t, 1)],
                                      nst[:, 7, ds(t, 1)], ALU.subtract, ALU.mult).then_inc(s_v, 1)
                t, i = tile(1), (s - 1) % 4
                if exists(t):
                    dve.wait_ge(s_xhi, t + 1)
                    dve.tensor_tensor(XH[i][:, D:2 * D], V[i % 2], XH[i][:, 0:D], ALU.subtract).then_inc(s_xlo, 1)
            over_tiles(dve, token_step)

            def bc_e(v):
                return v.rearrange("p (t a) -> p t a", a=1).to_broadcast([P, NT, E])

            def bc_t(v, n=E):
                return v.rearrange("p (a e) -> p a e", a=1).to_broadcast([P, NT, n])
            m1, zs, p1, p2 = nst[:, 1, :], nst[:, 2, :], nst[:, 3, :], nst[:, 4, :]
            i1, i2, pos = nst[:, 6, :], nst[:, 7, :], nst[:, 0, :]
            L, EX, PR, EQ, O1, O2, CHOSEN = (rt(i) for i in range(7))
            TOT, INC, SL, TMP = rt(7), rt(8), rt(9), rt(10)
            dve.wait_ge(s_log, NT)
            dve.wait_ge(s_wr, 32)
            dve.wait_ge(s_tri, 4)
            link(dve.tensor_scalar(nst[:, 5, :], nst[:, 5, :], 1.0 / XN_SCALE, None, ALU.mult))
            link(dve.tensor_tensor(L, PB[:, 0:NE].rearrange("p (t e) -> p t e", e=E), bc_e(nst[:, 5, :]), ALU.mult))
            link(dve.tensor_tensor(L, L, bc_t(brS), ALU.add))
            link(dve.tensor_reduce(m1, L, AX, ALU.max))
            dve.tensor_tensor(EX, L, bc_e(m1), ALU.subtract).then_inc(s_sh, 1)
            dve.wait_ge(s_exp, 1)
            link(dve.tensor_reduce(zs, EX, AX, ALU.add))
            link(dve.reciprocal(zs, zs))
            link(dve.tensor_tensor(PR, EX, bc_e(zs), ALU.mult))

            def choose(one, best, index):
                link(dve.tensor_reduce(best, PR, AX, ALU.max))
                link(dve.tensor_tensor(EQ, PR, bc_e(best), ALU.is_equal))
                link(dve.scalar_tensor_tensor(out=EQ, in0=EQ, scalar=-float(E), in1=bc_t(iota[:, E:2 * E]),
                                              op0=ALU.mult, op1=ALU.add))
                link(dve.tensor_reduce(index, EQ, AX, ALU.min))
                link(dve.tensor_tensor(one, bc_t(iota[:, 0:E]), bc_e(index), ALU.is_equal))
            choose(O1, p1, i1)
            link(dve.scalar_tensor_tensor(out=PR, in0=O1, scalar=-2.0, in1=PR, op0=ALU.mult, op1=ALU.add))
            choose(O2, p2, i2)
            link(dve.tensor_tensor(zs, p1, p2, ALU.add))
            link(dve.reciprocal(zs, zs))
            dve.tensor_tensor(wts[:, 0, :], p1, zs, ALU.mult)
            dve.tensor_tensor(wts[:, 1, :], p2, zs, ALU.mult)
            link(dve.tensor_tensor(CHOSEN, O1, O2, ALU.add))
            dve.tensor_tensor(CHOSEN, CHOSEN, bc_e(valid), ALU.mult).then_inc(s_msum, 1)
            dve.wait_ge(s_cnt, 1)
            link(dve.tensor_copy(TOT.rearrange("p t e -> p (t e)").rearrange("p (e t) -> p e t", e=E),
                                 Q[1][:, 0:NE].rearrange("p (t e) -> p e t", e=E)))
            tot = TOT.rearrange("p t e -> p (t e)").rearrange("p (e t) -> p e t", e=E)
            inc = INC.rearrange("p t e -> p (t e)").rearrange("p (e t) -> p e t", e=E)
            for e in range(E):
                last = dve.tensor_tensor_scan(inc[:, e, :], ones[:, 0:NT], tot[:, e, :], 0.0, ALU.mult, ALU.add)
            link(last)
            work = A[:, 24 * 256:24 * 256 + 8 * E]
            cf, ci, ti, te, tend, tst = (work[:, E * a:E * (a + 1)] for a in range(6))
            link(dve.tensor_scalar(cf, inc[:, :, NT - 1:NT].rearrange("p e a -> p (e a)"), float(SLOT_ROWS - 1), None, ALU.add))
            link(dve.tensor_copy(ci.bitcast(I32), cf))
            link(dve.tensor_scalar(ti.bitcast(I32), ci.bitcast(I32), SLOT_ROWS.bit_length() - 1, None,
                                   ALU.arith_shift_right))
            link(dve.tensor_copy(te, ti.bitcast(I32)))
            link(dve.tensor_tensor_scan(tend, ones[:, 0:E], te, 0.0, ALU.mult, ALU.add))
            link(dve.tensor_tensor(tst, tend, te, ALU.subtract))
            link(dve.tensor_scalar(tst, tst, float(SLOT_ROWS), None, ALU.mult))
            link(dve.tensor_tensor(SL, inc.rearrange("p e t -> p t e"), tot.rearrange("p e t -> p t e"), ALU.subtract))
            link(dve.tensor_tensor(SL, SL, Q[0][:, 0:NE].rearrange("p (t e) -> p t e", e=E), ALU.add))
            link(dve.tensor_tensor(SL, SL, bc_t(tst), ALU.add))
            link(dve.tensor_scalar(far, valid, -float(P * P * P), float(P * P * P), ALU.mult, ALU.add))
            tile_of = rt(12).rearrange("p t e -> p (t e)")[:, 0:2 * NT]
            posi = rt(13).rearrange("p t e -> p (t e)")[:, 0:2 * NT].bitcast(I32)
            pi2 = rt(14).rearrange("p t e -> p (t e)")[:, 0:2 * NT].bitcast(I32)
            for k, one in enumerate((O1, O2)):
                link(dve.tensor_tensor(TMP, SL, one, ALU.mult))
                link(dve.tensor_reduce(pos, TMP, AX, ALU.add))
                link(dve.tensor_tensor(pos, pos, far, ALU.add))
                link(dve.tensor_copy(posi.rearrange("p (t k) -> p t k", k=2)[:, :, k:k + 1],
                                     pos.rearrange("p (t a) -> p t a", a=1)))
            link(dve.tensor_scalar(pi2, posi, P - 1, None, ALU.bitwise_and))
            link(dve.tensor_copy(lane, pi2))
            link(dve.tensor_scalar(pi2, posi, P.bit_length() - 1, None, ALU.arith_shift_right))
            link(dve.tensor_copy(tile_of, pi2))

            link(dve.tensor_copy(lt16[:, 0, :], lane))
            link(dve.tensor_copy(lt16[:, 1, :], tile_of))

            ring_full(dve, s_xh_st)

            dve.sem_inc(s_lanes, 1)
            for c in range(2 * NT // PART):
                r = slice(c * PART, (c + 1) * PART)
                if c < LO_DVE:
                    dve.tensor_tensor(LO[:, r, :], spread_to(lt16[:, 0, r], P),
                                      iota16.rearrange("p (a n) -> p a n", a=1).to_broadcast([P, PART, P]), ALU.is_equal)
                link(dve.tensor_tensor(V2[:, 1, r, :], spread_to(lt16[:, 1, r], SC),
                                       iota16[:, 0:SC].rearrange("p (a n) -> p a n", a=1).to_broadcast([P, PART, SC]),
                                       ALU.is_equal))
                link(dve.tensor_tensor(V2[:, 0, r, :], V2[:, 1, r, :], spread_to(iota16[:, c * PART + 1:(c + 1) * PART + 1], SC),
                                       ALU.mult))
                dve.tensor_scalar(V2[:, 1, r, :], V2[:, 1, r, :], iota_p, None, ALU.mult).then_inc(s_onehots, 1)
            ef = rt(15).rearrange("p t e -> p (t e)")[:, 0:ST]
            link(dve.tensor_scalar(ef, iota[:, 0:ST], tend[:, 0:1], None, ALU.is_ge))
            for e in range(1, E):
                link(dve.scalar_tensor_tensor(out=ef, in0=iota[:, 0:ST], scalar=tend[:, e:e + 1], in1=ef,
                                              op0=ALU.is_ge, op1=ALU.add))
            dve.tensor_scalar(exp_i, ef, float(E - 1), None, ALU.min)
            dve.wait_ge(s_perm, 1)
            v1, lane_s = Q[2][:, 0:SC], Q[2][:, SC:2 * SC]
            sf = [rt(16 + a).rearrange("p t e -> p (t e)")[:, 0:SC] for a in range(4)]
            slot_id = A[:, 21 * 256 + 64:21 * 256 + 64 + SC]
            filled, vi, vh, tok = sf
            link(dve.tensor_scalar(filled, v1, 0.0, None, ALU.is_gt))
            link(dve.tensor_scalar(vi.bitcast(I32), v1, -1.0, 0.0, ALU.add, ALU.max))
            link(dve.tensor_scalar(vh.bitcast(I32), vi.bitcast(I32), 1, None, ALU.arith_shift_right))
            link(dve.tensor_copy(tok, vh.bitcast(I32)))
            link(dve.scalar_tensor_tensor(out=tok, in0=tok, scalar=float(P), in1=lane_s, op0=ALU.mult, op1=ALU.add))
            dve.tensor_copy(gidx, tok)
            link(dve.tensor_scalar(vh.bitcast(I32), vi.bitcast(I32), 1, None, ALU.bitwise_and))
            link(dve.tensor_copy(vi, vh.bitcast(I32)))
            link(dve.scalar_tensor_tensor(out=vi, in0=tok, scalar=2.0, in1=vi, op0=ALU.mult, op1=ALU.add))
            link(dve.tensor_tensor(vi, vi, slot_id, ALU.subtract))
            link(dve.tensor_tensor(vi, vi, filled, ALU.mult))
            link(dve.tensor_tensor(vi, vi, slot_id, ALU.add))
            dve.tensor_copy(sidx, vi).then_inc(s_routed, 1)

            dve.wait_ge(s_b2, 16)
            dve.wait_ge(s_routed, 1)

            def expert(n):
                return dve.value_load(exp_i[0:1, ds(n, 1)], min_val=0, max_val=E - 1)

            def result(n, e, b, i, first):
                for h in range(2):
                    j = 2 * i + h
                    if h == 0:
                        dve.wait_ge(s_y, n * 2 + 2)
                    if not first:
                        dve.wait_ge(s_sc[j], b * 16)
                    dve.scalar_tensor_tensor(out=Y[j], in0=PA[h][:, 0:D], scalar=sc2[:, ds(e, 1)],
                                             in1=b2bc[:, ds(e, 1), :].rearrange("p a d -> p (a d)"),
                                             op0=ALU.mult, op1=ALU.add).then_inc(s_yr, 1)

            def split(n, e, half, first):
                c0, c1 = half * KH // 2 * SLOT_ROWS, (half + 1) * KH // 2 * SLOT_ROWS
                dve.wait_ge(s_gelu, n * KH + (half + 1) * KH // 2)
                if not first:
                    dve.wait_ge(s_y, n * 2 + (half - 1))
                dve.tensor_scalar(HHI[:, c0:c1], HF[:, c0:c1], shs[:, ds(e, 1)], None, ALU.mult).then_inc(s_hs, 1)
                dve.wait_ge(s_hs, n * 4 + (2 * half + 1))
                dve.scalar_tensor_tensor(out=HLO[:, c0:c1], in0=HF[:, c0:c1], scalar=shs[:, ds(e, 1)],
                                         in1=HHI[:, c0:c1], op0=ALU.mult, op1=ALU.subtract).then_inc(s_hs, 1)

            def step(n, e, before, b, i, first_tile, first_turn):
                split(n, e, 0, first_tile)
                if not first_tile:
                    result(n - 1, before, b, 1 - i, first_turn)
                split(n, e, 1, first_tile)

            e0, e1, e2, e3 = (expert(n) for n in range(4))
            step(0, e0, None, 0, 0, True, True)
            step(1, e1, e0, 0, 1, False, True)
            step(2, e2, e1, 0, 0, False, True)
            step(3, e3, e2, 1, 1, False, False)
            with dve.Fori(2, NB) as b:
                before, ea, eb = (expert(b * U + d) for d in (-1, 0, 1))
                step(b * U, ea, before, b - 1, 0, False, False)
                step(b * U + 1, eb, ea, b, 1, False, False)
            result(ST - 1, expert(ST - 1), NB - 1, 1, False)

            def final(t, y, rows):
                o = BR[0:rows, ds(t, 1), :].rearrange("p a d -> p (a d)")
                dve.scalar_tensor_tensor(out=o, in0=y[0:rows, 0, :], scalar=wts[0:rows, 0, ds(t, 1)], in1=o,
                                         op0=ALU.mult, op1=ALU.add).then_inc(s_fin0, 1)
                dve.wait_ge(s_fin0, t + 1)
                dve.scalar_tensor_tensor(out=o, in0=y[0:rows, 1, :], scalar=wts[0:rows, 1, ds(t, 1)], in1=o,
                                         op0=ALU.mult, op1=ALU.add).then_inc(s_fin, 1)
            for g in range(NT // 4):
                dve.wait_ge(s_yload[g % 3], (g // 3 + 1) * 16)
                for a in range(4):
                    final(g * 4 + a, FIN[g % 3][:, a], P)
            dve.wait_ge(s_yload[NT // 4 % 3], (NT // 12 + 1) * 16)
            final(NT - 1, FIN[NT // 4 % 3][:, 0], LAST)


_INS = ['x', 'src', 'dst', 'L0_gnn_gcn_W', 'L0_gnn_gcn_b', 'L0_gnn_lin_W', 'L0_gnn_lin_b', 'L0_gnn_gate_W',
        'L0_gnn_gate_b', 'L0_gnn_bn_gamma', 'L0_gnn_bn_beta', 'L0_ffn_Wr', 'L0_ffn_br', 'L0_ffn_ln_g', 'L0_ffn_ln_b',
        'L0_ffn_W1', 'L0_ffn_b1', 'L0_ffn_W2', 'L0_ffn_b2']


def kernel(**inputs):
    import numpy as _np
    import concourse.bacc as _bacc
    from concourse import mybir as _mybir
    from concourse.bass_utils import run_bass_kernel_spmd as _run

    nc = _bacc.Bacc("TRN2", target_bir_lowering=False, num_devices=1)
    arrays, args = {}, []
    for name in _INS:
        a = _np.ascontiguousarray(inputs[name])
        arrays[f"in_{name}"] = a
        args.append(nc.dram_tensor(f"in_{name}", a.shape, _mybir.dt.from_np(a.dtype), kind="ExternalInput").ap())
    args.append(nc.dram_tensor("out_0", inputs["x"].shape, _mybir.dt.float32, kind="ExternalOutput").ap())
    build_gnn_moe(nc, *args)
    r = _run(nc, [arrays], core_ids=[0])
    return r.results[0]["out_0"]
```
